# Optimizing a Trainium2 kernel written in Bass

```python
import numpy as np
import jax
import jax.numpy as jnp

def _softmax(x, axis=-1):
    return jax.nn.softmax(x, axis=axis)

def _gelu(x):
    return jax.nn.gelu(x, approximate=True)

def _silu(x):
    return jax.nn.silu(x)

def _sigmoid(x):
    return jax.nn.sigmoid(x)

def _layernorm(x, axis=-1, eps=1e-05):
    m = jnp.mean(x, axis=axis, keepdims=True)
    v = jnp.var(x, axis=axis, keepdims=True)
    return (x - m) / jnp.sqrt(v + eps)

def _scatter_add(tgt, idx, src, axis=0):
    return tgt.at[idx].add(src)

def _segment_sum(src, seg, n):
    return jax.ops.segment_sum(src, seg, n)
kernel_name = 'mk_adj_ffn_d1_adj_r2_ed1724'

def setup_inputs(seed: int=0):
    np.random.seed(seed)
    _w = jnp.asarray

    def _rec_inputs():
        import jax
        import jax.numpy as jnp
        _gk = jax.random.key(seed)
        x = 7.22e-05 + 1 * jax.random.normal(jax.random.fold_in(_gk, 1), (16, 512, 128), jnp.float32)
        _a = jax.random.bernoulli(jax.random.fold_in(_gk, 2), 0.015625, (16, 512, 512))
        _af = _a.astype(jnp.float32)
        adj = _af
        _nm = jnp.ones((16, 512), dtype=bool)
        nodemask = jnp.where(_nm, 1.0, 0.0).astype(jnp.float32)
        return (x, adj, nodemask)
    x, adj, nodemask = _rec_inputs()

    def _L0_gnn_setup():
        import jax, jax.numpy as jnp
        import numpy as np
        B, N, D, C, L = (64, 256, 128, 128, 5)
        EDGE_P = 0.02

        def _gru_cell(m, h, w_ih, w_hh, b_ih, b_hh):
            gi = m @ w_ih.T + b_ih
            gh = h @ w_hh.T + b_hh
            i_r, i_z, i_n = jnp.split(gi, 3, axis=-1)
            h_r, h_z, h_n = jnp.split(gh, 3, axis=-1)
            r = jax.nn.sigmoid(i_r + h_r)
            z = jax.nn.sigmoid(i_z + h_z)
            n = jnp.tanh(i_n + r * h_n)
            return (1.0 - z) * n + z * h
        key = jax.random.key(seed)
        ks = jax.random.split(key, 8)
        x = jax.random.normal(ks[0], (B, N, D), dtype=jnp.float32)
        adj = (jax.random.uniform(ks[1], (B, N, N)) < EDGE_P).astype(jnp.float32)
        mask = jnp.ones((B, N), dtype=jnp.float32)
        s = 1.0 / np.sqrt(C).astype(np.float32)
        weight = jax.random.uniform(ks[2], (L, C, C), minval=-s, maxval=s, dtype=jnp.float32)
        w_ih = jax.random.uniform(ks[3], (3 * C, C), minval=-s, maxval=s, dtype=jnp.float32)
        w_hh = jax.random.uniform(ks[4], (3 * C, C), minval=-s, maxval=s, dtype=jnp.float32)
        b_ih = jax.random.uniform(ks[5], (3 * C,), minval=-s, maxval=s, dtype=jnp.float32)
        b_hh = jax.random.uniform(ks[6], (3 * C,), minval=-s, maxval=s, dtype=jnp.float32)
        return dict(x=x, adj=adj, mask=mask, weight=weight, w_ih=w_ih, w_hh=w_hh, b_ih=b_ih, b_hh=b_hh)
    _L0_gnn_all = _L0_gnn_setup()
    _L0_gnn_in = {k: v for k, v in _L0_gnn_all.items() if k in ('weight', 'w_ih', 'w_hh', 'b_ih', 'b_hh')}
    del _L0_gnn_all

    def _L0_ffn_setup():
        import jax, jax.numpy as jnp
        import numpy as np
        B, S, H, F, E, K = (8, 2048, 128, 256, 16, 2)
        EPS = 1e-05
        key = jax.random.key(seed)
        ks = jax.random.split(key, 9)
        sc = 0.02
        return {'x': jax.random.normal(ks[0], (B, S, H), dtype=jnp.float32), 'gate_w': jax.random.normal(ks[1], (H, E), dtype=jnp.float32) * sc, 'gate_b': jnp.zeros((E,), dtype=jnp.float32), 'w1': jax.random.normal(ks[2], (E, H, F), dtype=jnp.float32) * sc, 'b1': jnp.zeros((E, F), dtype=jnp.float32), 'w2': jax.random.normal(ks[3], (E, F, H), dtype=jnp.float32) * sc, 'b2': jnp.zeros((E, H), dtype=jnp.float32), 'gamma': jnp.ones((H,), dtype=jnp.float32), 'beta': jnp.zeros((H,), dtype=jnp.float32)}
    _L0_ffn_all = _L0_ffn_setup()
    _L0_ffn_in = {k: v for k, v in _L0_ffn_all.items() if k in ('gate_w', 'gate_b', 'w1', 'b1', 'w2', 'b2', 'gamma', 'beta')}
    del _L0_ffn_all
    return {'x': x, 'adj': adj, 'nodemask': nodemask, 'L0_gnn_weight': _L0_gnn_in['weight'], 'L0_gnn_w_ih': _L0_gnn_in['w_ih'], 'L0_gnn_w_hh': _L0_gnn_in['w_hh'], 'L0_gnn_b_ih': _L0_gnn_in['b_ih'], 'L0_gnn_b_hh': _L0_gnn_in['b_hh'], 'L0_ffn_gate_w': _L0_ffn_in['gate_w'], 'L0_ffn_gate_b': _L0_ffn_in['gate_b'], 'L0_ffn_w1': _L0_ffn_in['w1'], 'L0_ffn_b1': _L0_ffn_in['b1'], 'L0_ffn_w2': _L0_ffn_in['w2'], 'L0_ffn_b2': _L0_ffn_in['b2'], 'L0_ffn_gamma': _L0_ffn_in['gamma'], 'L0_ffn_beta': _L0_ffn_in['beta']}

def reference(x, adj, nodemask, L0_gnn_weight, L0_gnn_w_ih, L0_gnn_w_hh, L0_gnn_b_ih, L0_gnn_b_hh, L0_ffn_gate_w, L0_ffn_gate_b, L0_ffn_w1, L0_ffn_b1, L0_ffn_w2, L0_ffn_b2, L0_ffn_gamma, L0_ffn_beta):
    import jax
    import jax.numpy as jnp

    def _L0_gnn_ref(x, adj, mask, weight, w_ih, w_hh, b_ih, b_hh):
        import jax, jax.numpy as jnp
        import numpy as np
        B, N, D, C, L = (64, 256, 128, 128, 5)
        EDGE_P = 0.02

        def _gru_cell(m, h, w_ih, w_hh, b_ih, b_hh):
            gi = m @ w_ih.T + b_ih
            gh = h @ w_hh.T + b_hh
            i_r, i_z, i_n = jnp.split(gi, 3, axis=-1)
            h_r, h_z, h_n = jnp.split(gh, 3, axis=-1)
            r = jax.nn.sigmoid(i_r + h_r)
            z = jax.nn.sigmoid(i_z + h_z)
            n = jnp.tanh(i_n + r * h_n)
            return (1.0 - z) * n + z * h
        A = (adj != 0).astype(x.dtype)
        h = x
        for l in range(weight.shape[0]):
            m = jnp.einsum('bnd,de->bne', h, weight[l])
            agg = jnp.einsum('bij,bid->bjd', A, m)
            h = _gru_cell(agg, h, w_ih, w_hh, b_ih, b_hh)
        return h * mask[..., None]

    def _L0_ffn_ref(x, gate_w, gate_b, w1, b1, w2, b2, gamma, beta):
        import jax, jax.numpy as jnp
        import numpy as np
        B, S, H, F, E, K = (8, 2048, 128, 256, 16, 2)
        EPS = 1e-05
        gate_logits = x @ gate_w + gate_b
        topk_vals, topk_idx = jax.lax.top_k(gate_logits, K)
        topk_w = jax.nn.softmax(topk_vals, axis=-1)
        h = jax.nn.relu(jnp.einsum('bsh,ehf->bsef', x, w1) + b1)
        expert_out = jnp.einsum('bsef,efh->bseh', h, w2) + b2
        sel = jnp.take_along_axis(expert_out, topk_idx[:, :, :, None], axis=2)
        moe = jnp.sum(topk_w[..., None] * sel, axis=2)
        y = x + moe
        mu = jnp.mean(y, axis=-1, keepdims=True)
        var = jnp.var(y, axis=-1, keepdims=True)
        return (y - mu) / jnp.sqrt(var + EPS) * gamma + beta
    x = x + _L0_gnn_ref(_layernorm(x, axis=-1), adj, nodemask, L0_gnn_weight, L0_gnn_w_ih, L0_gnn_w_hh, L0_gnn_b_ih, L0_gnn_b_hh)
    x = x + _L0_ffn_ref(_layernorm(x, axis=-1), L0_ffn_gate_w, L0_ffn_gate_b, L0_ffn_w1, L0_ffn_b1, L0_ffn_w2, L0_ffn_b2, L0_ffn_gamma, L0_ffn_beta)
    return x

_drawn_inputs = setup_inputs


def setup_inputs(seed=0):
    import zlib

    import numpy as np

    out = dict(_drawn_inputs(seed))
    spreads = {'L0_ffn_gate_b': (0.0, 0.1),
     'L0_ffn_b1': (0.0, 0.8),
     'L0_ffn_b2': (0.0, 0.1),
     'L0_ffn_gamma': (1.0, 0.2),
     'L0_ffn_beta': (0.0, 0.1)}
    factors = {'L0_ffn_w1': 3.719, 'L0_ffn_w2': 2.918}
    for name, (base, spread) in spreads.items():
        noise = np.random.default_rng([zlib.crc32(name.encode()), seed]).standard_normal(out[name].shape)
        drawn = base * np.exp(spread * noise) if base else spread * noise
        out[name] = jnp.asarray(drawn.astype(out[name].dtype))
    for name, factor in factors.items():
        out[name] = (out[name] * factor).astype(out[name].dtype)
    return out
```

```python
import concourse.bass as bass
from concourse import mybir
from contextlib import ExitStack

FP32 = mybir.dt.float32
FP32R = mybir.dt.float32r
BF16 = mybir.dt.bfloat16
I32 = mybir.dt.int32
U32 = mybir.dt.uint32
ALU = mybir.AluOpType
ACT = mybir.ActivationFunctionType
AX = mybir.AxisListType

EPS = 1e-5
P = 128


def build(nc, x, adj, nodemask, weight, w_ih, w_hh, b_ih, b_hh, gate_w, gate_b, w1, b1, w2, b2, gamma, beta, out):
    B, N, D = x.shape
    L = weight.shape[0]
    E, _, F = w1.shape
    K = 2
    C = N // P
    FC = F // P
    T = B * N
    S = 2
    G = B // S
    ST = S * L
    ROW = D + 2
    REGION = T + P
    TILES = (K * T + E * (P - 1)) // P
    TILES += -TILES % 8
    PAIRS = TILES // 2
    SLOTS = 4
    SKIP = 1 << 20
    LOADS = 8

    dispatched = nc.dram_tensor("dispatched", [E * REGION + P, ROW], FP32, kind="Internal").ap()
    result = nc.dram_tensor("result", [K * T, D], FP32, kind="Internal").ap()

    ctx = ExitStack()
    with ctx:
        def sb(name, shape, dt=FP32):
            return ctx.enter_context(nc.sbuf_tensor(name, shape, dt))

        def sem(name):
            return ctx.enter_context(nc.semaphore(name))

        ident = sb("ident", [P, P])
        lower = sb("lower", [P, P], BF16)
        ones = sb("ones", [P, P], BF16)
        iota_e = sb("iota_e", [P, E])
        exponent = sb("exponent", [P, C])
        dest = sb("dest", [P, B * C, K], I32)
        pad = sb("pad", [P, ROW])
        rows = sb("rows", [2 * 3 + B * C, P])
        cols = sb("cols", [P, 2 * 3 + B * C])
        bias_rz = sb("bias_rz", [P, 2])
        w_fused_hi = sb("w_fused_hi", [P, L, 3 * D], FP32R)
        w_fused_lo = sb("w_fused_lo", [P, L, 3 * D], FP32R)
        w_hh_hi = sb("w_hh_hi", [P, 3 * D], FP32R)
        w_hh_lo = sb("w_hh_lo", [P, 3 * D], FP32R)
        gate_w_sb = sb("gate_w_sb", [P, E])
        gate_b_sb = sb("gate_b_sb", [P, E])
        gamma_sb = sb("gamma_sb", [P, D])
        beta_sb = sb("beta_sb", [P, D])
        w1_hi = sb("w1_hi", [P, E * F], FP32R)
        w1_lo = sb("w1_lo", [P, E * F], FP32R)
        w2_hi = sb("w2_hi", [P, E * FC * D], FP32R)
        w2_lo = sb("w2_lo", [P, E * FC * D], FP32R)
        x1 = sb("x1", [P, B * C, D])
        norm2_all = sb("norm2_all", [P, B * C, 2])
        base_e = sb("base_e", [P, E])
        adj_raw = [sb(f"adj_raw{s}", [P, C, N]) for s in range(S)]
        edges_all = sb("edges_all", [P, S * C * N], FP32R)
        edges = [edges_all[:, s * C * N:(s + 1) * C * N].rearrange("p (c n) -> p c n", c=C) for s in range(S)]
        h = [sb(f"h{s}", [P, N]) for s in range(S)]
        halves = sb("halves", [P, S, 4, N], FP32R)
        h_hi, h_lo = ([halves[:, s, i, :] for s in range(S)] for i in (0, 1))
        ht_hi, ht_lo = ([halves[:, s, i, :].rearrange("p (c d) -> p c d", c=C) for s in range(S)] for i in (2, 3))
        agg_hi = sb("agg_hi", [P, N], FP32R)
        agg_lo = sb("agg_lo", [P, N], FP32R)
        r_sb = sb("r_sb", [P, N])
        z_sb = sb("z_sb", [P, N])
        n_sb = sb("n_sb", [P, N])
        t_sb = sb("t_sb", [P, N])
        d_sb = sb("d_sb", [P, N])
        xn = [sb(f"xn{s}", [P, C, D]) for s in range(S)]
        held = sb("held", [P, 1])
        held_pool = sb("held_pool", [P, 1])
        stat1 = sb("stat1", [P, C, 6])
        norm1 = [sb(f"norm1{s}", [P, C, 2]) for s in range(S)]
        norm2 = [sb(f"norm2{s}", [P, C, 2]) for s in range(S)]
        stat2 = sb("stat2", [P, C, 6])
        payload = [sb(f"payload{s}", [P, C, K, ROW]) for s in range(S)]
        xfT = sb("xfT", [P, N])
        logits = sb("logits", [P, C, E])
        top = sb("top", [P, C, 8])
        top_at = sb("top_at", [P, C, 8], U32)
        chosen = sb("chosen", [P, C, K])
        onehot = sb("onehot", [P, C, K, E])
        both = sb("both", [P, C * E], BF16)
        margin = sb("margin", [P, C, K])
        place = sb("place", [P, C, E])
        picked = sb("picked", [P, C, K, E])
        slots_f = sb("slots_f", [P, C, K])
        slots = [sb(f"slots{s}", [P, C * K], U32) for s in range(S)]
        region_e = sb("region_e", [P, E])
        tile_at = sb("tile_at", [P, 2])
        count_i = sb("count_i", [P, E], I32)
        count_f = sb("count_f", [P, E])
        tiles_e = sb("tiles_e", [P, E])
        tile_end = sb("tile_end", [P, E])
        no_more = sb("no_more", [P, E])
        ended = sb("ended", [P, 2, E])
        ended_tiles = sb("ended_tiles", [P, 2, E])
        tile_expert = sb("tile_expert", [P, 2])
        tile_first = sb("tile_first", [P, 2])
        tile_row = sb("tile_row", [P, 2])
        clipped = sb("clipped", [P, 2, 2])
        tile_map = d_sb[0:1, 0:4 * P].bitcast(I32)
        pad_rows = sb("pad_rows", [1, E], I32)
        bias_raw = sb("bias_raw", [E, F + D])
        bias_hi = sb("bias_hi", [E, F + D], FP32R)
        bias_lo = bias_raw
        two_rows = sb("two_rows", [P, P], FP32R)
        b1_parts = edges_all
        b2_parts = halves[:, 0, :, :].rearrange("p i n -> p (i n)")
        assert E * F == S * C * N and E * D == 4 * N
        room = [adj_raw[q][:, 1:4, :].rearrange("p c n -> p (c n)") for q in range(2)]
        slot = [room[u % 2][:, u // 2 * 2 * ROW:(u // 2 + 1) * 2 * ROW].rearrange("p (j r) -> p j r", j=2) for u in range(SLOTS)]
        res = [room[u % 2][:, 4 * ROW + u // 2 * 2 * D:4 * ROW + (u // 2 + 1) * 2 * D].rearrange("p (j d) -> p j d", j=2) for u in range(SLOTS)]
        hid = [adj_raw[q][:, 0, :].rearrange("p (j f) -> p j f", j=2) for q in range(2)]
        xs_hi, xs_lo = ([halves[:, 1, i, q * 2 * P:(q + 1) * 2 * P] for q in range(2)] for i in (0, 1))
        hid_hi = [halves[:, 1, 2, :], agg_hi[:, :]]
        hid_lo = [halves[:, 1, 3, :], agg_lo[:, :]]
        y0 = [r_sb, z_sb]
        y1 = [n_sb, t_sb]
        y = [h[0], h[1]]
        x_beta = [xn[0], xn[1]]
        final = [adj_raw[q][:, 3, :].rearrange("p (c d) -> p c d", c=C) for q in range(2)]
        weight_raw = adj_raw[1][:, 0:2, :].rearrange("p c n -> p (c n)")[:, 0:L * D].rearrange("p (l e) -> p l e", l=L)
        w_ih_raw = h[0][:, 0:3 * D].rearrange("p (g e) -> p g e", g=3)
        w_hh_raw = h[1][:, 0:3 * D].rearrange("p (g e) -> p g e", g=3)
        weightT = adj_raw[1][:, 2:4, :].rearrange("p c n -> p (c n)")[:, 0:L * D].rearrange("p (l e) -> p l e", l=L)
        w_ihT = d_sb[:, 0:3 * D]
        raw = [payload[0][:, :, :, :].rearrange("p c k r -> p (c k r)")[:, 0:1024],
               payload[1][:, :, :, :].rearrange("p c k r -> p (c k r)")[:, 0:1024]]

        bank = [ctx.enter_context(nc.psum_tensor(f"bank{i}", [P, 512], FP32)) for i in range(8)]
        ps_agg, ps_r, ps_z, ps_in, ps_hn, ps_t, ps_prep, ps_post = bank
        ps_up, ps_hid, ps_down, ps_xs = bank[0:2], bank[2:4], bank[4:6], bank[6:8]

        loaded_weights = sem("loaded_weights")
        loaded_rows = sem("loaded_rows")
        loaded_consts = sem("loaded_consts")
        loaded_x0 = sem("loaded_x0")
        loaded_x = sem("loaded_x")
        loaded_adj = [sem(f"loaded_adj{s}") for s in range(S)]
        loaded_raw = [sem(f"loaded_raw{s}") for s in range(2)]
        raw_used = sem("raw_used")
        experts_split = sem("experts_split")
        consts_set = sem("consts_set")
        ident_ready = sem("ident_ready")
        w_transposed = sem("w_transposed")
        w_copied = sem("w_copied")
        w_fused = sem("w_fused")
        w_hi_ready = sem("w_hi_ready")
        w_lo_ready = sem("w_lo_ready")
        bias_ready = sem("bias_ready")
        edges_ready = [sem(f"edges_ready{s}") for s in range(S)]
        agg_done, r_done, in_done, z_done, t_done = (sem(f"{n}_done") for n in ("agg", "r", "in", "z", "t"))
        r_ready, z_ready, n_ready = (sem(f"{n}_ready") for n in "rzn")
        rh_done, pre_n_ready, d_ready, zd_ready, h_ready = (sem(n) for n in ("rh_done", "pre_n_ready", "d_ready", "zd_ready", "h_ready"))
        agg_hi_ready, agg_lo_ready = sem("agg_hi_ready"), sem("agg_lo_ready")
        h_hi_ready, h_lo_ready = sem("h_hi_ready"), sem("h_lo_ready")
        ht_hi_ready, ht_lo_ready = sem("ht_hi_ready"), sem("ht_lo_ready")
        stat1_ready, aggr1_ready, norm1_ready, rstd1_ready, xn_ready = (sem(n) for n in ("stat1_ready", "aggr1_ready", "norm1_ready", "rstd1_ready", "xn_ready"))
        prep_t_done, h_copied = sem("prep_t_done"), sem("h_copied")
        x1_ready, stat2_ready, aggr2_ready, norm2_ready, rstd2_ready = (sem(n) for n in ("x1_ready", "stat2_ready", "aggr2_ready", "norm2_ready", "rstd2_ready"))
        payload_ready, post_t_done, xfT_ready, logits_done = (sem(n) for n in ("payload_ready", "post_t_done", "xfT_ready", "logits_done"))
        gate_weight_ready, both_ready, prefix_done, route = (sem(n) for n in ("gate_weight_ready", "both_ready", "prefix_done", "route"))
        slots_ready = sem("slots_ready")
        row_sent = [sem(f"row_sent{s}") for s in range(S)]
        stored = sem("stored")
        loaded_bias = sem("loaded_bias")
        bias_split_hi, bias_split = sem("bias_split_hi"), sem("bias_split")
        bias_zeroed, bias_placed = sem("bias_zeroed"), sem("bias_placed")
        mapping, mapped, map_done, map_ready = sem("mapping"), sem("mapped"), sem("map_done"), sem("map_ready")
        padded = sem("padded")
        all_sent = sem("all_sent")
        pool_held = sem("pool_held")
        slot_loaded = [sem(f"slot_loaded{u}") for u in range(SLOTS)]
        xs_t_done, xs_hi_ready, xs_lo_ready, up_done, hid_ready = (sem(n) for n in ("xs_t_done", "xs_hi_ready", "xs_lo_ready", "up_done", "hid_ready"))
        hid_t_done, hid_hi_ready, hid_lo_ready, down_done, res_ready = (sem(n) for n in ("hid_t_done", "hid_hi_ready", "hid_lo_ready", "down_done", "res_ready"))
        res_sent = [sem(f"res_sent{u}") for u in range(SLOTS)]
        results_in = sem("results_in")
        loaded_y = [sem(f"loaded_y{q}") for q in range(2)]
        y_step, y_stats, y_aggr, norm3_ready, rstd3_ready = (sem(n) for n in ("y_step", "y_stats", "y_aggr", "norm3_ready", "rstd3_ready"))
        x_beta_ready, final_step, final_ready = sem("x_beta_ready"), sem("final_step"), sem("final_ready")
        final_stored = [sem(f"final_stored{q}") for q in range(2)]

        def post_index(g, s):
            return g * S + s

        block = ctx.enter_context(nc.Block())

        PREP_STAT = {3: 0, 5: 1}
        PREP_NORM = {4: 0, 6: 1}
        POST_STAT = {0: 0, 4: 1}
        POST_NORM = {1: 0, 5: 1}
        POST_T = {2: 0, 6: 1}
        POST_GATE = {3: 0, 7: 1}
        POST_PLACE = {4: 0, 8: 1}
        CONSTS = 15
        TOP_STEPS, ROUTE_STEPS = 5, 9

        def w_piece(i):
            half = i % (LOADS // 2)
            if i < LOADS // 2:
                return w1.rearrange("e h f -> h e f")[:, half * 4:half * 4 + 4, :]
            return w2.rearrange("e (c p) d -> p (e c) d", p=P)[:, half * 8:half * 8 + 8, :]

        def groups(eng, step):
            for k in range(ST):
                step(0, k, True, False)
            with eng.Fori(1, G - 1) as g:
                for k in range(ST):
                    step(g, k, False, False)
            for k in range(ST):
                step(G - 1, k, False, True)

        def pairs(eng, unit):
            for p in range(-1, SLOTS):
                unit(p, p)
            with eng.Fori(1, PAIRS // SLOTS - 1) as i:
                for u in range(SLOTS):
                    unit(i * SLOTS + u, SLOTS + u)
            for p in range(PAIRS - SLOTS, PAIRS + 2):
                unit(p, p)

        def loads_until(p, static):
            u = static % SLOTS
            return (p - u) * (2 * 16 // SLOTS) + 2 * 16

        def batches(eng, unit):
            for b in range(4):
                unit(b, b)
            with eng.Fori(2, B // 2 - 1) as i:
                for q in range(2):
                    unit(i * 2 + q, 4 + q)
            for b in range(B - 2, B + 1):
                unit(b, b)

        @block.sync
        def _(sp):
            sp.dma_start(weight_raw, weight.rearrange("l d e -> d l e")).then_inc(loaded_weights, 16)
            sp.dma_start(w_ih_raw, w_ih.rearrange("(g f) e -> f g e", f=D)).then_inc(loaded_weights, 16)
            sp.dma_start(w_hh_raw, w_hh.rearrange("(g f) e -> f g e", f=D)).then_inc(loaded_weights, 16)
            sp.dma_start(rows[0:3, :], b_ih.rearrange("(g f) -> g f", f=D)).then_inc(loaded_rows, 16)
            sp.dma_start(rows[3:6, :], b_hh.rearrange("(g f) -> g f", f=D)).then_inc(loaded_rows, 16)
            sp.dma_start(rows[6:6 + B * C, :], nodemask.rearrange("b (c p) -> (b c) p", p=P)).then_inc(loaded_rows, 16)
            x_rows = x.rearrange("b (c p) d -> p (b c) d", p=P)
            sp.dma_start(x1[:, 0:S * C, :], x_rows[:, 0:S * C, :]).then_inc(loaded_x0, 16)
            sp.dma_start(adj_raw[0][:, :, :], adj[0].rearrange("(c p) j -> p c j", p=P)).then_inc(loaded_adj[0], 16)
            sp.wait_ge(w_fused, L)
            sp.dma_start(adj_raw[1][:, :, :], adj[1].rearrange("(c p) j -> p c j", p=P)).then_inc(loaded_adj[1], 16)
            sp.dma_start(x1[:, S * C:, :], x_rows[:, S * C:, :]).then_inc(loaded_x, 16)
            sp.dma_start(gate_w_sb[:, :], gate_w).then_inc(loaded_consts, 16)
            sp.dma_start(bias_raw[:, 0:F], b1).then_inc(loaded_bias, 16)
            sp.dma_start(bias_raw[:, F:F + D], b2).then_inc(loaded_bias, 16)
            sp.wait_ge(consts_set, CONSTS)
            sp.dma_start(dispatched[E * REGION:E * REGION + P, :], pad[:, :]).then_inc(padded, 16)
            for dst, src in ((gate_b_sb, gate_b), (gamma_sb, gamma), (beta_sb, beta)):
                sp.dma_start(dst[:, :], src.rearrange("(a n) -> a n", a=1).to_broadcast([P, src.shape[0]])).then_inc(loaded_consts, 16)
            for i in range(2, LOADS):
                src = w_piece(i)
                sp.wait_ge(experts_split, i - 1)
                sp.dma_start(raw[i % 2][:, :].rearrange("p (a b) -> p a b", a=src.shape[1]), src).then_inc(loaded_raw[i % 2], 16)
            with sp.Fori(1, G) as g:
                for s in range(S):
                    sp.wait_ge(edges_ready[s], g)
                    sp.dma_start(adj_raw[s][:, :, :], adj[bass.ds(g * S + s, 1), :, :].rearrange("b (c p) j -> p (b c) j", p=P)).then_inc(loaded_adj[s], 16)
            sp.wait_ge(bias_zeroed, 2)
            for part, row in ((bias_hi[:, :].bitcast(FP32), 0), (bias_lo[:, :], 32)):
                for parts, at, width in ((b1_parts, 0, F), (b2_parts, F, D)):
                    sp.dma_start(parts[row:row + 1, :].bitcast(FP32).rearrange("o (e f) -> o e f", e=E), part[:, at:at + width]).then_inc(bias_placed, 16)
            sp.wait_ge(map_ready, 2)
            for e in range(E):
                row = sp.value_load(pad_rows[0:1, e:e + 1], min_val=e * REGION, max_val=e * REGION + T)
                sp.dma_start(dispatched[bass.ds(row, P), :], pad[:, :]).then_inc(padded, 16)
            sp.wait_ge(padded, (E + 1) * 16)
            sp.wait_ge(all_sent, 1)

            def load_slots(i, reused):
                for u in range(SLOTS):
                    if reused:
                        sp.wait_ge(res_sent[u], i * 2 * 16)
                    for j in range(2):
                        row = sp.value_load(tile_map[0:1, bass.ds(i * (2 * SLOTS) + (2 * u + j + 2 * P), 1)], min_val=0, max_val=E * REGION)
                        sp.dma_start(slot[u][:, j, :], dispatched[bass.ds(row, P), :]).then_inc(slot_loaded[u], 16)

            load_slots(0, False)
            with sp.Fori(1, PAIRS // SLOTS) as i:
                load_slots(i, True)
            sp.wait_ge(results_in, 1)
            result_rows = result.rearrange("(k m p) d -> k p m d", k=K, p=P)

            def load_y(b, static):
                q = static % 2
                if static >= B:
                    return
                if static >= 2:
                    sp.wait_ge(y_step, (b - 1) * 3)
                for k, dst in enumerate((y0[q], y1[q])):
                    sp.dma_start(dst[:, :].rearrange("p (c d) -> p c d", c=C), result_rows[k][:, bass.ds(b * C, C), :]).then_inc(loaded_y[q], 16)

            batches(sp, load_y)

        @block.gpsimd
        def _(pool):
            pool.memset(ident[:, :], 0.0).then_inc(consts_set, 1)
            pool.memset(ones[:, :], 1.0).then_inc(consts_set, 1)
            pool.memset(lower[:, :], 1.0).then_inc(consts_set, 1)
            pool.memset(exponent[:, :], -0.5).then_inc(consts_set, 1)
            pool.wait_ge(consts_set, 1)
            pool.affine_select(out=ident[:, :], in_=ident[:, :], compare_op=ALU.not_equal, fill=1.0, base=0,
                               pattern=[[-1, P]], channel_multiplier=1).then_inc(ident_ready, 1)
            pool.wait_ge(consts_set, 3)
            pool.affine_select(out=lower[:, :], in_=lower[:, :], compare_op=ALU.is_gt, fill=0.0, base=0,
                               pattern=[[1, P]], channel_multiplier=-1).then_inc(consts_set, 1)
            pool.iota(iota_e[:, :], [[1, E]], base=0, channel_multiplier=0, allow_small_or_imprecise_dtypes=True).then_inc(consts_set, 1)
            pool.iota(base_e[:, :], [[REGION, E]], base=0, channel_multiplier=0, allow_small_or_imprecise_dtypes=True).then_inc(consts_set, 1)
            pool.iota(dest[:, :, :], [[P, B * C], [T, K]], base=0, channel_multiplier=1).then_inc(consts_set, 1)

            pool.iota(region_e[:, :], [[REGION, E]], base=0, channel_multiplier=0, allow_small_or_imprecise_dtypes=True).then_inc(consts_set, 1)
            pool.iota(tile_at[:, :], [[P, 2]], base=0, channel_multiplier=1, allow_small_or_imprecise_dtypes=True).then_inc(consts_set, 1)
            pool.memset(no_more[:, :], 0.0).then_inc(consts_set, 1)
            pool.memset(pad[:, 0:D + 1], 0.0).then_inc(consts_set, 1)
            pool.memset(pad[:, D + 1:D + 2].bitcast(I32), SKIP).then_inc(consts_set, 1)
            pool.memset(two_rows[:, :].bitcast(FP32), 0.0).then_inc(consts_set, 1)
            pool.wait_ge(consts_set, 14)
            pool.memset(two_rows[0:1, :].bitcast(FP32), 1.0)
            pool.memset(two_rows[32:33, :].bitcast(FP32), 1.0).then_inc(consts_set, 1)
            pool.wait_ge(consts_set, CONSTS)

            def rstd_of(i, summed, norm, ready):
                pool.wait_ge(summed, i + 1)
                pool.tensor_tensor(norm[:, :, 1], norm[:, :, 1], exponent[:, :], ALU.pow).then_inc(ready, 1)

            def rstd1_of(g, s):
                rstd_of(post_index(g, s), norm1_ready, norm1[s], rstd1_ready)

            def rstd2_of(g, s):
                rstd_of(post_index(g, s), norm2_ready, norm2[s], rstd2_ready)

            def send_rows(g, s):
                i = post_index(g, s)
                pool.wait_ge(consts_set, 4)
                pool.wait_ge(slots_ready, i + 1)
                pool.wait_ge(gate_weight_ready, i + 1)
                for c in range(C):
                    for k in range(K):
                        pool.indirect_dma_start(
                            out=dispatched[:, :],
                            out_offset=bass.IndirectOffsetOnAxis(ap=slots[s][:, c * K + k:c * K + k + 1], axis=0),
                            in_=payload[s][:, c, k, :], in_offset=None).then_inc(row_sent[s], 16)

            def step(g, k, first, last):
                if not first and k in POST_STAT:
                    rstd2_of(g - 1, POST_STAT[k])
                if not last and k in PREP_STAT:
                    rstd1_of(g + 1, PREP_STAT[k])
                if not first and k in POST_PLACE:
                    send_rows(g - 1, POST_PLACE[k])

            for s in range(S):
                rstd1_of(0, s)
            for i in range(LOADS):
                pool.wait_ge(loaded_raw[i % 2], (i // 2 + 1) * 16)
                hi, lo = ((w1_hi, w1_lo) if i < LOADS // 2 else (w2_hi, w2_lo))
                part = slice(i % (LOADS // 2) * 1024, (i % (LOADS // 2) + 1) * 1024)
                pool.tensor_copy(hi[:, part], raw[i % 2]).then_inc(raw_used, 1)
                pool.wait_ge(raw_used, i + 1)
                pool.tensor_tensor(lo[:, part], raw[i % 2], hi[:, part].bitcast(FP32), ALU.subtract).then_inc(experts_split, 1)
            pool.wait_ge(loaded_bias, 32)
            pool.tensor_copy(bias_hi[:, :], bias_raw[:, :]).then_inc(bias_split_hi, 1)
            pool.wait_ge(bias_split_hi, 1)
            pool.tensor_tensor(bias_raw[:, :], bias_raw[:, :], bias_hi[:, :].bitcast(FP32), ALU.subtract).then_inc(bias_split, 1)
            groups(pool, step)
            pool.wait_ge(z_done, G * ST)
            pool.wait_ge(bias_split, 1)
            pool.memset(b1_parts[:, :].bitcast(FP32), 0.0).then_inc(bias_zeroed, 1)
            pool.memset(b2_parts.bitcast(FP32), 0.0).then_inc(bias_zeroed, 1)
            for s in range(S):
                rstd2_of(G - 1, s)
                send_rows(G - 1, s)
            for s in range(S):
                pool.wait_ge(row_sent[s], G * C * K * 16)
            pool.sem_inc(all_sent, 1)

            def hold(n, static):
                if static:
                    pool.wait_ge(pool_held, n)
                pool.tensor_tensor(held_pool[:, :], exponent[:, 0:1], exponent[:, 0:1], ALU.add).then_inc(pool_held, 1)

            def send_results(p, static):
                if not 0 <= static < PAIRS:
                    return
                u = static % SLOTS
                pool.wait_ge(res_ready, p + 1)
                hold(p, static)
                for j in range(2):
                    pool.indirect_dma_start(
                        out=result[:, :], out_offset=bass.IndirectOffsetOnAxis(ap=slot[u][:, j, D + 1:D + 2].bitcast(U32), axis=0),
                        in_=res[u][:, j, :], in_offset=None, bounds_check=K * T - 1, oob_is_err=False).then_inc(res_sent[u], 16)

            pairs(pool, send_results)
            for u in range(SLOTS):
                pool.wait_ge(res_sent[u], PAIRS // SLOTS * 2 * 16)
            pool.sem_inc(results_in, 1)

            def norms(b, static):
                if static < B:
                    q = static % 2
                    if static >= 2:
                        pool.wait_ge(final_ready, b - 1)
                        hold(b - 2 + PAIRS, static)
                    pool.tensor_tensor(x_beta[q][:, :, :], x1[:, bass.ds(b * C, C), :], beta_sb[:, None, :].to_broadcast([P, C, D]), ALU.add).then_inc(x_beta_ready, 1)
                    rstd_of(b, norm3_ready, norm1[q], rstd3_ready)

            batches(pool, norms)

        @block.tensor
        def _(pe):
            def mm3(ps, w_hi, w_lo, v_hi, v_lo, start, stop):
                pe.matmul(ps, lhsT=w_hi, rhs=v_lo, start=start, stop=False)
                pe.matmul(ps, lhsT=w_lo, rhs=v_hi, start=False, stop=False)
                return pe.matmul(ps, lhsT=w_hi, rhs=v_hi, start=False, stop=stop)

            R, Z, NN = (slice(i * D, (i + 1) * D) for i in range(3))

            pe.wait_ge(ident_ready, 1)
            pe.wait_ge(loaded_rows, 48)
            nrow = 2 * 3 + B * C
            pe.transpose(ps_agg[:, 0:nrow], rows[:, :], ident[0:nrow, 0:nrow]).then_inc(w_transposed, 1)
            pe.wait_ge(loaded_weights, 48)
            for i in range(3):
                pe.transpose(ps_in[:, i * D:(i + 1) * D], w_ih_raw[:, i, :], ident[:, :])
                last = pe.transpose(ps_hn[:, i * D:(i + 1) * D], w_hh_raw[:, i, :], ident[:, :])
            for l in range(L):
                last = pe.transpose((ps_r if l < 4 else ps_z)[:, (l % 4) * D:(l % 4 + 1) * D], weight_raw[:, l, :], ident[:, :])
            last.then_inc(w_transposed, 1)
            pe.wait_ge(w_copied, 4)
            fused_bank = [ps_t, ps_prep, ps_post, ps_r, ps_z]
            for l in range(L):
                pe.matmul(fused_bank[l][:, 0:3 * D], lhsT=weightT[:, l, :], rhs=w_ihT, start=True, stop=True).then_inc(w_fused, 1)
            pe.wait_ge(w_lo_ready, L + 1)

            def aggregate(st, g, s):
                pe.wait_ge(ht_lo_ready, st + 1)
                pe.wait_ge(agg_lo_ready, st)
                for c in range(C):
                    pe.matmul(ps_agg[:, :], lhsT=ht_lo[s][:, c, :], rhs=edges[s][:, c, :], start=(c == 0), stop=False)
                    last = pe.matmul(ps_agg[:, :], lhsT=ht_hi[s][:, c, :], rhs=edges[s][:, c, :], start=False, stop=(c == C - 1))
                last.then_inc(agg_done, 1)

            def hidden_gates(st, s):
                pe.wait_ge(h_lo_ready, st + 1)
                pe.wait_ge(rh_done, st)
                mm3(ps_hn[:, :], w_hh_hi[:, NN], w_hh_lo[:, NN], h_hi[s], h_lo[s], True, True)
                pe.wait_ge(z_ready, st)
                mm3(ps_r[:, :], w_hh_hi[:, R], w_hh_lo[:, R], h_hi[s], h_lo[s], True, False)
                mm3(ps_z[:, :], w_hh_hi[:, Z], w_hh_lo[:, Z], h_hi[s], h_lo[s], True, False)

            def input_gates(st, l):
                pe.wait_ge(agg_lo_ready, st + 1)
                mm3(ps_r[:, :], w_fused_hi[:, l, R], w_fused_lo[:, l, R], agg_hi[:, :], agg_lo[:, :], False, True).then_inc(r_done, 1)
                pe.wait_ge(pre_n_ready, st)
                mm3(ps_in[:, :], w_fused_hi[:, l, NN], w_fused_lo[:, l, NN], agg_hi[:, :], agg_lo[:, :], True, True).then_inc(in_done, 1)
                mm3(ps_z[:, :], w_fused_hi[:, l, Z], w_fused_lo[:, l, Z], agg_hi[:, :], agg_lo[:, :], False, True).then_inc(z_done, 1)

            def transpose_prepared(g, s):
                pe.wait_ge(xn_ready, post_index(g, s) + 1)
                for c in range(C):
                    last = pe.transpose(ps_prep[:, c * P:(c + 1) * P], xn[s][:, c, :], ident[:, :])
                last.then_inc(prep_t_done, 1)

            def transpose_post(g, s):
                i = post_index(g, s)
                pe.wait_ge(payload_ready, i + 1)
                pe.wait_ge(slots_ready, i)
                for c in range(C):
                    last = pe.transpose(ps_post[:, c * P:(c + 1) * P], payload[s][:, c, 0, 0:D], ident[:, :])
                last.then_inc(post_t_done, 1)

            def gate(g, s):
                i = post_index(g, s)
                pe.wait_ge(xfT_ready, i + 1)
                for c in range(C):
                    last = pe.matmul(ps_post[:, c * E:(c + 1) * E], lhsT=xfT[:, c * P:(c + 1) * P], rhs=gate_w_sb[:, :], start=True, stop=True)
                last.then_inc(logits_done, 1)

            def count(g, s):
                i = post_index(g, s)
                pe.wait_ge(both_ready, i + 1)
                pe.matmul(ps_post[:, 0:C * E], lhsT=lower[:, :], rhs=both[:, :], start=True, stop=False, skip_group_check=True)
                for c in range(1, C):
                    pe.matmul(ps_post[:, c * E:C * E], lhsT=ones[:, :], rhs=both[:, 0:(C - c) * E], start=False, stop=(c == C - 1), skip_group_check=True)
                for c in range(C):
                    last = pe.matmul(ps_post[:, C * E:(C + 1) * E], lhsT=ones[:, :], rhs=both[:, c * E:(c + 1) * E], start=False, stop=(c == C - 1), skip_group_check=True)
                last.then_inc(prefix_done, 1)

            def step(g, k, first, last):
                st = g * ST + k
                s, l = k % S, k // S
                input_gates(st, l)
                if not (last and k == ST - 1):
                    if k == ST - 1:
                        pe.wait_ge(edges_ready[0], g + 2)
                    elif k + 1 < S:
                        pe.wait_ge(edges_ready[k + 1], g + 1)
                    aggregate(st + 1, g, (k + 1) % S)
                    hidden_gates(st + 1, (k + 1) % S)
                pe.wait_ge(h_ready, st + 1)
                if k == 0:
                    if not first:
                        pe.wait_ge(x1_ready, g * S)
                elif k == ST - 1:
                    pe.wait_ge(x1_ready, g * S + 1)
                else:
                    pe.wait_ge(ht_lo_ready, st + 2)
                for c in range(C):
                    t = pe.transpose(ps_t[:, c * P:(c + 1) * P], h[s][:, c * P:(c + 1) * P], ident[:, :])
                t.then_inc(t_done, 1)
                if k >= ST - S and not last:
                    transpose_prepared(g + 1, s)
                if not first and k in POST_T:
                    transpose_post(g - 1, POST_T[k])
                if not first and k in POST_GATE:
                    gate(g - 1, POST_GATE[k])
                if not first and k in POST_PLACE:
                    count(g - 1, POST_PLACE[k])

            for s in range(S):
                if s:
                    pe.wait_ge(h_lo_ready, s)
                transpose_prepared(0, s)
            pe.wait_ge(edges_ready[0], 1)
            aggregate(0, 0, 0)
            hidden_gates(0, 0)

            groups(pe, step)
            for s in range(S):
                transpose_post(G - 1, s)
                gate(G - 1, s)
                count(G - 1, s)

            pe.wait_ge(mapped, 1)
            for i in range(2):
                for j in range(2):
                    last = pe.matmul(ps_post[0:1, (i * 2 + j) * P:(i * 2 + j + 1) * P], lhsT=clipped[:, i, j:j + 1], rhs=ident[:, :], start=True, stop=True)
            last.then_inc(map_done, 1)
            pe.wait_ge(map_ready, 2)
            pe.wait_ge(bias_placed, 4 * 16)
            pe.wait_ge(experts_split, LOADS)

            def experts_of(p):
                return [pe.value_load(tile_map[0:1, bass.ds(p * 2 + j, 1)], min_val=0, max_val=E - 1) for j in range(2)]

            def unit(p, static):
                q = static % 2
                if 0 <= static < PAIRS:
                    e = experts_of(p)
                    pe.wait_ge(xs_lo_ready, p + 1)
                    if static >= 2:
                        pe.wait_ge(hid_ready, p - 1)
                    for j in range(2):
                        o = ps_up[q][:, j * F:(j + 1) * F]
                        hi, lo = (xs[q][:, j * P:(j + 1) * P] for xs in (xs_hi, xs_lo))
                        pe.matmul(o, lhsT=two_rows[:, :], rhs=b1_parts[:, bass.ds(e[j] * F, F)], start=True, stop=False)
                        pe.matmul(o, lhsT=lo, rhs=w1_hi[:, bass.ds(e[j] * F, F)], start=False, stop=False)
                        pe.matmul(o, lhsT=hi, rhs=w1_lo[:, bass.ds(e[j] * F, F)], start=False, stop=False)
                        last = pe.matmul(o, lhsT=hi, rhs=w1_hi[:, bass.ds(e[j] * F, F)], start=False, stop=True)
                    last.then_inc(up_done, 1)
                if 0 <= static - 1 < PAIRS:
                    r = 1 - q
                    pe.wait_ge(hid_ready, p)
                    if static >= 3:
                        pe.wait_ge(hid_lo_ready, p - 2)
                    for j in range(2):
                        for c in range(FC):
                            last = pe.transpose(ps_hid[r][:, (j * FC + c) * P:(j * FC + c + 1) * P], hid[r][:, j, c * P:(c + 1) * P], ident[:, :])
                    last.then_inc(hid_t_done, 1)
                if 0 <= static - 2 < PAIRS:
                    e = experts_of(p - 2)
                    pe.wait_ge(hid_lo_ready, p - 1)
                    if static >= 4:
                        pe.wait_ge(res_ready, p - 3)
                    for j in range(2):
                        o = ps_down[q][:, j * D:(j + 1) * D]
                        pe.matmul(o, lhsT=two_rows[:, :], rhs=b2_parts[:, bass.ds(e[j] * D, D)], start=True, stop=False)
                        for c in range(FC):
                            hi, lo = (x[q][:, (j * FC + c) * P:(j * FC + c + 1) * P] for x in (hid_hi, hid_lo))
                            at = e[j] * (FC * D) + c * D
                            pe.matmul(o, lhsT=lo, rhs=w2_hi[:, bass.ds(at, D)], start=False, stop=False)
                            pe.matmul(o, lhsT=hi, rhs=w2_lo[:, bass.ds(at, D)], start=False, stop=False)
                            last = pe.matmul(o, lhsT=hi, rhs=w2_hi[:, bass.ds(at, D)], start=False, stop=(c == FC - 1))
                    last.then_inc(down_done, 1)
                if 0 <= static + 1 < PAIRS:
                    r = 1 - q
                    u = (static + 1) % SLOTS
                    pe.wait_ge(slot_loaded[u], loads_until(p + 1, static + 1))
                    if static >= 1:
                        pe.wait_ge(xs_lo_ready, p)
                    for j in range(2):
                        last = pe.transpose(ps_xs[r][:, j * P:(j + 1) * P], slot[u][:, j, 0:D], ident[:, :])
                    last.then_inc(xs_t_done, 1)

            pairs(pe, unit)

        @block.scalar
        def _(act):
            def copy(o, i):
                return act.activation(o, i, ACT.Copy)

            for i in range(2):
                src = w_piece(i)
                act.dma_start(raw[i][:, :].rearrange("p (a b) -> p a b", a=src.shape[1]), src).then_inc(loaded_raw[i], 16)
            act.wait_ge(w_transposed, 2)
            copy(w_hh_hi[:, :], ps_hn[:, 0:3 * D]).then_inc(w_hi_ready, 1)
            fused_bank = [ps_t, ps_prep, ps_post, ps_r, ps_z]
            for l in range(L):
                act.wait_ge(w_fused, l + 1)
                copy(w_fused_hi[:, l, :], fused_bank[l][:, 0:3 * D]).then_inc(w_hi_ready, 1)

            def prepared(g, s, i):
                act.wait_ge(xn_ready, post_index(g, s) + 1)
                copy(ht_hi[s], xn[s][:, :, :]).then_inc(ht_hi_ready, 1)
                act.wait_ge(prep_t_done, post_index(g, s) + 1)
                copy(h[s][:, :], ps_prep[:, :]).then_inc(h_copied, 1)
                copy(h_hi[s], ps_prep[:, :]).then_inc(h_hi_ready, 1)

            def split_agg(st):
                act.wait_ge(agg_done, st + 1)
                copy(agg_hi[:, :], ps_agg[:, :]).then_inc(agg_hi_ready, 1)

            def post_copy(g, s):
                i = post_index(g, s)
                act.wait_ge(post_t_done, i + 1)
                copy(xfT[:, :], ps_post[:, :]).then_inc(xfT_ready, 1)

            def gate_weights(g, s):
                i = post_index(g, s)
                act.wait_ge(both_ready, i + 1)
                act.activation(payload[s][:, :, :, D], margin[:, :, :], ACT.Sigmoid).then_inc(gate_weight_ready, 1)

            def step(g, k, first, last):
                st = g * ST + k
                s = k % S
                act.wait_ge(r_done, st + 1)
                act.wait_ge(rh_done, st)
                act.activation(r_sb[:, :], ps_r[:, :], ACT.Sigmoid, bias=bias_rz[:, 0:1]).then_inc(r_ready, 1)
                act.wait_ge(z_done, st + 1)
                act.wait_ge(zd_ready, st)
                act.activation(z_sb[:, :], ps_z[:, :], ACT.Sigmoid, bias=bias_rz[:, 1:2]).then_inc(z_ready, 1)
                act.wait_ge(pre_n_ready, st + 1)
                act.activation(n_sb[:, :], t_sb[:, :], ACT.Tanh, bias=cols[:, 2:3]).then_inc(n_ready, 1)
                if not (last and k == ST - 1):
                    split_agg(st + 1)
                if k < ST - S:
                    act.wait_ge(h_ready, st + 1)
                    copy(h_hi[s], h[s][:, :]).then_inc(h_hi_ready, 1)
                    act.wait_ge(t_done, st + 1)
                    copy(ht_hi[s], ps_t[:, :].rearrange("p (c d) -> p c d", c=C)).then_inc(ht_hi_ready, 1)
                elif not last:
                    act.wait_ge(t_done, st + 1)
                    prepared(g + 1, s, st + 2)
                if not first and k in POST_T:
                    post_copy(g - 1, POST_T[k])
                if not first and k in POST_PLACE:
                    gate_weights(g - 1, POST_PLACE[k])

            act.wait_ge(bias_ready, 1)
            for s in range(S):
                prepared(0, s, s)
            split_agg(0)
            groups(act, step)
            for s in range(S):
                post_copy(G - 1, s)
                gate_weights(G - 1, s)

            def unit(p, static):
                q = static % 2
                if 0 <= static < PAIRS:
                    act.wait_ge(up_done, p + 1)
                    if static >= 2:
                        act.wait_ge(hid_t_done, p - 1)
                    act.activation(hid[q], ps_up[q][:, :].rearrange("p (j f) -> p j f", j=2), ACT.Relu).then_inc(hid_ready, 1)
                if 0 <= static - 1 < PAIRS:
                    r = 1 - q
                    act.wait_ge(hid_t_done, p)
                    if static >= 3:
                        act.wait_ge(down_done, p - 2)
                    copy(hid_hi[r], ps_hid[r][:, :]).then_inc(hid_hi_ready, 1)
                if 0 <= static + 1 < PAIRS:
                    r = 1 - q
                    act.wait_ge(xs_t_done, p + 2)
                    if static >= 1:
                        act.wait_ge(up_done, p)
                    copy(xs_hi[r], ps_xs[r][:, 0:2 * P]).then_inc(xs_hi_ready, 1)

            pairs(act, unit)

            out_rows = out.rearrange("b (c p) d -> p (b c) d", p=P)

            def store(b, static):
                if static >= 1:
                    q = (static - 1) % 2
                    act.wait_ge(final_ready, b)
                    act.dma_start(out_rows[:, bass.ds((b - 1) * C, C), :], final[q]).then_inc(final_stored[q], 16)

            batches(act, store)
            for q in range(2):
                act.wait_ge(final_stored[q], B // 2 * 16)

        @block.vector
        def _(dve):
            v = dve
            v.wait_ge(w_transposed, 1)
            v.tensor_copy(cols[:, :], ps_agg[:, 0:2 * 3 + B * C]).then_inc(bias_ready, 1)
            v.wait_ge(w_transposed, 2)
            v.tensor_copy(w_ihT, ps_in[:, 0:3 * D]).then_inc(w_copied, 1)
            v.tensor_copy(weightT[:, 0:4, :].rearrange("p l e -> p (l e)"), ps_r[:, :]).then_inc(w_copied, 1)
            v.tensor_copy(weightT[:, 4, :], ps_z[:, 0:D]).then_inc(w_copied, 1)
            v.wait_ge(bias_ready, 1)
            v.tensor_tensor(bias_rz[:, :], cols[:, 0:2], cols[:, 3:5], ALU.add).then_inc(w_copied, 1)
            v.wait_ge(w_hi_ready, 1)
            v.tensor_tensor(w_hh_lo[:, :], ps_hn[:, 0:3 * D], w_hh_hi[:, :].bitcast(FP32), ALU.subtract).then_inc(w_lo_ready, 1)
            fused_bank = [ps_t, ps_prep, ps_post, ps_r, ps_z]
            for l in range(L):
                v.wait_ge(w_hi_ready, l + 2)
                v.tensor_tensor(w_fused_lo[:, l, :], fused_bank[l][:, 0:3 * D], w_fused_hi[:, l, :].bitcast(FP32), ALU.subtract).then_inc(w_lo_ready, 1)

            def make_edges(g, s):
                v.wait_ge(loaded_adj[s], (g + 1) * 16)
                v.tensor_scalar(edges[s][:, :, :], adj_raw[s][:, :, :], 0.0, None, ALU.not_equal).then_inc(edges_ready[s], 1)

            def aggregate_stats(stat, norm, stat_ready, aggr_ready, ready, i):
                v.wait_ge(stat_ready, (i + 1) * C)
                v.memset(held[:, :], 0.0)
                for c in range(C):
                    last = v.bn_aggr(norm[:, c, :], stat[:, c, :])
                last.then_inc(aggr_ready, 1)
                v.wait_ge(aggr_ready, i + 1)
                v.tensor_scalar(norm[:, :, 1], norm[:, :, 1], EPS, None, ALU.add).then_inc(ready, 1)

            def prep_stats(g, s):
                i = post_index(g, s)
                for c in range(C):
                    v.bn_stats(stat1[:, c, :], x1[:, bass.ds(i * C + c, 1), :]).then_inc(stat1_ready, 1)
                aggregate_stats(stat1, norm1[s], stat1_ready, aggr1_ready, norm1_ready, i)

            def prep_norm(g, s):
                i = post_index(g, s)
                v.wait_ge(rstd1_ready, i + 1)
                for c in range(C):
                    last = v.tensor_scalar(xn[s][:, c, :], x1[:, bass.ds(i * C + c, 1), :], norm1[s][:, c, 0:1], norm1[s][:, c, 1:2],
                                           ALU.subtract, ALU.mult)
                last.then_inc(xn_ready, 1)

            def prepared(g, s, i):
                v.wait_ge(ht_hi_ready, i + 1)
                v.tensor_tensor(ht_lo[s], xn[s][:, :, :], ht_hi[s].bitcast(FP32), ALU.subtract).then_inc(ht_lo_ready, 1)
                v.wait_ge(h_hi_ready, i + 1)
                v.tensor_tensor(h_lo[s], ps_prep[:, :], h_hi[s].bitcast(FP32), ALU.subtract).then_inc(h_lo_ready, 1)

            def split_agg(st):
                v.wait_ge(agg_hi_ready, st + 1)
                v.tensor_tensor(agg_lo[:, :], ps_agg[:, :], agg_hi[:, :].bitcast(FP32), ALU.subtract).then_inc(agg_lo_ready, 1)

            def post_x1(g, s):
                i = post_index(g, s)
                v.wait_ge(t_done, g * ST + ST - S + s + 1)
                for c in range(C):
                    b = i * C + c
                    last = v.scalar_tensor_tensor(x1[:, bass.ds(b, 1), :], ps_t[:, c * P:(c + 1) * P], cols[:, bass.ds(6 + b, 1)],
                                                  x1[:, bass.ds(b, 1), :], ALU.mult, ALU.add)
                last.then_inc(x1_ready, 1)

            def post_stats(g, s):
                i = post_index(g, s)
                v.wait_ge(x1_ready, i + 1)
                for c in range(C):
                    v.bn_stats(stat2[:, c, :], x1[:, bass.ds(i * C + c, 1), :]).then_inc(stat2_ready, 1)
                aggregate_stats(stat2, norm2[s], stat2_ready, aggr2_ready, norm2_ready, i)

            def post_norm(g, s):
                i = post_index(g, s)
                v.wait_ge(rstd2_ready, i + 1)
                if isinstance(g, int) and g == 0:
                    v.wait_ge(experts_split, LOADS)
                else:
                    v.wait_ge(row_sent[s], g * C * K * 16)
                for c in range(C):
                    b = i * C + c
                    v.tensor_scalar(payload[s][:, c, :, 0:D], x1[:, bass.ds(b, 1), :].to_broadcast([P, K, D]),
                                    norm2[s][:, c, 0:1], norm2[s][:, c, 1:2], ALU.subtract, ALU.mult)
                v.tensor_copy(norm2_all[:, bass.ds(i * C, C), :], norm2[s][:, :, :])
                v.tensor_copy(payload[s][:, :, :, D + 1].bitcast(I32), dest[:, bass.ds(i * C, C), :]).then_inc(payload_ready, 1)

            def post_gate(g, s, part):
                i = post_index(g, s)
                done = [0 if part == 0 else TOP_STEPS]

                def chain(ins, then_max=False):
                    done[0] += 1
                    ins.then_inc(route, 1)
                    v.wait_ge(route, i * ROUTE_STEPS + done[0])
                    if then_max:
                        v.memset(held[:, :], 0.0)

                if part == 0:
                    v.wait_ge(logits_done, i + 1)
                    chain(v.tensor_tensor(logits[:, :, :], ps_post[:, 0:C * E].rearrange("p (c e) -> p c e", c=C),
                                          gate_b_sb[:, None, :].to_broadcast([P, C, E]), ALU.add), True)
                    for c in range(C):
                        last = v.max(top[:, c, :], logits[:, c, :])
                    chain(last)
                    v.tensor_tensor(margin[:, :, 0], top[:, :, 0], top[:, :, 1], ALU.subtract)
                    v.tensor_tensor(margin[:, :, 1], top[:, :, 1], top[:, :, 0], ALU.subtract)
                    for c in range(C):
                        last = v.max_index(top_at[:, c, :], top[:, c, :], logits[:, c, :])
                    chain(last)
                    chain(v.tensor_copy(chosen[:, :, :], top_at[:, :, 0:K]))
                    chain(v.tensor_tensor(onehot[:, :, :, :], iota_e[:, None, None, :].to_broadcast([P, C, K, E]),
                                          chosen[:, :, :, None].to_broadcast([P, C, K, E]), ALU.is_equal))
                    v.tensor_tensor(both[:, :].rearrange("p (c e) -> p c e", c=C), onehot[:, :, 0, :], onehot[:, :, 1, :], ALU.add).then_inc(both_ready, 1)
                else:
                    v.wait_ge(prefix_done, i + 1)
                    chain(v.tensor_tensor(place[:, :, :], ps_post[:, 0:C * E].rearrange("p (c e) -> p c e", c=C),
                                          base_e[:, None, :].to_broadcast([P, C, E]), ALU.add))
                    chain(v.tensor_tensor(base_e[:, :], ps_post[:, C * E:(C + 1) * E], base_e[:, :], ALU.add))
                    for k in range(K):
                        last = v.tensor_tensor(picked[:, :, k, :], onehot[:, :, k, :], place[:, :, :], ALU.mult)
                    chain(last)
                    chain(v.tensor_reduce(slots_f[:, :, :], picked[:, :, :, :], AX.X, ALU.add))
                    v.tensor_copy(slots[s][:, :].rearrange("p (c k) -> p c k", c=C), slots_f[:, :, :]).then_inc(slots_ready, 1)
                assert done[0] == (ROUTE_STEPS if part else TOP_STEPS)

            def step(g, k, first, last):
                st = g * ST + k
                s = k % S
                v.wait_ge(r_ready, st + 1)
                v.scalar_tensor_tensor(t_sb[:, :], ps_hn[:, :], cols[:, 5:6], r_sb[:, :], ALU.add, ALU.mult).then_inc(rh_done, 1)
                v.wait_ge(in_done, st + 1)
                v.wait_ge(rh_done, st + 1)
                v.tensor_tensor(t_sb[:, :], ps_in[:, :], t_sb[:, :], ALU.add).then_inc(pre_n_ready, 1)
                if first is False and k in POST_STAT:
                    post_stats(g - 1, POST_STAT[k])
                v.wait_ge(n_ready, st + 1)
                v.tensor_tensor(d_sb[:, :], h[s][:, :], n_sb[:, :], ALU.subtract).then_inc(d_ready, 1)
                v.wait_ge(d_ready, st + 1)
                v.tensor_tensor(d_sb[:, :], d_sb[:, :], z_sb[:, :], ALU.mult).then_inc(zd_ready, 1)
                v.wait_ge(zd_ready, st + 1)
                v.tensor_tensor(h[s][:, :], n_sb[:, :], d_sb[:, :], ALU.add).then_inc(h_ready, 1)
                if not (last and k == ST - 1):
                    split_agg(st + 1)
                if k < ST - S:
                    v.wait_ge(h_hi_ready, st + 3)
                    v.tensor_tensor(h_lo[s], h[s][:, :], h_hi[s].bitcast(FP32), ALU.subtract).then_inc(h_lo_ready, 1)
                    v.wait_ge(ht_hi_ready, st + 3)
                    v.tensor_tensor(ht_lo[s], ps_t[:, :].rearrange("p (c d) -> p c d", c=C), ht_hi[s].bitcast(FP32), ALU.subtract).then_inc(ht_lo_ready, 1)
                else:
                    post_x1(g, s)
                    if not last:
                        v.wait_ge(agg_done, st + 1)
                        make_edges(g + 1, s)
                        prepared(g + 1, s, st + 2)
                if not last and k in PREP_STAT:
                    prep_stats(g + 1, PREP_STAT[k])
                if not last and k in PREP_NORM:
                    prep_norm(g + 1, PREP_NORM[k])
                if not first and k in POST_NORM:
                    post_norm(g - 1, POST_NORM[k])
                if not first and k in POST_GATE:
                    post_gate(g - 1, POST_GATE[k], 0)
                if not first and k in POST_PLACE:
                    post_gate(g - 1, POST_PLACE[k], 1)

            v.wait_ge(loaded_x0, 16)
            for s in range(S):
                make_edges(0, s)
                prep_stats(0, s)
            for s in range(S):
                prep_norm(0, s)
            for s in range(S):
                prepared(0, s, s)
            split_agg(0)
            v.wait_ge(loaded_x, 16)
            v.wait_ge(loaded_consts, 64)
            v.wait_ge(consts_set, CONSTS)
            groups(v, step)
            for s in range(S):
                post_stats(G - 1, s)
                post_norm(G - 1, s)
                post_gate(G - 1, s, 0)
                post_gate(G - 1, s, 1)

            steps = [0]

            def chain(ins):
                steps[0] += 1
                ins.then_inc(mapping, 1)
                v.wait_ge(mapping, steps[0])

            v.wait_ge(slots_ready, B)
            v.tensor_copy(pad_rows[:, :], base_e[0:1, :]).then_inc(map_ready, 1)
            chain(v.tensor_tensor(count_f[:, :], base_e[:, :], region_e[:, :], ALU.subtract))
            chain(v.tensor_scalar(count_i[:, :], count_f[:, :], float(P - 1), None, ALU.add))
            chain(v.tensor_scalar(count_i[:, :], count_i[:, :], 7, None, ALU.arith_shift_right))
            chain(v.tensor_copy(tiles_e[:, :], count_i[:, :]))
            chain(v.tensor_tensor_scan(tile_end[:, :], tiles_e[:, :], no_more[:, :], 0.0, ALU.add, ALU.add))
            chain(v.tensor_tensor(ended[:, :, :], tile_end[:, None, :].to_broadcast([P, 2, E]), tile_at[:, :, None].to_broadcast([P, 2, E]), ALU.is_le))
            v.tensor_reduce(tile_expert[:, :], ended[:, :, :], AX.X, ALU.add)
            chain(v.tensor_tensor(ended_tiles[:, :, :], ended[:, :, :], tiles_e[:, None, :].to_broadcast([P, 2, E]), ALU.mult))
            chain(v.tensor_reduce(tile_first[:, :], ended_tiles[:, :, :], AX.X, ALU.add))
            chain(v.tensor_tensor(tile_first[:, :], tile_at[:, :], tile_first[:, :], ALU.subtract))
            chain(v.tensor_scalar(tile_first[:, :], tile_first[:, :], float(P), None, ALU.mult))
            chain(v.scalar_tensor_tensor(tile_row[:, :], tile_expert[:, :], float(REGION), tile_first[:, :], ALU.mult, ALU.add))
            v.tensor_scalar(clipped[:, 1, :], tile_row[:, :], float(E * REGION), None, ALU.min)
            v.tensor_scalar(clipped[:, 0, :], tile_expert[:, :], float(E - 1), None, ALU.min).then_inc(mapped, 1)
            v.wait_ge(map_done, 1)
            v.tensor_copy(tile_map, ps_post[0:1, :]).then_inc(map_ready, 1)

            def unit(p, static):
                q = static % 2
                if 0 <= static - 1 < PAIRS:
                    r = 1 - q
                    v.wait_ge(hid_hi_ready, p)
                    v.tensor_tensor(hid_lo[r], ps_hid[r][:, :], hid_hi[r].bitcast(FP32), ALU.subtract).then_inc(hid_lo_ready, 1)
                if 0 <= static + 1 < PAIRS:
                    r = 1 - q
                    v.wait_ge(xs_hi_ready, p + 2)
                    v.tensor_tensor(xs_lo[r], ps_xs[r][:, 0:2 * P], xs_hi[r].bitcast(FP32), ALU.subtract).then_inc(xs_lo_ready, 1)
                if 0 <= static - 2 < PAIRS:
                    u = (static - 2) % SLOTS
                    v.wait_ge(down_done, p - 1)
                    for j in range(2):
                        last = v.tensor_scalar(res[u][:, j, :], ps_down[q][:, j * D:(j + 1) * D], slot[u][:, j, D:D + 1], None, ALU.mult)
                    last.then_inc(res_ready, 1)

            pairs(v, unit)

            def finish(b, static):
                q = static % 2
                if static < B:
                    for c in range(C):
                        i = b * C + c
                        last = v.tensor_scalar(y[q][:, c * D:(c + 1) * D], x1[:, bass.ds(i, 1), :], norm2_all[:, bass.ds(i, 1), 0], norm2_all[:, bass.ds(i, 1), 1],
                                               ALU.subtract, ALU.mult)
                    last.then_inc(y_step, 1)
                    v.wait_ge(y_step, b * 3 + 1)
                    v.wait_ge(loaded_y[q], ((b - q) // 2 + 1) * 32 if isinstance(b, int) else (b - q) * 16 + 32)
                    v.tensor_tensor(y[q][:, :], y[q][:, :], y0[q][:, :], ALU.add).then_inc(y_step, 1)
                    v.wait_ge(y_step, b * 3 + 2)
                    v.tensor_tensor(y[q][:, :], y[q][:, :], y1[q][:, :], ALU.add).then_inc(y_step, 1)
                    v.wait_ge(y_step, b * 3 + 3)
                    for c in range(C):
                        last = v.bn_stats(stat2[:, c, :], y[q][:, c * D:(c + 1) * D])
                    last.then_inc(y_stats, 1)
                    v.wait_ge(y_stats, b + 1)
                    v.memset(held[:, :], 0.0)
                    for c in range(C):
                        last = v.bn_aggr(norm1[q][:, c, :], stat2[:, c, :])
                    last.then_inc(y_aggr, 1)
                    v.wait_ge(y_aggr, b + 1)
                    v.tensor_scalar(norm1[q][:, :, 1], norm1[q][:, :, 1], EPS, None, ALU.add).then_inc(norm3_ready, 1)
                if static >= 1:
                    r = 1 - q
                    v.wait_ge(rstd3_ready, b)
                    if static >= 3:
                        v.wait_ge(final_stored[r], (b - 1 - r) * 8)
                    for c in range(C):
                        last = v.tensor_scalar(final[r][:, c, :], y[r][:, c * D:(c + 1) * D], norm1[r][:, c, 0:1], norm1[r][:, c, 1:2], ALU.subtract, ALU.mult)
                    last.then_inc(final_step, 1)
                    v.wait_ge(final_step, b * 2 - 1)
                    v.tensor_tensor(final[r], final[r], gamma_sb[:, None, :].to_broadcast([P, C, D]), ALU.mult).then_inc(final_step, 1)
                    v.wait_ge(final_step, b * 2)
                    v.wait_ge(x_beta_ready, b)
                    v.tensor_tensor(final[r], final[r], x_beta[r][:, :, :], ALU.add).then_inc(final_ready, 1)

            batches(v, finish)


_INS = ['x', 'adj', 'nodemask', 'L0_gnn_weight', 'L0_gnn_w_ih', 'L0_gnn_w_hh', 'L0_gnn_b_ih', 'L0_gnn_b_hh',
        'L0_ffn_gate_w', 'L0_ffn_gate_b', 'L0_ffn_w1', 'L0_ffn_b1', 'L0_ffn_w2', 'L0_ffn_b2', 'L0_ffn_gamma', 'L0_ffn_beta']


def kernel(**inputs):
    import numpy as np
    import concourse.bacc as bacc
    from concourse import mybir as mb
    from concourse.bass_utils import run_bass_kernel_spmd

    nc = bacc.Bacc("TRN2", target_bir_lowering=False, num_devices=1)
    arrays, args = {}, []
    for name in _INS:
        a = np.ascontiguousarray(inputs[name])
        arrays[f"in_{name}"] = a
        args.append(nc.dram_tensor(f"in_{name}", a.shape, mb.dt.from_np(a.dtype), kind="ExternalInput").ap())
    out = nc.dram_tensor("out_x", inputs["x"].shape, mb.dt.from_np(np.dtype("float32")), kind="ExternalOutput").ap()
    build(nc, *args, out)
    r = run_bass_kernel_spmd(nc, [arrays], core_ids=[0])
    return r.results[0]["out_x"]
```

```python
import concourse.bass as bass
from concourse import mybir
from contextlib import ExitStack

FP32 = mybir.dt.float32
FP32R = mybir.dt.float32r
BF16 = mybir.dt.bfloat16
I32 = mybir.dt.int32
U32 = mybir.dt.uint32
ALU = mybir.AluOpType
ACT = mybir.ActivationFunctionType
AX = mybir.AxisListType

EPS = 1e-5
P = 128


def build(nc, x, adj, nodemask, weight, w_ih, w_hh, b_ih, b_hh, gate_w, gate_b, w1, b1, w2, b2, gamma, beta, out):
    B, N, D = x.shape
    L = weight.shape[0]
    E, _, F = w1.shape
    K = 2
    C = N // P
    FC = F // P
    T = B * N
    S = 2
    G = B // S
    ST = S * L
    ROW = D + 2
    REGION = T + P
    TILES = (K * T + E * (P - 1)) // P
    SLOTS = 8
    TILES += -TILES % (2 * SLOTS)
    PAIRS = TILES // 2
    SKIP = 1 << 20
    RING = 4
    LOADS = 8

    dispatched = nc.dram_tensor("dispatched", [E * REGION + P, ROW], FP32, kind="Internal").ap()
    result = nc.dram_tensor("result", [K * T, D], FP32, kind="Internal").ap()

    ctx = ExitStack()
    with ctx:
        def sb(name, shape, dt=FP32):
            return ctx.enter_context(nc.sbuf_tensor(name, shape, dt))

        def sem(name):
            return ctx.enter_context(nc.semaphore(name))

        ident = sb("ident", [P, P])
        lower = sb("lower", [P, P], BF16)
        ones = sb("ones", [P, P], BF16)
        iota_e = sb("iota_e", [P, E])
        exponent = sb("exponent", [P, C])
        dest = sb("dest", [P, B * C, K], I32)
        pad = sb("pad", [P, ROW])
        rows = sb("rows", [2 * 3 + B * C, P])
        cols = sb("cols", [P, 2 * 3 + B * C])
        bias_rz = sb("bias_rz", [P, 2])
        w_fused_hi = sb("w_fused_hi", [P, L, 3 * D], FP32R)
        w_fused_lo = sb("w_fused_lo", [P, L, 3 * D], FP32R)
        w_hh_hi = sb("w_hh_hi", [P, 3 * D], FP32R)
        w_hh_lo = sb("w_hh_lo", [P, 3 * D], FP32R)
        gate_w_sb = sb("gate_w_sb", [P, E])
        gate_b_sb = sb("gate_b_sb", [P, E])
        gamma_sb = sb("gamma_sb", [P, D])
        beta_sb = sb("beta_sb", [P, D])
        w1_hi = sb("w1_hi", [P, E * F], FP32R)
        w1_lo = sb("w1_lo", [P, E * F], FP32R)
        w2_hi = sb("w2_hi", [P, E * FC * D], FP32R)
        w2_lo = sb("w2_lo", [P, E * FC * D], FP32R)
        x1 = sb("x1", [P, B * C, D])
        norm2_all = sb("norm2_all", [P, B * C, 2])
        base_e = sb("base_e", [P, E])
        adj_raw = [sb(f"adj_raw{s}", [P, C, N]) for s in range(S)]
        edges_all = sb("edges_all", [P, S * C * N], FP32R)
        edges = [edges_all[:, s * C * N:(s + 1) * C * N].rearrange("p (c n) -> p c n", c=C) for s in range(S)]
        h = [sb(f"h{s}", [P, N]) for s in range(S)]
        halves = sb("halves", [P, S, 4, N], FP32R)
        h_hi, h_lo = ([halves[:, s, i, :] for s in range(S)] for i in (0, 1))
        ht_hi, ht_lo = ([halves[:, s, i, :].rearrange("p (c d) -> p c d", c=C) for s in range(S)] for i in (2, 3))
        agg_hi = sb("agg_hi", [P, N], FP32R)
        agg_lo = sb("agg_lo", [P, N], FP32R)
        r_sb = sb("r_sb", [P, N])
        z_sb = sb("z_sb", [P, N])
        n_sb = sb("n_sb", [P, N])
        t_sb = sb("t_sb", [P, N])
        d_sb = sb("d_sb", [P, N])
        xn = [sb(f"xn{s}", [P, C, D]) for s in range(S)]
        held = sb("held", [P, 1])
        held_pool = sb("held_pool", [P, 1])
        stat1 = sb("stat1", [P, C, 6])
        norm1 = [sb(f"norm1{s}", [P, C, 2]) for s in range(S)]
        norm2 = [sb(f"norm2{s}", [P, C, 2]) for s in range(S)]
        stat2 = sb("stat2", [P, C, 6])
        payload = [sb(f"payload{s}", [P, C, K, ROW]) for s in range(S)]
        xfT = sb("xfT", [P, N])
        logits = sb("logits", [P, C, E])
        top = sb("top", [P, C, 8])
        top_at = sb("top_at", [P, C, 8], U32)
        chosen = sb("chosen", [P, C, K])
        onehot = sb("onehot", [P, C, K, E])
        both = sb("both", [P, C * E], BF16)
        margin = sb("margin", [P, C, K])
        place = sb("place", [P, C, E])
        picked = sb("picked", [P, C, K, E])
        slots_f = sb("slots_f", [P, C, K])
        slots = [sb(f"slots{s}", [P, C * K], U32) for s in range(S)]
        region_e = sb("region_e", [P, E])
        tile_at = sb("tile_at", [P, 2])
        count_i = sb("count_i", [P, E], I32)
        count_f = sb("count_f", [P, E])
        tiles_e = sb("tiles_e", [P, E])
        tile_end = sb("tile_end", [P, E])
        no_more = sb("no_more", [P, E])
        ended = sb("ended", [P, 2, E])
        ended_tiles = sb("ended_tiles", [P, 2, E])
        tile_expert = sb("tile_expert", [P, 2])
        tile_first = sb("tile_first", [P, 2])
        tile_row = sb("tile_row", [P, 2])
        clipped = sb("clipped", [P, 2, 2])
        tile_map = d_sb[0:1, 0:4 * P].bitcast(I32)
        pad_rows = sb("pad_rows", [1, E], I32)
        bias_raw = sb("bias_raw", [E, F + D])
        bias_hi = sb("bias_hi", [E, F + D], FP32R)
        bias_lo = bias_raw
        two_rows = sb("two_rows", [P, P], FP32R)
        b1_parts = edges_all
        b2_parts = halves[:, 0, :, :].rearrange("p i n -> p (i n)")
        assert E * F == S * C * N and E * D == 4 * N
        room = [adj_raw[q][:, 1:4, :].rearrange("p c n -> p (c n)") for q in range(2)]
        out_room = [payload[q][:, :, :, :].rearrange("p c k r -> p (c k r)") for q in range(2)]
        slot = [room[u % 2][:, u // 2 * 2 * ROW:(u // 2 + 1) * 2 * ROW].rearrange("p (j r) -> p j r", j=2) for u in range(SLOTS)]
        res = [out_room[u % 2][:, u // 2 * 2 * D:(u // 2 + 1) * 2 * D].rearrange("p (j d) -> p j d", j=2) for u in range(SLOTS)]
        hid = [adj_raw[q][:, 0, :].rearrange("p (j f) -> p j f", j=2) for q in range(2)]
        xs_hi, xs_lo = ([halves[:, 1, i, q * 2 * P:(q + 1) * 2 * P] for q in range(2)] for i in (0, 1))
        hid_hi = [halves[:, 1, 2, :], agg_hi[:, :]]
        hid_lo = [halves[:, 1, 3, :], agg_lo[:, :]]
        y0, y1 = ([edges_all[:, (k * 4 + q) * N:(k * 4 + q + 1) * N].bitcast(FP32) for q in range(RING)] for k in range(K))
        y_sum = [h[0][:, :], h[1][:, :]] + [xn[q][:, :, :].rearrange("p c d -> p (c d)") for q in range(2)]
        y = [r_sb[:, :], z_sb[:, :], n_sb[:, :], t_sb[:, :]]
        x_beta = [adj_raw[0][:, q, :].rearrange("p (c d) -> p c d", c=C) for q in range(RING)]
        final = [adj_raw[1][:, q, :].rearrange("p (c d) -> p c d", c=C) for q in range(RING)]
        norm3 = [sb(f"norm3{q}", [P, C, 2]) for q in range(RING)]
        weight_raw = adj_raw[1][:, 0:2, :].rearrange("p c n -> p (c n)")[:, 0:L * D].rearrange("p (l e) -> p l e", l=L)
        w_ih_raw = h[0][:, 0:3 * D].rearrange("p (g e) -> p g e", g=3)
        w_hh_raw = h[1][:, 0:3 * D].rearrange("p (g e) -> p g e", g=3)
        weightT = adj_raw[1][:, 2:4, :].rearrange("p c n -> p (c n)")[:, 0:L * D].rearrange("p (l e) -> p l e", l=L)
        w_ihT = d_sb[:, 0:3 * D]
        raw = [payload[0][:, :, :, :].rearrange("p c k r -> p (c k r)")[:, 0:1024],
               payload[1][:, :, :, :].rearrange("p c k r -> p (c k r)")[:, 0:1024]]

        bank = [ctx.enter_context(nc.psum_tensor(f"bank{i}", [P, 512], FP32)) for i in range(8)]
        ps_agg, ps_r, ps_z, ps_in, ps_hn, ps_t, ps_prep, ps_post = bank
        ps_up, ps_hid, ps_down, ps_xs = bank[0:2], bank[2:4], bank[4:6], bank[6:8]

        loaded_weights = sem("loaded_weights")
        loaded_rows = sem("loaded_rows")
        loaded_consts = sem("loaded_consts")
        loaded_x0 = sem("loaded_x0")
        loaded_x = sem("loaded_x")
        loaded_adj = [sem(f"loaded_adj{s}") for s in range(S)]
        loaded_raw = [sem(f"loaded_raw{s}") for s in range(2)]
        raw_used = sem("raw_used")
        experts_split = sem("experts_split")
        consts_set = sem("consts_set")
        ident_ready = sem("ident_ready")
        w_transposed = sem("w_transposed")
        w_copied = sem("w_copied")
        w_fused = sem("w_fused")
        w_hi_ready = sem("w_hi_ready")
        w_lo_ready = sem("w_lo_ready")
        bias_ready = sem("bias_ready")
        edges_ready = [sem(f"edges_ready{s}") for s in range(S)]
        agg_done, r_done, in_done, z_done, t_done = (sem(f"{n}_done") for n in ("agg", "r", "in", "z", "t"))
        r_ready, z_ready, n_ready = (sem(f"{n}_ready") for n in "rzn")
        rh_done, pre_n_ready, d_ready, zd_ready, h_ready = (sem(n) for n in ("rh_done", "pre_n_ready", "d_ready", "zd_ready", "h_ready"))
        agg_hi_ready, agg_lo_ready = sem("agg_hi_ready"), sem("agg_lo_ready")
        h_hi_ready, h_lo_ready = sem("h_hi_ready"), sem("h_lo_ready")
        ht_hi_ready, ht_lo_ready = sem("ht_hi_ready"), sem("ht_lo_ready")
        stat1_ready, aggr1_ready, norm1_ready, rstd1_ready, xn_ready = (sem(n) for n in ("stat1_ready", "aggr1_ready", "norm1_ready", "rstd1_ready", "xn_ready"))
        prep_t_done, h_copied = sem("prep_t_done"), sem("h_copied")
        power1_ready, power2_ready, power3_ready = (sem(f"power{i}_ready") for i in (1, 2, 3))
        x1_ready, stat2_ready, aggr2_ready, norm2_ready, rstd2_ready = (sem(n) for n in ("x1_ready", "stat2_ready", "aggr2_ready", "norm2_ready", "rstd2_ready"))
        payload_ready, post_t_done, xfT_ready, logits_done = (sem(n) for n in ("payload_ready", "post_t_done", "xfT_ready", "logits_done"))
        gate_weight_ready, both_ready, prefix_done, route = (sem(n) for n in ("gate_weight_ready", "both_ready", "prefix_done", "route"))
        slots_ready = sem("slots_ready")
        row_sent = [sem(f"row_sent{s}") for s in range(S)]
        stored = sem("stored")
        loaded_bias = sem("loaded_bias")
        bias_split_hi, bias_split = sem("bias_split_hi"), sem("bias_split")
        bias_zeroed, bias_placed = sem("bias_zeroed"), sem("bias_placed")
        mapping, mapped, map_done, map_ready = sem("mapping"), sem("mapped"), sem("map_done"), sem("map_ready")
        padded = sem("padded")
        all_sent = sem("all_sent")
        pool_held = sem("pool_held")
        slot_loaded = [sem(f"slot_loaded{u}") for u in range(SLOTS)]
        xs_t_done, xs_hi_ready, xs_lo_ready, up_done, hid_ready = (sem(n) for n in ("xs_t_done", "xs_hi_ready", "xs_lo_ready", "up_done", "hid_ready"))
        hid_t_done, hid_hi_ready, hid_lo_ready, down_done, res_ready = (sem(n) for n in ("hid_t_done", "hid_hi_ready", "hid_lo_ready", "down_done", "res_ready"))
        res_sent = [sem(f"res_sent{u}") for u in range(SLOTS)]
        results_in = sem("results_in")
        loaded_y = [sem(f"loaded_y{q}") for q in range(RING)]
        y_sum_ready, xf_ready, y_ready, y_stats, y_aggr, norm3_ready, rstd3_ready = (sem(n) for n in ("y_sum_ready", "xf_ready", "y_ready", "y_stats", "y_aggr", "norm3_ready", "rstd3_ready"))
        x_beta_ready, yn_ready, scaled_ready, final_ready = (sem(n) for n in ("x_beta_ready", "yn_ready", "scaled_ready", "final_ready"))
        final_stored = [sem(f"final_stored{q}") for q in range(RING)]

        def post_index(g, s):
            return g * S + s

        block = ctx.enter_context(nc.Block())

        PREP_STAT = {2: 0, 5: 1}
        PREP_NORM = {3: 0, 6: 1}
        POST_STAT = {0: 0, 1: 1}
        POST_NORM = {0: 0, 2: 1}
        POST_T = {1: 0, 4: 1}
        POST_GATE = {2: 0, 5: 1}
        POST_TOP = {3: 0, 6: 1}
        POST_COUNT = {3: 0, 6: 1}
        POST_PLACE = {4: 0, 7: 1}
        SEND = {4: (0, 0), 5: (0, 1), 7: (1, 0), 8: (1, 1)}
        CONSTS = 15
        TOP_STEPS, ROUTE_STEPS = 5, 9

        def w_piece(i):
            half = i % (LOADS // 2)
            if i < LOADS // 2:
                return w1.rearrange("e h f -> h e f")[:, half * 4:half * 4 + 4, :]
            return w2.rearrange("e (c p) d -> p (e c) d", p=P)[:, half * 8:half * 8 + 8, :]

        def groups(eng, step):
            for k in range(ST):
                step(0, k, True, False)
            with eng.Fori(1, G - 1) as g:
                for k in range(ST):
                    step(g, k, False, False)
            for k in range(ST):
                step(G - 1, k, False, True)

        def pairs(eng, unit):
            for p in range(-2, SLOTS):
                unit(p, p)
            with eng.Fori(1, PAIRS // SLOTS - 1) as i:
                for u in range(SLOTS):
                    unit(i * SLOTS + u, SLOTS + u)
            for p in range(PAIRS - SLOTS, PAIRS + 2):
                unit(p, p)

        def loads_until(p, static):
            u = static % SLOTS
            return (p - u) * (2 * 16 // SLOTS) + 2 * 16

        def tile_values(eng, at, n, most):
            _, values = nc.values_load_multi_w_load_instructions(
                tile_map[0:1, bass.ds(at, n)], engines=[eng.engine], min_val=0, max_val=most, bass_reorder=False,
                skip_runtime_bounds_check_because="the map is a sum of counts from 0 on, clipped to these bounds on the chip")
            return values

        def batches(eng, unit):
            first, turns = RING + 1, (B - 3 - (RING + 1)) // RING
            for b in range(-3, first):
                unit(b, b)
            with eng.Fori(0, turns) as i:
                for q in range(RING):
                    unit(i * RING + (first + q), first + q)
            for b in range(first + turns * RING, B + 2):
                unit(b, b)

        @block.sync
        def _(sp):
            sp.dma_start(weight_raw, weight.rearrange("l d e -> d l e")).then_inc(loaded_weights, 16)
            sp.dma_start(w_ih_raw, w_ih.rearrange("(g f) e -> f g e", f=D)).then_inc(loaded_weights, 16)
            sp.dma_start(w_hh_raw, w_hh.rearrange("(g f) e -> f g e", f=D)).then_inc(loaded_weights, 16)
            sp.dma_start(rows[0:3, :], b_ih.rearrange("(g f) -> g f", f=D)).then_inc(loaded_rows, 16)
            sp.dma_start(rows[3:6, :], b_hh.rearrange("(g f) -> g f", f=D)).then_inc(loaded_rows, 16)
            sp.dma_start(rows[6:6 + B * C, :], nodemask.rearrange("b (c p) -> (b c) p", p=P)).then_inc(loaded_rows, 16)
            x_rows = x.rearrange("b (c p) d -> p (b c) d", p=P)
            sp.dma_start(x1[:, 0:S * C, :], x_rows[:, 0:S * C, :]).then_inc(loaded_x0, 16)
            sp.dma_start(adj_raw[0][:, :, :], adj[0].rearrange("(c p) j -> p c j", p=P)).then_inc(loaded_adj[0], 16)
            sp.wait_ge(w_fused, L)
            sp.dma_start(adj_raw[1][:, :, :], adj[1].rearrange("(c p) j -> p c j", p=P)).then_inc(loaded_adj[1], 16)
            sp.dma_start(x1[:, S * C:, :], x_rows[:, S * C:, :]).then_inc(loaded_x, 16)
            sp.dma_start(gate_w_sb[:, :], gate_w).then_inc(loaded_consts, 16)
            sp.dma_start(bias_raw[:, 0:F], b1).then_inc(loaded_bias, 16)
            sp.dma_start(bias_raw[:, F:F + D], b2).then_inc(loaded_bias, 16)
            sp.wait_ge(consts_set, CONSTS)
            sp.dma_start(dispatched[E * REGION:E * REGION + P, :], pad[:, :]).then_inc(padded, 16)
            for dst, src in ((gate_b_sb, gate_b), (gamma_sb, gamma), (beta_sb, beta)):
                sp.dma_start(dst[:, :], src.rearrange("(a n) -> a n", a=1).to_broadcast([P, src.shape[0]])).then_inc(loaded_consts, 16)
            for i in range(2, LOADS):
                src = w_piece(i)
                sp.wait_ge(experts_split, i - 1)
                sp.dma_start(raw[i % 2][:, :].rearrange("p (a b) -> p a b", a=src.shape[1]), src).then_inc(loaded_raw[i % 2], 16)
            with sp.Fori(1, G) as g:
                for s in range(S):
                    sp.wait_ge(edges_ready[s], g)
                    sp.dma_start(adj_raw[s][:, :, :], adj[bass.ds(g * S + s, 1), :, :].rearrange("b (c p) j -> p (b c) j", p=P)).then_inc(loaded_adj[s], 16)
            sp.wait_ge(bias_zeroed, 2)
            for part, row in ((bias_hi[:, :].bitcast(FP32), 0), (bias_lo[:, :], 32)):
                for parts, at, width in ((b1_parts, 0, F), (b2_parts, F, D)):
                    sp.dma_start(parts[row:row + 1, :].bitcast(FP32).rearrange("o (e f) -> o e f", e=E), part[:, at:at + width]).then_inc(bias_placed, 16)
            sp.wait_ge(map_ready, 2)
            for e in range(E):
                row = sp.value_load(pad_rows[0:1, e:e + 1], min_val=e * REGION, max_val=e * REGION + T)
                sp.dma_start(dispatched[bass.ds(row, P), :], pad[:, :]).then_inc(padded, 16)
            sp.wait_ge(padded, (E + 1) * 16)
            sp.wait_ge(all_sent, 1)

            def load_slots(i, reused):
                for u in range(SLOTS):
                    if reused:
                        sp.wait_ge(res_sent[u], i * 2 * 16)
                    for j, row in enumerate(tile_values(sp, i * (2 * SLOTS) + (2 * u + 2 * P), 2, E * REGION)):
                        sp.dma_start(slot[u][:, j, :], dispatched[bass.ds(row, P), :]).then_inc(slot_loaded[u], 16)

            load_slots(0, False)
            with sp.Fori(1, PAIRS // SLOTS) as i:
                load_slots(i, True)
            sp.wait_ge(results_in, 1)
            result_rows = result.rearrange("(k m p) d -> k p m d", k=K, p=P)

            out_rows = out.rearrange("b (c p) d -> p (b c) d", p=P)

            def move(b, static):
                if static + 3 < B:
                    q = (static + 3) % RING
                    if static >= 1:
                        sp.wait_ge(y_sum_ready, b)
                    for k, dst in enumerate((y0[q], y1[q])):
                        sp.dma_start(dst.rearrange("p (c d) -> p c d", c=C), result_rows[k][:, bass.ds((b + 3) * C, C), :]).then_inc(loaded_y[q], 16)
                if static >= 2:
                    q = (static - 2) % RING
                    sp.wait_ge(final_ready, b - 1)
                    sp.dma_start(out_rows[:, bass.ds((b - 2) * C, C), :], final[q]).then_inc(final_stored[q], 16)

            batches(sp, move)
            for q in range(RING):
                sp.wait_ge(final_stored[q], B // RING * 16)

        @block.gpsimd
        def _(pool):
            pool.memset(ident[:, :], 0.0).then_inc(consts_set, 1)
            pool.memset(ones[:, :], 1.0).then_inc(consts_set, 1)
            pool.memset(lower[:, :], 1.0).then_inc(consts_set, 1)
            pool.memset(exponent[:, :], -0.5).then_inc(consts_set, 1)
            pool.wait_ge(consts_set, 1)
            pool.affine_select(out=ident[:, :], in_=ident[:, :], compare_op=ALU.not_equal, fill=1.0, base=0,
                               pattern=[[-1, P]], channel_multiplier=1).then_inc(ident_ready, 1)
            pool.wait_ge(consts_set, 3)
            pool.affine_select(out=lower[:, :], in_=lower[:, :], compare_op=ALU.is_gt, fill=0.0, base=0,
                               pattern=[[1, P]], channel_multiplier=-1).then_inc(consts_set, 1)
            pool.iota(iota_e[:, :], [[1, E]], base=0, channel_multiplier=0, allow_small_or_imprecise_dtypes=True).then_inc(consts_set, 1)
            pool.iota(base_e[:, :], [[REGION, E]], base=0, channel_multiplier=0, allow_small_or_imprecise_dtypes=True).then_inc(consts_set, 1)
            pool.iota(dest[:, :, :], [[P, B * C], [T, K]], base=0, channel_multiplier=1).then_inc(consts_set, 1)

            pool.iota(region_e[:, :], [[REGION, E]], base=0, channel_multiplier=0, allow_small_or_imprecise_dtypes=True).then_inc(consts_set, 1)
            pool.iota(tile_at[:, :], [[P, 2]], base=0, channel_multiplier=1, allow_small_or_imprecise_dtypes=True).then_inc(consts_set, 1)
            pool.memset(no_more[:, :], 0.0).then_inc(consts_set, 1)
            pool.memset(pad[:, 0:D + 1], 0.0).then_inc(consts_set, 1)
            pool.memset(pad[:, D + 1:D + 2].bitcast(I32), SKIP).then_inc(consts_set, 1)
            pool.memset(two_rows[:, :].bitcast(FP32), 0.0).then_inc(consts_set, 1)
            pool.wait_ge(consts_set, 14)
            pool.memset(two_rows[0:1, :].bitcast(FP32), 1.0)
            pool.memset(two_rows[32:33, :].bitcast(FP32), 1.0).then_inc(consts_set, 1)
            pool.wait_ge(consts_set, CONSTS)

            def rstd_of(i, summed, norm, powered, ready):
                pool.wait_ge(summed, i + 1)
                pool.tensor_tensor(norm[:, :, 1], norm[:, :, 1], exponent[:, :], ALU.pow).then_inc(powered, 1)
                pool.wait_ge(powered, i + 1)
                pool.tensor_tensor(norm[:, :, 0], norm[:, :, 0], norm[:, :, 1], ALU.mult).then_inc(ready, 1)

            def low_part(s, i):
                pool.wait_ge(h_hi_ready, i + 1)
                pool.tensor_tensor(h_lo[s], h[s][:, :], h_hi[s].bitcast(FP32), ALU.subtract).then_inc(h_lo_ready, 1)

            def rstd1_of(g, s):
                rstd_of(post_index(g, s), norm1_ready, norm1[s], power1_ready, rstd1_ready)

            def rstd2_of(g, s):
                rstd_of(post_index(g, s), norm2_ready, norm2[s], power2_ready, rstd2_ready)

            def send_rows(g, s, half):
                i = post_index(g, s)
                pool.wait_ge(consts_set, 4)
                pool.wait_ge(slots_ready, i + 1)
                pool.wait_ge(gate_weight_ready, i + 1)
                for c in range(half * C // 2, (half + 1) * C // 2):
                    for k in range(K):
                        pool.indirect_dma_start(
                            out=dispatched[:, :],
                            out_offset=bass.IndirectOffsetOnAxis(ap=slots[s][:, c * K + k:c * K + k + 1], axis=0),
                            in_=payload[s][:, c, k, :], in_offset=None).then_inc(row_sent[s], 16)

            def step(g, k, first, last):
                if not first and k in POST_STAT:
                    rstd2_of(g - 1, POST_STAT[k])
                if not last and k in PREP_STAT:
                    rstd1_of(g + 1, PREP_STAT[k])
                if not (last and k >= ST - S):
                    low_part(k % S, g * ST + k + S)
                if not first and k in SEND:
                    send_rows(g - 1, *SEND[k])

            for s in range(S):
                rstd1_of(0, s)
            for s in range(S):
                low_part(s, s)
            for i in range(LOADS):
                pool.wait_ge(loaded_raw[i % 2], (i // 2 + 1) * 16)
                hi, lo = ((w1_hi, w1_lo) if i < LOADS // 2 else (w2_hi, w2_lo))
                part = slice(i % (LOADS // 2) * 1024, (i % (LOADS // 2) + 1) * 1024)
                pool.tensor_copy(hi[:, part], raw[i % 2]).then_inc(raw_used, 1)
                pool.wait_ge(raw_used, i + 1)
                pool.tensor_tensor(lo[:, part], raw[i % 2], hi[:, part].bitcast(FP32), ALU.subtract).then_inc(experts_split, 1)
            pool.wait_ge(loaded_bias, 32)
            pool.tensor_copy(bias_hi[:, :], bias_raw[:, :]).then_inc(bias_split_hi, 1)
            pool.wait_ge(bias_split_hi, 1)
            pool.tensor_tensor(bias_raw[:, :], bias_raw[:, :], bias_hi[:, :].bitcast(FP32), ALU.subtract).then_inc(bias_split, 1)
            groups(pool, step)
            pool.wait_ge(z_done, G * ST)
            pool.wait_ge(bias_split, 1)
            pool.memset(b1_parts[:, :].bitcast(FP32), 0.0).then_inc(bias_zeroed, 1)
            pool.memset(b2_parts.bitcast(FP32), 0.0).then_inc(bias_zeroed, 1)
            for s in range(S):
                rstd2_of(G - 1, s)
                for half in range(2):
                    send_rows(G - 1, s, half)
            for s in range(S):
                pool.wait_ge(row_sent[s], G * C * K * 16)
            pool.sem_inc(all_sent, 1)

            def hold(n, static):
                if static:
                    pool.wait_ge(pool_held, n)
                pool.tensor_tensor(held_pool[:, :], exponent[:, 0:1], exponent[:, 0:1], ALU.add).then_inc(pool_held, 1)

            def send_results(p, static):
                if not 0 <= static < PAIRS:
                    return
                u = static % SLOTS
                pool.wait_ge(res_ready, p + 1)
                hold(p, static)
                for j in range(2):
                    pool.indirect_dma_start(
                        out=result[:, :], out_offset=bass.IndirectOffsetOnAxis(ap=slot[u][:, j, D + 1:D + 2].bitcast(U32), axis=0),
                        in_=res[u][:, j, :], in_offset=None, bounds_check=K * T - 1, oob_is_err=False).then_inc(res_sent[u], 16)

            pairs(pool, send_results)
            for u in range(SLOTS):
                pool.wait_ge(res_sent[u], PAIRS // SLOTS * 2 * 16)
            pool.sem_inc(results_in, 1)

            def norms(b, static):
                if 0 <= static + 1 < B:
                    q = (static + 1) % RING
                    pool.wait_ge(loaded_y[q], (b + 1 - q) * (32 // RING) + 32)
                    if static + 1 >= RING:
                        pool.wait_ge(final_ready, b + 2 - RING)
                    pool.tensor_tensor(y_sum[q], y0[q], y1[q], ALU.add).then_inc(y_sum_ready, 1)
                    pool.tensor_tensor(x_beta[q], x1[:, bass.ds((b + 1) * C, C), :], beta_sb[:, None, :].to_broadcast([P, C, D]), ALU.add).then_inc(x_beta_ready, 1)
                if 0 <= static < B:
                    rstd_of(b, norm3_ready, norm3[static % RING], power3_ready, rstd3_ready)

            batches(pool, norms)

        @block.tensor
        def _(pe):
            def mm3(ps, w_hi, w_lo, v_hi, v_lo, start, stop):
                pe.matmul(ps, lhsT=w_hi, rhs=v_lo, start=start, stop=False)
                pe.matmul(ps, lhsT=w_lo, rhs=v_hi, start=False, stop=False)
                return pe.matmul(ps, lhsT=w_hi, rhs=v_hi, start=False, stop=stop)

            R, Z, NN = (slice(i * D, (i + 1) * D) for i in range(3))

            pe.wait_ge(ident_ready, 1)
            pe.wait_ge(loaded_rows, 48)
            nrow = 2 * 3 + B * C
            pe.transpose(ps_agg[:, 0:nrow], rows[:, :], ident[0:nrow, 0:nrow]).then_inc(w_transposed, 1)
            pe.wait_ge(loaded_weights, 48)
            for i in range(3):
                pe.transpose(ps_in[:, i * D:(i + 1) * D], w_ih_raw[:, i, :], ident[:, :])
                last = pe.transpose(ps_hn[:, i * D:(i + 1) * D], w_hh_raw[:, i, :], ident[:, :])
            for l in range(L):
                last = pe.transpose((ps_r if l < 4 else ps_z)[:, (l % 4) * D:(l % 4 + 1) * D], weight_raw[:, l, :], ident[:, :])
            last.then_inc(w_transposed, 1)
            pe.wait_ge(w_copied, 4)
            fused_bank = [ps_t, ps_prep, ps_post, ps_r, ps_z]
            for l in range(L):
                pe.matmul(fused_bank[l][:, 0:3 * D], lhsT=weightT[:, l, :], rhs=w_ihT, start=True, stop=True).then_inc(w_fused, 1)
            pe.wait_ge(w_lo_ready, L + 1)

            def aggregate(st, g, s):
                pe.wait_ge(ht_lo_ready, st + 1)
                pe.wait_ge(agg_lo_ready, st)
                for c in range(C):
                    pe.matmul(ps_agg[:, :], lhsT=ht_lo[s][:, c, :], rhs=edges[s][:, c, :], start=(c == 0), stop=False)
                    last = pe.matmul(ps_agg[:, :], lhsT=ht_hi[s][:, c, :], rhs=edges[s][:, c, :], start=False, stop=(c == C - 1))
                last.then_inc(agg_done, 1)

            def hidden_gates(st, s):
                pe.wait_ge(h_lo_ready, st + 1)
                pe.wait_ge(rh_done, st)
                mm3(ps_hn[:, :], w_hh_hi[:, NN], w_hh_lo[:, NN], h_hi[s], h_lo[s], True, True)
                pe.wait_ge(z_ready, st)
                mm3(ps_r[:, :], w_hh_hi[:, R], w_hh_lo[:, R], h_hi[s], h_lo[s], True, False)
                mm3(ps_z[:, :], w_hh_hi[:, Z], w_hh_lo[:, Z], h_hi[s], h_lo[s], True, False)

            def input_gates(st, l):
                pe.wait_ge(agg_lo_ready, st + 1)
                mm3(ps_r[:, :], w_fused_hi[:, l, R], w_fused_lo[:, l, R], agg_hi[:, :], agg_lo[:, :], False, True).then_inc(r_done, 1)
                pe.wait_ge(pre_n_ready, st)
                mm3(ps_in[:, :], w_fused_hi[:, l, NN], w_fused_lo[:, l, NN], agg_hi[:, :], agg_lo[:, :], True, True).then_inc(in_done, 1)
                mm3(ps_z[:, :], w_fused_hi[:, l, Z], w_fused_lo[:, l, Z], agg_hi[:, :], agg_lo[:, :], False, True).then_inc(z_done, 1)

            def transpose_prepared(g, s):
                pe.wait_ge(xn_ready, post_index(g, s) + 1)
                for c in range(C):
                    last = pe.transpose(ps_prep[:, c * P:(c + 1) * P], xn[s][:, c, :], ident[:, :])
                last.then_inc(prep_t_done, 1)

            def transpose_post(g, s):
                i = post_index(g, s)
                pe.wait_ge(payload_ready, i + 1)
                pe.wait_ge(slots_ready, i)
                for c in range(C):
                    last = pe.transpose(ps_post[:, c * P:(c + 1) * P], payload[s][:, c, 0, 0:D], ident[:, :])
                last.then_inc(post_t_done, 1)

            def gate(g, s):
                i = post_index(g, s)
                pe.wait_ge(xfT_ready, i + 1)
                for c in range(C):
                    last = pe.matmul(ps_post[:, c * E:(c + 1) * E], lhsT=xfT[:, c * P:(c + 1) * P], rhs=gate_w_sb[:, :], start=True, stop=True)
                last.then_inc(logits_done, 1)

            def count(g, s):
                i = post_index(g, s)
                pe.wait_ge(both_ready, i + 1)
                pe.matmul(ps_post[:, 0:C * E], lhsT=lower[:, :], rhs=both[:, :], start=True, stop=False, skip_group_check=True)
                for c in range(1, C):
                    pe.matmul(ps_post[:, c * E:C * E], lhsT=ones[:, :], rhs=both[:, 0:(C - c) * E], start=False, stop=(c == C - 1), skip_group_check=True)
                for c in range(C):
                    last = pe.matmul(ps_post[:, C * E:(C + 1) * E], lhsT=ones[:, :], rhs=both[:, c * E:(c + 1) * E], start=False, stop=(c == C - 1), skip_group_check=True)
                last.then_inc(prefix_done, 1)

            def step(g, k, first, last):
                st = g * ST + k
                s, l = k % S, k // S
                input_gates(st, l)
                if not (last and k == ST - 1):
                    if k == ST - 1:
                        pe.wait_ge(edges_ready[0], g + 2)
                    elif k + 1 < S:
                        pe.wait_ge(edges_ready[k + 1], g + 1)
                    aggregate(st + 1, g, (k + 1) % S)
                    hidden_gates(st + 1, (k + 1) % S)
                if not first and k in POST_T:
                    transpose_post(g - 1, POST_T[k])
                if not first and k in POST_GATE:
                    gate(g - 1, POST_GATE[k])
                if not first and k in POST_COUNT:
                    count(g - 1, POST_COUNT[k])
                if k == 0:
                    if not first:
                        pe.wait_ge(x1_ready, g * S)
                elif k == ST - 1:
                    pe.wait_ge(x1_ready, g * S + 1)
                else:
                    pe.wait_ge(ht_lo_ready, st + 2)
                for c in range(C):
                    if c % (C // 2) == 0:
                        pe.wait_ge(h_ready, st * 2 + c // (C // 2) + 1)
                    t = pe.transpose(ps_t[:, c * P:(c + 1) * P], h[s][:, c * P:(c + 1) * P], ident[:, :])
                t.then_inc(t_done, 1)
                if k >= ST - S and not last:
                    transpose_prepared(g + 1, s)

            for s in range(S):
                if s:
                    pe.wait_ge(h_hi_ready, s)
                transpose_prepared(0, s)
            pe.wait_ge(edges_ready[0], 1)
            aggregate(0, 0, 0)
            hidden_gates(0, 0)

            groups(pe, step)
            for s in range(S):
                transpose_post(G - 1, s)
                gate(G - 1, s)
                count(G - 1, s)

            pe.wait_ge(mapped, 1)
            for i in range(2):
                for j in range(2):
                    last = pe.matmul(ps_post[0:1, (i * 2 + j) * P:(i * 2 + j + 1) * P], lhsT=clipped[:, i, j:j + 1], rhs=ident[:, :], start=True, stop=True)
            last.then_inc(map_done, 1)
            pe.wait_ge(map_ready, 2)
            pe.wait_ge(bias_placed, 4 * 16)
            pe.wait_ge(experts_split, LOADS)

            def experts_of(p):
                return tile_values(pe, p * 2, 2, E - 1)

            def unit(p, static):
                q = static % 2
                up, hidden, down, rows_in = (0 <= static + ahead < PAIRS for ahead in (0, -1, -2, 2))
                e_up = experts_of(p) if up else None
                e_down = experts_of(p - 2) if down else None
                if up:
                    pe.wait_ge(xs_lo_ready, p + 1)
                    if static >= 2:
                        pe.wait_ge(hid_ready, p - 1)
                    for j in range(2):
                        o = ps_up[q][:, j * F:(j + 1) * F]
                        hi, lo = (xs[q][:, j * P:(j + 1) * P] for xs in (xs_hi, xs_lo))
                        pe.matmul(o, lhsT=two_rows[:, :], rhs=b1_parts[:, bass.ds(e_up[j] * F, F)], start=True, stop=False)
                        pe.matmul(o, lhsT=lo, rhs=w1_hi[:, bass.ds(e_up[j] * F, F)], start=False, stop=False)
                        pe.matmul(o, lhsT=hi, rhs=w1_lo[:, bass.ds(e_up[j] * F, F)], start=False, stop=False)
                        last = pe.matmul(o, lhsT=hi, rhs=w1_hi[:, bass.ds(e_up[j] * F, F)], start=False, stop=True)
                    last.then_inc(up_done, 1)
                if hidden:
                    r = 1 - q
                    pe.wait_ge(hid_ready, p)
                    if static >= 3:
                        pe.wait_ge(hid_lo_ready, p - 2)
                    for j in range(2):
                        for c in range(FC):
                            last = pe.transpose(ps_hid[r][:, (j * FC + c) * P:(j * FC + c + 1) * P], hid[r][:, j, c * P:(c + 1) * P], ident[:, :])
                    last.then_inc(hid_t_done, 1)
                if rows_in:
                    u = (static + 2) % SLOTS
                    pe.wait_ge(slot_loaded[u], loads_until(p + 2, static + 2))
                    if static >= 0:
                        pe.wait_ge(xs_lo_ready, p + 1)
                    for j in range(2):
                        last = pe.transpose(ps_xs[q][:, j * P:(j + 1) * P], slot[u][:, j, 0:D], ident[:, :])
                    last.then_inc(xs_t_done, 1)
                if down:
                    pe.wait_ge(hid_lo_ready, p - 1)
                    if static >= 4:
                        pe.wait_ge(res_ready, p - 3)
                    for j in range(2):
                        o = ps_down[q][:, j * D:(j + 1) * D]
                        pe.matmul(o, lhsT=two_rows[:, :], rhs=b2_parts[:, bass.ds(e_down[j] * D, D)], start=True, stop=False)
                        for c in range(FC):
                            hi, lo = (x[q][:, (j * FC + c) * P:(j * FC + c + 1) * P] for x in (hid_hi, hid_lo))
                            at = e_down[j] * (FC * D) + c * D
                            pe.matmul(o, lhsT=lo, rhs=w2_hi[:, bass.ds(at, D)], start=False, stop=False)
                            pe.matmul(o, lhsT=hi, rhs=w2_lo[:, bass.ds(at, D)], start=False, stop=False)
                            last = pe.matmul(o, lhsT=hi, rhs=w2_hi[:, bass.ds(at, D)], start=False, stop=(c == FC - 1))
                    last.then_inc(down_done, 1)

            pairs(pe, unit)

        @block.scalar
        def _(act):
            def copy(o, i):
                return act.activation(o, i, ACT.Copy)

            for i in range(2):
                src = w_piece(i)
                act.dma_start(raw[i][:, :].rearrange("p (a b) -> p a b", a=src.shape[1]), src).then_inc(loaded_raw[i], 16)
            act.wait_ge(w_transposed, 2)
            copy(w_hh_hi[:, :], ps_hn[:, 0:3 * D]).then_inc(w_hi_ready, 1)
            fused_bank = [ps_t, ps_prep, ps_post, ps_r, ps_z]
            for l in range(L):
                act.wait_ge(w_fused, l + 1)
                copy(w_fused_hi[:, l, :], fused_bank[l][:, 0:3 * D]).then_inc(w_hi_ready, 1)

            def prepared(g, s, i):
                act.wait_ge(xn_ready, post_index(g, s) + 1)
                copy(ht_hi[s], xn[s][:, :, :]).then_inc(ht_hi_ready, 1)
                act.wait_ge(prep_t_done, post_index(g, s) + 1)
                copy(h[s][:, :], ps_prep[:, :]).then_inc(h_copied, 1)
                copy(h_hi[s], ps_prep[:, :]).then_inc(h_hi_ready, 1)

            def split_agg(st):
                act.wait_ge(agg_done, st + 1)
                copy(agg_hi[:, :], ps_agg[:, :]).then_inc(agg_hi_ready, 1)

            def normalised(out_of, x, norm):
                for c in range(C):
                    last = act.activation(out_of(c), x(c), ACT.Identity, bias=norm[:, c, 0:1], scale=norm[:, c, 1:2])
                return last

            def prep_norm(g, s):
                i = post_index(g, s)
                act.wait_ge(rstd1_ready, i + 1)
                normalised(lambda c: xn[s][:, c, :], lambda c: x1[:, bass.ds(i * C + c, 1), :], norm1[s]).then_inc(xn_ready, 1)

            def post_norm(g, s):
                i = post_index(g, s)
                act.wait_ge(rstd2_ready, i + 1)
                if isinstance(g, int) and g == 0:
                    act.wait_ge(experts_split, LOADS)
                else:
                    act.wait_ge(row_sent[s], g * C * K * 16)
                normalised(lambda c: payload[s][:, c, :, 0:D],
                           lambda c: x1[:, bass.ds(i * C + c, 1), :].to_broadcast([P, K, D]), norm2[s]).then_inc(payload_ready, 1)

            def post_copy(g, s):
                i = post_index(g, s)
                act.wait_ge(post_t_done, i + 1)
                copy(xfT[:, :], ps_post[:, :]).then_inc(xfT_ready, 1)

            def gate_weights(g, s):
                i = post_index(g, s)
                act.wait_ge(both_ready, i + 1)
                act.activation(payload[s][:, :, :, D], margin[:, :, :], ACT.Sigmoid).then_inc(gate_weight_ready, 1)

            def step(g, k, first, last):
                st = g * ST + k
                s = k % S
                act.wait_ge(r_done, st + 1)
                act.wait_ge(rh_done, st)
                act.activation(r_sb[:, :], ps_r[:, :], ACT.Sigmoid, bias=bias_rz[:, 0:1]).then_inc(r_ready, 1)
                act.wait_ge(z_done, st + 1)
                act.wait_ge(zd_ready, st * 2)
                act.activation(z_sb[:, :], ps_z[:, :], ACT.Sigmoid, bias=bias_rz[:, 1:2]).then_inc(z_ready, 1)
                act.wait_ge(pre_n_ready, st + 1)
                for i in range(2):
                    half = slice(i * N // 2, (i + 1) * N // 2)
                    act.activation(n_sb[:, half], t_sb[:, half], ACT.Tanh, bias=cols[:, 2:3]).then_inc(n_ready, 1)
                if not (last and k == ST - 1):
                    split_agg(st + 1)
                if not last and k in PREP_NORM:
                    prep_norm(g + 1, PREP_NORM[k])
                if not first and k in POST_NORM:
                    post_norm(g - 1, POST_NORM[k])
                if k < ST - S:
                    act.wait_ge(h_ready, st * 2 + 2)
                    copy(h_hi[s], h[s][:, :]).then_inc(h_hi_ready, 1)
                    act.wait_ge(t_done, st + 1)
                    copy(ht_hi[s], ps_t[:, :].rearrange("p (c d) -> p c d", c=C)).then_inc(ht_hi_ready, 1)
                elif not last:
                    act.wait_ge(t_done, st + 1)
                    prepared(g + 1, s, st + 2)
                if not first and k in POST_T:
                    post_copy(g - 1, POST_T[k])
                if not first and k in POST_COUNT:
                    gate_weights(g - 1, POST_COUNT[k])

            act.wait_ge(bias_ready, 1)
            act.wait_ge(loaded_x0, 16)
            for s in range(S):
                prep_norm(0, s)
            for s in range(S):
                prepared(0, s, s)
            split_agg(0)
            groups(act, step)
            for s in range(S):
                post_norm(G - 1, s)
                post_copy(G - 1, s)
                gate_weights(G - 1, s)

            def unit(p, static):
                q = static % 2
                if 0 <= static < PAIRS:
                    act.wait_ge(up_done, p + 1)
                    if static >= 2:
                        act.wait_ge(hid_t_done, p - 1)
                    act.activation(hid[q], ps_up[q][:, :].rearrange("p (j f) -> p j f", j=2), ACT.Relu).then_inc(hid_ready, 1)
                if 0 <= static - 1 < PAIRS:
                    r = 1 - q
                    act.wait_ge(hid_t_done, p)
                    if static >= 3:
                        act.wait_ge(down_done, p - 2)
                    copy(hid_hi[r], ps_hid[r][:, :]).then_inc(hid_hi_ready, 1)
                if 0 <= static + 2 < PAIRS:
                    act.wait_ge(xs_t_done, p + 3)
                    copy(xs_hi[q], ps_xs[q][:, 0:2 * P]).then_inc(xs_hi_ready, 1)

            pairs(act, unit)

            def norms(b, static):
                if 0 <= static + 1 < B:
                    q = (static + 1) % RING
                    if static + 1 >= RING:
                        act.wait_ge(yn_ready, b + 2 - RING)
                    for c in range(C):
                        i = (b + 1) * C + c
                        last = act.activation(y[q][:, c * D:(c + 1) * D], x1[:, bass.ds(i, 1), :], ACT.Identity,
                                              bias=norm2_all[:, bass.ds(i, 1), 0], scale=norm2_all[:, bass.ds(i, 1), 1])
                    last.then_inc(xf_ready, 1)
                if 0 <= static - 1 < B:
                    q = (static - 1) % RING
                    act.wait_ge(rstd3_ready, b)
                    if static - 1 >= RING:
                        act.wait_ge(final_stored[q], (b - 1 - q) * (16 // RING))
                    normalised(lambda c: final[q][:, c, :], lambda c: y[q][:, c * D:(c + 1) * D], norm3[q]).then_inc(yn_ready, 1)

            batches(act, norms)

        @block.vector
        def _(dve):
            v = dve
            v.wait_ge(w_transposed, 1)
            v.tensor_copy(cols[:, :], ps_agg[:, 0:2 * 3 + B * C]).then_inc(bias_ready, 1)
            v.wait_ge(w_transposed, 2)
            v.tensor_copy(w_ihT, ps_in[:, 0:3 * D]).then_inc(w_copied, 1)
            v.tensor_copy(weightT[:, 0:4, :].rearrange("p l e -> p (l e)"), ps_r[:, :]).then_inc(w_copied, 1)
            v.tensor_copy(weightT[:, 4, :], ps_z[:, 0:D]).then_inc(w_copied, 1)
            v.wait_ge(bias_ready, 1)
            v.tensor_tensor(bias_rz[:, :], cols[:, 0:2], cols[:, 3:5], ALU.add).then_inc(w_copied, 1)
            v.wait_ge(w_hi_ready, 1)
            v.tensor_tensor(w_hh_lo[:, :], ps_hn[:, 0:3 * D], w_hh_hi[:, :].bitcast(FP32), ALU.subtract).then_inc(w_lo_ready, 1)
            fused_bank = [ps_t, ps_prep, ps_post, ps_r, ps_z]
            for l in range(L):
                v.wait_ge(w_hi_ready, l + 2)
                v.tensor_tensor(w_fused_lo[:, l, :], fused_bank[l][:, 0:3 * D], w_fused_hi[:, l, :].bitcast(FP32), ALU.subtract).then_inc(w_lo_ready, 1)

            def make_edges(g, s):
                v.wait_ge(loaded_adj[s], (g + 1) * 16)
                v.tensor_scalar(edges[s][:, :, :], adj_raw[s][:, :, :], 0.0, None, ALU.not_equal).then_inc(edges_ready[s], 1)

            def aggregate_stats(stat, norm, stat_ready, aggr_ready, ready, i):
                v.wait_ge(stat_ready, (i + 1) * C)
                v.memset(held[:, :], 0.0)
                for c in range(C):
                    last = v.bn_aggr(norm[:, c, :], stat[:, c, :])
                last.then_inc(aggr_ready, 1)
                v.wait_ge(aggr_ready, i + 1)
                v.tensor_scalar(norm[:, :, 0], norm[:, :, 0], -1.0, None, ALU.mult)
                v.tensor_scalar(norm[:, :, 1], norm[:, :, 1], EPS, None, ALU.add).then_inc(ready, 1)

            def prep_stats(g, s):
                i = post_index(g, s)
                for c in range(C):
                    v.bn_stats(stat1[:, c, :], x1[:, bass.ds(i * C + c, 1), :]).then_inc(stat1_ready, 1)
                aggregate_stats(stat1, norm1[s], stat1_ready, aggr1_ready, norm1_ready, i)

            def prepared(g, s, i):
                v.wait_ge(ht_hi_ready, i + 1)
                v.tensor_tensor(ht_lo[s], xn[s][:, :, :], ht_hi[s].bitcast(FP32), ALU.subtract).then_inc(ht_lo_ready, 1)

            def split_agg(st):
                v.wait_ge(agg_hi_ready, st + 1)
                v.tensor_tensor(agg_lo[:, :], ps_agg[:, :], agg_hi[:, :].bitcast(FP32), ALU.subtract).then_inc(agg_lo_ready, 1)

            def post_x1(g, s):
                i = post_index(g, s)
                v.wait_ge(t_done, g * ST + ST - S + s + 1)
                for c in range(C):
                    b = i * C + c
                    last = v.scalar_tensor_tensor(x1[:, bass.ds(b, 1), :], ps_t[:, c * P:(c + 1) * P], cols[:, bass.ds(6 + b, 1)],
                                                  x1[:, bass.ds(b, 1), :], ALU.mult, ALU.add)
                last.then_inc(x1_ready, 1)

            def post_stats(g, s):
                i = post_index(g, s)
                v.wait_ge(x1_ready, i + 1)
                for c in range(C):
                    v.bn_stats(stat2[:, c, :], x1[:, bass.ds(i * C + c, 1), :]).then_inc(stat2_ready, 1)
                aggregate_stats(stat2, norm2[s], stat2_ready, aggr2_ready, norm2_ready, i)

            def post_dest(g, s):
                i = post_index(g, s)
                v.wait_ge(payload_ready, i + 1)
                v.tensor_copy(payload[s][:, :, :, D + 1].bitcast(I32), dest[:, bass.ds(i * C, C), :])
                v.tensor_copy(norm2_all[:, bass.ds(i * C, C), :], norm2[s][:, :, :])

            def post_gate(g, s, part):
                i = post_index(g, s)
                done = [0 if part == 0 else TOP_STEPS]

                def chain(ins, then_max=False):
                    done[0] += 1
                    ins.then_inc(route, 1)
                    v.wait_ge(route, i * ROUTE_STEPS + done[0])
                    if then_max:
                        v.memset(held[:, :], 0.0)

                if part == 0:
                    v.wait_ge(logits_done, i + 1)
                    chain(v.tensor_tensor(logits[:, :, :], ps_post[:, 0:C * E].rearrange("p (c e) -> p c e", c=C),
                                          gate_b_sb[:, None, :].to_broadcast([P, C, E]), ALU.add), True)
                    for c in range(C):
                        last = v.max(top[:, c, :], logits[:, c, :])
                    chain(last)
                    v.tensor_tensor(margin[:, :, 0], top[:, :, 0], top[:, :, 1], ALU.subtract)
                    v.tensor_tensor(margin[:, :, 1], top[:, :, 1], top[:, :, 0], ALU.subtract)
                    for c in range(C):
                        last = v.max_index(top_at[:, c, :], top[:, c, :], logits[:, c, :])
                    chain(last)
                    chain(v.tensor_copy(chosen[:, :, :], top_at[:, :, 0:K]))
                    chain(v.tensor_tensor(onehot[:, :, :, :], iota_e[:, None, None, :].to_broadcast([P, C, K, E]),
                                          chosen[:, :, :, None].to_broadcast([P, C, K, E]), ALU.is_equal))
                    v.tensor_tensor(both[:, :].rearrange("p (c e) -> p c e", c=C), onehot[:, :, 0, :], onehot[:, :, 1, :], ALU.add).then_inc(both_ready, 1)
                else:
                    v.wait_ge(prefix_done, i + 1)
                    chain(v.tensor_tensor(place[:, :, :], ps_post[:, 0:C * E].rearrange("p (c e) -> p c e", c=C),
                                          base_e[:, None, :].to_broadcast([P, C, E]), ALU.add))
                    chain(v.tensor_tensor(base_e[:, :], ps_post[:, C * E:(C + 1) * E], base_e[:, :], ALU.add))
                    for k in range(K):
                        last = v.tensor_tensor(picked[:, :, k, :], onehot[:, :, k, :], place[:, :, :], ALU.mult)
                    chain(last)
                    chain(v.tensor_reduce(slots_f[:, :, :], picked[:, :, :, :], AX.X, ALU.add))
                    v.tensor_copy(slots[s][:, :].rearrange("p (c k) -> p c k", c=C), slots_f[:, :, :]).then_inc(slots_ready, 1)
                assert done[0] == (ROUTE_STEPS if part else TOP_STEPS)

            def extras(g, k, first, last):
                if not first and k in POST_STAT:
                    post_stats(g - 1, POST_STAT[k])
                if not last and k in PREP_STAT:
                    prep_stats(g + 1, PREP_STAT[k])
                if not first and k in POST_TOP:
                    post_dest(g - 1, POST_TOP[k])
                    post_gate(g - 1, POST_TOP[k], 0)
                if not first and k in POST_PLACE:
                    post_gate(g - 1, POST_PLACE[k], 1)
                if not last and k >= ST - S:
                    v.wait_ge(agg_done, g * ST + k + 1)
                    make_edges(g + 1, k % S)

            def step(g, k, first, last):
                st = g * ST + k
                s = k % S
                halves_of = [slice(i * N // 2, (i + 1) * N // 2) for i in range(2)]
                v.wait_ge(r_ready, st + 1)
                v.scalar_tensor_tensor(t_sb[:, :], ps_hn[:, :], cols[:, 5:6], r_sb[:, :], ALU.add, ALU.mult).then_inc(rh_done, 1)
                v.wait_ge(in_done, st + 1)
                v.wait_ge(rh_done, st + 1)
                v.tensor_tensor(t_sb[:, :], ps_in[:, :], t_sb[:, :], ALU.add).then_inc(pre_n_ready, 1)
                extras(g, k, first, last)
                for i, half in enumerate(halves_of):
                    v.wait_ge(n_ready, st * 2 + i + 1)
                    v.tensor_tensor(d_sb[:, half], h[s][:, half], n_sb[:, half], ALU.subtract).then_inc(d_ready, 1)
                for i, half in enumerate(halves_of):
                    v.wait_ge(d_ready, st * 2 + i + 1)
                    v.tensor_tensor(d_sb[:, half], d_sb[:, half], z_sb[:, half], ALU.mult).then_inc(zd_ready, 1)
                for i, half in enumerate(halves_of):
                    v.wait_ge(zd_ready, st * 2 + i + 1)
                    v.tensor_tensor(h[s][:, half], n_sb[:, half], d_sb[:, half], ALU.add).then_inc(h_ready, 1)
                if not (last and k == ST - 1):
                    split_agg(st + 1)
                if k < ST - S:
                    v.wait_ge(ht_hi_ready, st + 3)
                    v.tensor_tensor(ht_lo[s], ps_t[:, :].rearrange("p (c d) -> p c d", c=C), ht_hi[s].bitcast(FP32), ALU.subtract).then_inc(ht_lo_ready, 1)
                else:
                    post_x1(g, s)
                    if not last:
                        prepared(g + 1, s, st + 2)

            v.wait_ge(loaded_x0, 16)
            for s in range(S):
                make_edges(0, s)
                prep_stats(0, s)
            for s in range(S):
                prepared(0, s, s)
            split_agg(0)
            v.wait_ge(loaded_x, 16)
            v.wait_ge(loaded_consts, 64)
            v.wait_ge(consts_set, CONSTS)
            groups(v, step)
            for s in range(S):
                post_stats(G - 1, s)
                post_dest(G - 1, s)
                post_gate(G - 1, s, 0)
                post_gate(G - 1, s, 1)

            steps = [0]

            def chain(ins):
                steps[0] += 1
                ins.then_inc(mapping, 1)
                v.wait_ge(mapping, steps[0])

            v.wait_ge(slots_ready, B)
            v.tensor_copy(pad_rows[:, :], base_e[0:1, :]).then_inc(map_ready, 1)
            chain(v.tensor_tensor(count_f[:, :], base_e[:, :], region_e[:, :], ALU.subtract))
            chain(v.tensor_scalar(count_i[:, :], count_f[:, :], float(P - 1), None, ALU.add))
            chain(v.tensor_scalar(count_i[:, :], count_i[:, :], 7, None, ALU.arith_shift_right))
            chain(v.tensor_copy(tiles_e[:, :], count_i[:, :]))
            chain(v.tensor_tensor_scan(tile_end[:, :], tiles_e[:, :], no_more[:, :], 0.0, ALU.add, ALU.add))
            chain(v.tensor_tensor(ended[:, :, :], tile_end[:, None, :].to_broadcast([P, 2, E]), tile_at[:, :, None].to_broadcast([P, 2, E]), ALU.is_le))
            v.tensor_reduce(tile_expert[:, :], ended[:, :, :], AX.X, ALU.add)
            chain(v.tensor_tensor(ended_tiles[:, :, :], ended[:, :, :], tiles_e[:, None, :].to_broadcast([P, 2, E]), ALU.mult))
            chain(v.tensor_reduce(tile_first[:, :], ended_tiles[:, :, :], AX.X, ALU.add))
            chain(v.tensor_tensor(tile_first[:, :], tile_at[:, :], tile_first[:, :], ALU.subtract))
            chain(v.tensor_scalar(tile_first[:, :], tile_first[:, :], float(P), None, ALU.mult))
            chain(v.scalar_tensor_tensor(tile_row[:, :], tile_expert[:, :], float(REGION), tile_first[:, :], ALU.mult, ALU.add))
            v.tensor_scalar(clipped[:, 1, :], tile_row[:, :], float(E * REGION), None, ALU.min)
            v.tensor_scalar(clipped[:, 0, :], tile_expert[:, :], float(E - 1), None, ALU.min).then_inc(mapped, 1)
            v.wait_ge(map_done, 1)
            v.tensor_copy(tile_map, ps_post[0:1, :]).then_inc(map_ready, 1)

            def unit(p, static):
                q = static % 2
                if 0 <= static - 1 < PAIRS:
                    r = 1 - q
                    v.wait_ge(hid_hi_ready, p)
                    v.tensor_tensor(hid_lo[r], ps_hid[r][:, :], hid_hi[r].bitcast(FP32), ALU.subtract).then_inc(hid_lo_ready, 1)
                if 0 <= static + 2 < PAIRS:
                    v.wait_ge(xs_hi_ready, p + 3)
                    v.tensor_tensor(xs_lo[q], ps_xs[q][:, 0:2 * P], xs_hi[q].bitcast(FP32), ALU.subtract).then_inc(xs_lo_ready, 1)
                if 0 <= static - 2 < PAIRS:
                    u = (static - 2) % SLOTS
                    v.wait_ge(down_done, p - 1)
                    for j in range(2):
                        last = v.tensor_scalar(res[u][:, j, :], ps_down[q][:, j * D:(j + 1) * D], slot[u][:, j, D:D + 1], None, ALU.mult)
                    last.then_inc(res_ready, 1)

            pairs(v, unit)

            def finish(b, static):
                now, before = 0 <= static < B, 0 <= static - 2 < B
                q, r = static % RING, (static - 2) % RING
                if now:
                    v.wait_ge(xf_ready, b + 1)
                    v.wait_ge(y_sum_ready, b + 1)
                    v.tensor_tensor(y[q], y[q], y_sum[q], ALU.add).then_inc(y_ready, 1)
                if before:
                    v.wait_ge(yn_ready, b - 1)
                    v.tensor_tensor(final[r], final[r], gamma_sb[:, None, :].to_broadcast([P, C, D]), ALU.mult).then_inc(scaled_ready, 1)
                if now:
                    v.wait_ge(y_ready, b + 1)
                    v.memset(held[:, :], 0.0)
                    for c in range(C):
                        last = v.bn_stats(stat2[:, c, :], y[q][:, c * D:(c + 1) * D])
                    last.then_inc(y_stats, 1)
                    v.wait_ge(y_stats, b + 1)
                    v.memset(held[:, :], 0.0)
                    for c in range(C):
                        last = v.bn_aggr(norm3[q][:, c, :], stat2[:, c, :])
                    last.then_inc(y_aggr, 1)
                if before:
                    v.wait_ge(scaled_ready, b - 1)
                    v.wait_ge(x_beta_ready, b - 1)
                    v.tensor_tensor(final[r], final[r], x_beta[r], ALU.add).then_inc(final_ready, 1)
                if now:
                    v.wait_ge(y_aggr, b + 1)
                    v.tensor_scalar(norm3[q][:, :, 0], norm3[q][:, :, 0], -1.0, None, ALU.mult)
                    v.tensor_scalar(norm3[q][:, :, 1], norm3[q][:, :, 1], EPS, None, ALU.add).then_inc(norm3_ready, 1)

            batches(v, finish)


_INS = ['x', 'adj', 'nodemask', 'L0_gnn_weight', 'L0_gnn_w_ih', 'L0_gnn_w_hh', 'L0_gnn_b_ih', 'L0_gnn_b_hh',
        'L0_ffn_gate_w', 'L0_ffn_gate_b', 'L0_ffn_w1', 'L0_ffn_b1', 'L0_ffn_w2', 'L0_ffn_b2', 'L0_ffn_gamma', 'L0_ffn_beta']


def kernel(**inputs):
    import numpy as np
    import concourse.bacc as bacc
    from concourse import mybir as mb
    from concourse.bass_utils import run_bass_kernel_spmd

    nc = bacc.Bacc("TRN2", target_bir_lowering=False, num_devices=1)
    arrays, args = {}, []
    for name in _INS:
        a = np.ascontiguousarray(inputs[name])
        arrays[f"in_{name}"] = a
        args.append(nc.dram_tensor(f"in_{name}", a.shape, mb.dt.from_np(a.dtype), kind="ExternalInput").ap())
    out = nc.dram_tensor("out_x", inputs["x"].shape, mb.dt.from_np(np.dtype("float32")), kind="ExternalOutput").ap()
    build(nc, *args, out)
    r = run_bass_kernel_spmd(nc, [arrays], core_ids=[0])
    return r.results[0]["out_x"]
```

```python
import concourse.bass as bass
from concourse import mybir
from contextlib import ExitStack

FP32 = mybir.dt.float32
FP32R = mybir.dt.float32r
BF16 = mybir.dt.bfloat16
I32 = mybir.dt.int32
U32 = mybir.dt.uint32
ALU = mybir.AluOpType
ACT = mybir.ActivationFunctionType
AX = mybir.AxisListType

EPS = 1e-5
P = 128


def build(nc, x, adj, nodemask, weight, w_ih, w_hh, b_ih, b_hh, gate_w, gate_b, w1, b1, w2, b2, gamma, beta, out):
    B, N, D = x.shape
    L = weight.shape[0]
    E, _, F = w1.shape
    K = 2
    C = N // P
    FC = F // P
    T = B * N
    S = 2
    G = B // S
    ST = S * L
    ROW = D + 2
    REGION = T + P
    TILES = (K * T + E * (P - 1)) // P
    SLOTS = 12
    TILES += -TILES % (2 * SLOTS)
    PAIRS = TILES // 2
    EARLY = (K * (B - S) * N - E * (P - 1)) // P // (2 * SLOTS) * (2 * SLOTS)
    SKIP = 1 << 20
    RING = 4
    LOADS = 8

    dispatched = nc.dram_tensor("dispatched", [E * REGION + P, ROW], FP32, kind="Internal").ap()
    result = nc.dram_tensor("result", [K * T, D], FP32, kind="Internal").ap()

    ctx = ExitStack()
    with ctx:
        def sb(name, shape, dt=FP32):
            return ctx.enter_context(nc.sbuf_tensor(name, shape, dt))

        def sem(name):
            return ctx.enter_context(nc.semaphore(name))

        ident = sb("ident", [P, P])
        lower = sb("lower", [P, P], BF16)
        ones = sb("ones", [P, P], BF16)
        iota_e = sb("iota_e", [P, E])
        exponent = sb("exponent", [P, C])
        dest = sb("dest", [P, B * C, K], I32)
        pad = sb("pad", [P, ROW])
        rows = sb("rows", [2 * 3 + B * C, P])
        cols = sb("cols", [P, 2 * 3 + B * C])
        bias_rz = sb("bias_rz", [P, 2])
        w_fused_hi = sb("w_fused_hi", [P, L, 3 * D], FP32R)
        w_fused_lo = sb("w_fused_lo", [P, L, 3 * D], FP32R)
        w_hh_hi = sb("w_hh_hi", [P, 3 * D], FP32R)
        w_hh_lo = sb("w_hh_lo", [P, 3 * D], FP32R)
        gate_w_sb = sb("gate_w_sb", [P, E])
        gate_b_sb = sb("gate_b_sb", [P, E])
        gamma_sb = sb("gamma_sb", [P, D])
        beta_sb = sb("beta_sb", [P, D])
        w1_hi = sb("w1_hi", [P, E * F], FP32R)
        w1_lo = sb("w1_lo", [P, E * F], FP32R)
        w2_parts = sb("w2_parts", [P, E * FC, 2, D], FP32R)
        x1 = sb("x1", [P, B * C, D])
        norm2_all = sb("norm2_all", [P, B * C, 2])
        base_e = sb("base_e", [P, E])
        adj_raw = [sb(f"adj_raw{s}", [P, C, N]) for s in range(S)]
        edges_all = sb("edges_all", [P, S * C * N], FP32R)
        edges = [edges_all[:, s * C * N:(s + 1) * C * N].rearrange("p (c n) -> p c n", c=C) for s in range(S)]
        h = [sb(f"h{s}", [P, N]) for s in range(S)]
        halves = sb("halves", [P, S, 4, N], FP32R)
        h_hi, h_lo = ([halves[:, s, i, :] for s in range(S)] for i in (0, 1))
        ht_hi, ht_lo = ([halves[:, s, i, :].rearrange("p (c d) -> p c d", c=C) for s in range(S)] for i in (2, 3))
        agg_hi = sb("agg_hi", [P, N], FP32R)
        agg_lo = sb("agg_lo", [P, N], FP32R)
        r_sb = sb("r_sb", [P, N])
        z_sb = sb("z_sb", [P, N])
        n_sb = sb("n_sb", [P, N])
        t_sb = sb("t_sb", [P, N])
        d_sb = sb("d_sb", [P, N])
        xn = [sb(f"xn{s}", [P, C, D]) for s in range(S)]
        held = sb("held", [P, 1])
        held_pool = sb("held_pool", [P, 1])
        stat1 = sb("stat1", [P, C, 6])
        norm1 = [sb(f"norm1{s}", [P, C, 2]) for s in range(S)]
        norm2 = [sb(f"norm2{s}", [P, C, 2]) for s in range(S)]
        stat2 = sb("stat2", [P, C, 6])
        payload = [sb(f"payload{s}", [P, C, K, ROW]) for s in range(S)]
        xfT = sb("xfT", [P, N])
        logits = sb("logits", [P, C, E])
        top = sb("top", [P, C, 8])
        top_at = sb("top_at", [P, C, 8], U32)
        chosen = sb("chosen", [P, C, K])
        onehot = sb("onehot", [P, C, K, E])
        both = sb("both", [P, C * E], BF16)
        margin = [sb(f"margin{s}", [P, C, K]) for s in range(S)]
        place = sb("place", [P, C, E])
        picked = sb("picked", [P, C, K, E])
        slots_f = sb("slots_f", [P, C, K])
        slots = [sb(f"slots{s}", [P, C * K], U32) for s in range(S)]
        region_e = sb("region_e", [P, E])
        tile_at = sb("tile_at", [P, 2])
        tile_late = sb("tile_late", [P, 2])
        taken = sb("taken", [P, E + 1])
        open_e = sb("open_e", [P, E])
        passed_e = sb("passed_e", [P, E])
        count_i = sb("count_i", [P, E], I32)
        count_f = sb("count_f", [P, E])
        tiles_e = sb("tiles_e", [P, E])
        tile_end = sb("tile_end", [P, E])
        no_more = sb("no_more", [P, E])
        ended = sb("ended", [P, 2, E])
        ended_tiles = sb("ended_tiles", [P, 2, E])
        tile_expert = sb("tile_expert", [P, 2])
        tile_first = sb("tile_first", [P, 2])
        tile_row = sb("tile_row", [P, 2])
        clipped = sb("clipped", [P, 2, 2])
        tile_map = xn[0][0:1, :, :].rearrange("o c d -> o (c d)").bitcast(I32)
        MAP_ROWS = 2 * P
        assert EARLY <= P < TILES <= 2 * P
        pad_rows = sb("pad_rows", [1, E], I32)
        bias_raw = sb("bias_raw", [E, F + D])
        bias_hi = sb("bias_hi", [E, F + D], FP32R)
        bias_lo = bias_raw
        two_rows = sb("two_rows", [P, P], FP32R)
        b1_parts = edges_all
        b2_parts = halves[:, 0, :, :].rearrange("p i n -> p (i n)")
        assert E * F == S * C * N and E * D == 4 * N
        room = [adj_raw[q][:, 1:4, :].rearrange("p c n -> p (c n)") for q in range(2)]
        out_room = [r_sb, z_sb, n_sb, t_sb, xfT, d_sb]
        slot = [room[u % 2][:, u // 2 * 2 * ROW:(u // 2 + 1) * 2 * ROW].rearrange("p (j r) -> p j r", j=2) for u in range(SLOTS - 2)]
        slot += [h[q][:, 0:2 * ROW].rearrange("p (j r) -> p j r", j=2) for q in range(2)]
        res = [out_room[u // 2][:, u % 2 * 2 * D:(u % 2 + 1) * 2 * D].rearrange("p (j d) -> p j d", j=2) for u in range(SLOTS)]
        hid = [adj_raw[q][:, 0, :].rearrange("p (j f) -> p j f", j=2) for q in range(2)]
        xs_hi, xs_lo = ([halves[:, 1, i, q * 2 * P:(q + 1) * 2 * P] for q in range(2)] for i in (0, 1))
        hid_hi = [halves[:, 1, 2, :], agg_hi[:, :]]
        hid_lo = [halves[:, 1, 3, :], agg_lo[:, :]]
        y0, y1 = ([edges_all[:, (k * 4 + q) * N:(k * 4 + q + 1) * N].bitcast(FP32) for q in range(RING)] for k in range(K))
        xf = [payload[q][:, :, :, :].rearrange("p c k r -> p (c k r)")[:, i * N:(i + 1) * N] for q in range(2) for i in range(2)]
        x_beta = [adj_raw[0][:, q, :].rearrange("p (c d) -> p c d", c=C) for q in range(RING)]
        final = [adj_raw[1][:, q, :].rearrange("p (c d) -> p c d", c=C) for q in range(RING)]
        norm3 = [sb(f"norm3{q}", [P, C, 2]) for q in range(RING)]
        weight_raw = [r_sb[:, l * D:(l + 1) * D] for l in range(4)] + [z_sb[:, 0:D]]
        weightT = [n_sb[:, l * D:(l + 1) * D] for l in range(4)] + [z_sb[:, D:2 * D]]
        w_ih_raw = t_sb[:, 0:3 * D].rearrange("p (g e) -> p g e", g=3)
        w_hh_raw = xfT[:, 0:3 * D].rearrange("p (g e) -> p g e", g=3)
        w_ihT = d_sb[:, 0:3 * D]
        raw = [payload[0][:, :, :, :].rearrange("p c k r -> p (c k r)")[:, 0:1024],
               payload[1][:, :, :, :].rearrange("p c k r -> p (c k r)")[:, 0:1024]]

        bank = [ctx.enter_context(nc.psum_tensor(f"bank{i}", [P, 512], FP32)) for i in range(8)]
        ps_agg, ps_r, ps_z, ps_in, ps_hn, ps_t, ps_prep, ps_post = bank
        w2_flat = w2_parts[:, :, :, :].rearrange("p c i d -> p (c i d)")
        fused_bank = [ps_t, ps_in, ps_post, ps_r, ps_z]
        ps_y = bank[0:RING]
        ps_up, ps_hid, ps_down, ps_xs = bank[0:2], bank[2:4], bank[4:6], bank[6]

        loaded_weights = sem("loaded_weights")
        loaded_rows = sem("loaded_rows")
        loaded_consts = sem("loaded_consts")
        loaded_x0 = sem("loaded_x0")
        loaded_x = sem("loaded_x")
        loaded_adj = [sem(f"loaded_adj{s}") for s in range(S)]
        loaded_raw = [sem(f"loaded_raw{s}") for s in range(2)]
        expert_hi_ready = sem("expert_hi_ready")
        experts_split = sem("experts_split")
        consts_set = sem("consts_set")
        ident_ready = sem("ident_ready")
        w_transposed = sem("w_transposed")
        w_copied = sem("w_copied")
        w_fused = sem("w_fused")
        w_hi_ready = sem("w_hi_ready")
        w_lo_ready = sem("w_lo_ready")
        bias_ready = sem("bias_ready")
        edges_ready = [sem(f"edges_ready{s}") for s in range(S)]
        agg_done, r_done, in_done, z_done, t_done = (sem(f"{n}_done") for n in ("agg", "r", "in", "z", "t"))
        r_ready, z_ready, n_ready = (sem(f"{n}_ready") for n in "rzn")
        rh_done, pre_n_ready, d_ready, zd_ready, h_ready = (sem(n) for n in ("rh_done", "pre_n_ready", "d_ready", "zd_ready", "h_ready"))
        agg_hi_ready, agg_lo_ready = sem("agg_hi_ready"), sem("agg_lo_ready")
        h_hi_ready, h_lo_ready = sem("h_hi_ready"), sem("h_lo_ready")
        ht_hi_ready, ht_lo_ready = sem("ht_hi_ready"), sem("ht_lo_ready")
        stat1_ready, aggr1_ready, norm1_ready, rstd1_ready, xn_ready = (sem(n) for n in ("stat1_ready", "aggr1_ready", "norm1_ready", "rstd1_ready", "xn_ready"))
        prep_t_done, h_copied = sem("prep_t_done"), sem("h_copied")
        power1_ready, power2_ready, power3_ready = (sem(f"power{i}_ready") for i in (1, 2, 3))
        x1_ready, stat2_ready, aggr2_ready, norm2_ready, rstd2_ready = (sem(n) for n in ("x1_ready", "stat2_ready", "aggr2_ready", "norm2_ready", "rstd2_ready"))
        payload_ready, post_t_done, xfT_ready, logits_done = (sem(n) for n in ("payload_ready", "post_t_done", "xfT_ready", "logits_done"))
        gate_weight_ready, both_ready, prefix_done, route = (sem(n) for n in ("gate_weight_ready", "both_ready", "prefix_done", "route"))
        slots_ready = sem("slots_ready")
        row_sent = [sem(f"row_sent{s}") for s in range(S)]
        loaded_bias = sem("loaded_bias")
        bias_split_hi, bias_split = sem("bias_split_hi"), sem("bias_split")
        bias_zeroed, bias_placed = sem("bias_zeroed"), sem("bias_placed")
        mapping, mapped, map_done, map_ready = sem("mapping"), sem("mapped"), sem("map_done"), sem("map_ready")
        padded = sem("padded")
        pool_held = sem("pool_held")
        slot_loaded = [sem(f"slot_loaded{u}") for u in range(SLOTS)]
        xs_t_done, xs_hi_ready, xs_lo_ready, up_done, hid_ready = (sem(n) for n in ("xs_t_done", "xs_hi_ready", "xs_lo_ready", "up_done", "hid_ready"))
        hid_t_done, hid_hi_ready, hid_lo_ready, down_done, res_part, res_ready = (sem(n) for n in ("hid_t_done", "hid_hi_ready", "hid_lo_ready", "down_done", "res_part", "res_ready"))
        res_sent = [sem(f"res_sent{u}") for u in range(SLOTS)]
        loaded_y = [sem(f"loaded_y{q}") for q in range(RING)]
        xf_ready, y_ready, y_stats, y_aggr, norm3_ready, rstd3_ready = (sem(n) for n in ("xf_ready", "y_ready", "y_stats", "y_aggr", "norm3_ready", "rstd3_ready"))
        x_beta_ready, yn_ready, scaled_ready, final_ready = (sem(n) for n in ("x_beta_ready", "yn_ready", "scaled_ready", "final_ready"))
        final_stored = [sem(f"final_stored{q}") for q in range(RING)]

        def post_index(g, s):
            return g * S + s

        def post_bank(g, s):
            return ps_prep if s and not (isinstance(g, int) and g == G - 1) else ps_post

        block = ctx.enter_context(nc.Block())

        VECTOR_WORK = {
            (0, "a"): ["x1"], (0, "b"): ["post_stats 0"],
            (1, "a"): ["post_moments 0"], (1, "b"): ["post_stats 1"],
            (2, "a"): ["post_moments 1", "prep_stats 0"], (2, "b"): ["prep_moments 0"],
            (3, "a"): ["logits 0"], (3, "b"): ["chosen 0"],
            (4, "a"): ["places 0"], (4, "b"): ["slots 0"],
            (5, "a"): ["logits 1"], (5, "b"): ["chosen 1"],
            (6, "a"): ["places 1"], (6, "b"): ["slots 1"],
            (7, "a"): ["prep_stats 1"], (7, "b"): ["edges 0"],
            (8, "a"): ["edges 1", "prep_moments 1"], (8, "b"): ["edges 2"],
            (9, "a"): ["x1"], (9, "b"): ["edges 3"]}
        POST_RSTD, PREP_RSTD = {1: 0, 2: 1}, {2: 0, 8: 1}
        POST_NORM, PREP_NORM = {1: 0, 2: 1}, {3: 0, 9: 1}
        POST_T, POST_GATE, POST_COUNT = {2: 0, 3: 1}, {3: 0, 4: 1}, {4: 0, 6: 1}
        POST_COPY, POST_WEIGHT = {2: 0, 3: 1}, {4: 0, 6: 1}
        SEND = {4: (0, 0), 5: (0, 1), 6: (1, 0), 7: (1, 1)}
        assert S == 2 and ST == 10
        CONSTS = 16
        ROUTE_STARTS = (0, 2, 5, 8)
        ROUTE_STEPS = 9
        MAP_PARTS = 4
        LAST_T, LAST_GATE, LAST_COUNT, LATE_MAP = {0: 0, 4: 1}, {1: 0, 5: 1}, {3: 0, 7: 1}, 11
        LAST_VECTOR = {1: ["logits 0"], 2: ["chosen 0"], 3: ["places 0", "slots 0"],
                       5: ["logits 1"], 6: ["chosen 1"], 7: ["places 1", "slots 1", "ends"],
                       8: ["map 0"], 9: ["map 1"], 10: ["map 2", "map 3"], 11: ["map"]}
        LAST_NORM, LAST_COPY, LAST_WEIGHT = 1, {0: 0, 4: 1}, {3: 0, 7: 1}
        LAST_SEND = {2: (0, 0), 4: (0, 1), 7: (1, 0), 9: (1, 1)}
        assert LATE_MAP < SLOTS

        def w_piece(i):
            half = i % (LOADS // 2)
            if i < LOADS // 2:
                return w1.rearrange("e h f -> h e f")[:, half * 4:half * 4 + 4, :]
            return w2.rearrange("e (c p) d -> p (e c) d", p=P)[:, half * 8:half * 8 + 8, :]

        def before(g, k, first, last):
            if k == 0 and first:
                return None
            return g * ST + (k - 1), (k - 1) % S, (g if k else g - 1), (k - 1) % ST >= ST - S, not (last and k > 0)

        def expert_parts(i):
            half = i % (LOADS // 2)
            if i < LOADS // 2:
                return w1_hi[:, half * 1024:(half + 1) * 1024], w1_lo[:, half * 1024:(half + 1) * 1024]
            return tuple(w2_parts[:, half * 8:half * 8 + 8, part, :] for part in range(2))

        def raw_piece(i):
            return raw[i % 2] if i < LOADS // 2 else raw[i % 2].rearrange("p (a d) -> p a d", d=D)

        def groups(eng, step):
            for k in range(ST):
                step(0, k, True, False)
            with eng.Fori(1, G - 1) as g:
                for k in range(ST):
                    step(g, k, False, False)
            for k in range(ST):
                step(G - 1, k, False, True)

        def pairs(eng, unit):
            for p in range(-2, SLOTS):
                unit(p, p, 0)
            with eng.Fori(1, PAIRS // SLOTS - 1) as i:
                for u in range(SLOTS):
                    unit(i * SLOTS + u, SLOTS + u, i)
            for p in range(PAIRS - SLOTS, PAIRS + 2):
                unit(p, p, PAIRS // SLOTS - 1)

        def map_values(eng, values, most):
            _, loaded = nc.values_load_multi_w_load_instructions(
                values, engines=[eng.engine], min_val=0, max_val=most, bass_reorder=False,
                skip_runtime_bounds_check_because="sums of counts from 0 on that the shapes bound, or clipped to these bounds on the chip")
            return loaded

        def tile_values(eng, at, n, most):
            return map_values(eng, tile_map[0:1, bass.ds(at, n)], most)

        def batches(eng, unit):
            first, turns = RING + 1, (B - 3 - (RING + 1)) // RING
            for b in range(-3, first):
                unit(b, b)
            with eng.Fori(0, turns) as i:
                for q in range(RING):
                    unit(i * RING + (first + q), first + q)
            for b in range(first + turns * RING, B + 2):
                unit(b, b)

        def place_biases(eng, parts, at, width):
            eng.wait_ge(bias_zeroed, 2)
            for part, row in ((bias_hi[:, :].bitcast(FP32), 0), (bias_lo[:, :], 32)):
                eng.dma_start(parts[row:row + 1, :].bitcast(FP32).rearrange("o (e f) -> o e f", e=E), part[:, at:at + width]).then_inc(bias_placed, 16)

        @block.sync
        def _(sp):
            x_rows = x.rearrange("b (c p) d -> p (b c) d", p=P)
            sp.dma_start(x1[:, 0:S * C, :], x_rows[:, 0:S * C, :]).then_inc(loaded_x0, 16)
            sp.dma_start(r_sb[:, :].rearrange("p (l e) -> p l e", l=4), weight[0:4, :, :].rearrange("l d e -> d l e")).then_inc(loaded_weights, 16)
            sp.dma_start(weight_raw[4], weight[4, :, :]).then_inc(loaded_weights, 16)
            sp.dma_start(w_ih_raw, w_ih.rearrange("(g f) e -> f g e", f=D)).then_inc(loaded_weights, 16)
            sp.dma_start(w_hh_raw, w_hh.rearrange("(g f) e -> f g e", f=D)).then_inc(loaded_weights, 16)
            for s in range(S):
                sp.dma_start(adj_raw[s][:, :, :], adj[s].rearrange("(c p) j -> p c j", p=P)).then_inc(loaded_adj[s], 16)
            for i in range(2):
                src = w_piece(i)
                sp.dma_start(raw[i][:, :].rearrange("p (a b) -> p a b", a=src.shape[1]), src).then_inc(loaded_raw[i], 16)
            sp.dma_start(x1[:, S * C:, :], x_rows[:, S * C:, :]).then_inc(loaded_x, 16)
            sp.dma_start(gate_w_sb[:, :], gate_w).then_inc(loaded_consts, 16)
            sp.dma_start(bias_raw[:, 0:F], b1).then_inc(loaded_bias, 16)
            sp.dma_start(bias_raw[:, F:F + D], b2).then_inc(loaded_bias, 16)
            sp.wait_ge(consts_set, CONSTS)
            sp.dma_start(dispatched[E * REGION:E * REGION + P, :], pad[:, :]).then_inc(padded, 16)
            for dst, src in ((gate_b_sb, gate_b), (gamma_sb, gamma), (beta_sb, beta)):
                sp.dma_start(dst[:, :], src.rearrange("(a n) -> a n", a=1).to_broadcast([P, src.shape[0]])).then_inc(loaded_consts, 16)
            for i in range(2, LOADS):
                src = w_piece(i)
                sp.wait_ge(experts_split, i - 1)
                sp.dma_start(raw[i % 2][:, :].rearrange("p (a b) -> p a b", a=src.shape[1]), src).then_inc(loaded_raw[i % 2], 16)
            with sp.Fori(1, G) as g:
                for s in range(S):
                    sp.wait_ge(edges_ready[s], g)
                    sp.dma_start(adj_raw[s][:, :, :], adj[bass.ds(g * S + s, 1), :, :].rearrange("b (c p) j -> p (b c) j", p=P)).then_inc(loaded_adj[s], 16)
            def pad_regions(first):
                for row in map_values(sp, pad_rows[0:1, first:first + 2], E * REGION - P):
                    sp.dma_start(dispatched[bass.ds(row, P), :], pad[:, :]).then_inc(padded, 16)

            def load_slots(i, reused):
                for u in range(SLOTS):
                    if not reused and u == 2:
                        place_biases(sp, b2_parts, F, D)
                    if not reused and u == SLOTS - 2:
                        sp.wait_ge(t_done, G * ST)
                    if reused:
                        sp.wait_ge(res_sent[u], i * 2 * 16)
                    for j, row in enumerate(tile_values(sp, i * (2 * SLOTS) + (2 * u + MAP_ROWS), 2, E * REGION)):
                        sp.dma_start(slot[u][:, j, :], dispatched[bass.ds(row, P), :]).then_inc(slot_loaded[u], 16)
                    if isinstance(i, int) and i == 1 and u >= SLOTS - E // 2:
                        if u == SLOTS - E // 2:
                            sp.wait_ge(map_ready, 2)
                        pad_regions(2 * (u - (SLOTS - E // 2)))

            sp.wait_ge(map_ready, 1)
            for s in range(S):
                sp.wait_ge(row_sent[s], (G - 1) * C * K * 16)
            load_slots(0, False)
            load_slots(1, True)
            with sp.Fori(2, EARLY // (2 * SLOTS)) as i:
                load_slots(i, True)
            sp.wait_ge(map_ready, 3)
            sp.wait_ge(padded, (E + 1) * 16)
            for s in range(S):
                sp.wait_ge(row_sent[s], G * C * K * 16)
            with sp.Fori(EARLY // (2 * SLOTS), PAIRS // SLOTS) as i:
                load_slots(i, True)
            for u in range(SLOTS):
                sp.wait_ge(res_sent[u], PAIRS // SLOTS * 2 * 16)
            result_rows = result.rearrange("(k m p) d -> k p m d", k=K, p=P)

            out_rows = out.rearrange("b (c p) d -> p (b c) d", p=P)

            def move(b, static):
                if static + 3 < B:
                    q = (static + 3) % RING
                    if static >= 1:
                        sp.wait_ge(y_ready, b)
                    for k, dst in enumerate((y0[q], y1[q])):
                        sp.dma_start(dst.rearrange("p (c d) -> p c d", c=C), result_rows[k][:, bass.ds((b + 3) * C, C), :]).then_inc(loaded_y[q], 16)
                if static >= 2:
                    q = (static - 2) % RING
                    sp.wait_ge(final_ready, b - 1)
                    sp.dma_start(out_rows[:, bass.ds((b - 2) * C, C), :], final[q]).then_inc(final_stored[q], 16)

            batches(sp, move)
            for q in range(RING):
                sp.wait_ge(final_stored[q], B // RING * 16)

        @block.gpsimd
        def _(pool):
            pool.memset(ident[:, :], 0.0).then_inc(consts_set, 1)
            pool.memset(ones[:, :], 1.0).then_inc(consts_set, 1)
            pool.memset(lower[:, :], 1.0).then_inc(consts_set, 1)
            pool.memset(exponent[:, :], -0.5).then_inc(consts_set, 1)
            pool.wait_ge(consts_set, 1)
            pool.affine_select(out=ident[:, :], in_=ident[:, :], compare_op=ALU.not_equal, fill=1.0, base=0,
                               pattern=[[-1, P]], channel_multiplier=1).then_inc(ident_ready, 1)
            pool.wait_ge(consts_set, 3)
            pool.affine_select(out=lower[:, :], in_=lower[:, :], compare_op=ALU.is_gt, fill=0.0, base=0,
                               pattern=[[1, P]], channel_multiplier=-1).then_inc(consts_set, 1)
            pool.iota(iota_e[:, :], [[1, E]], base=0, channel_multiplier=0, allow_small_or_imprecise_dtypes=True).then_inc(consts_set, 1)
            pool.iota(base_e[:, :], [[REGION, E]], base=0, channel_multiplier=0, allow_small_or_imprecise_dtypes=True).then_inc(consts_set, 1)
            pool.iota(dest[:, :, :], [[P, B * C], [T, K]], base=0, channel_multiplier=1).then_inc(consts_set, 1)

            pool.iota(region_e[:, :], [[REGION, E]], base=0, channel_multiplier=0, allow_small_or_imprecise_dtypes=True).then_inc(consts_set, 1)
            pool.iota(tile_at[:, :], [[P, 2]], base=0, channel_multiplier=1, allow_small_or_imprecise_dtypes=True).then_inc(consts_set, 1)
            pool.iota(tile_late[:, :], [[P, 2]], base=-EARLY, channel_multiplier=1, allow_small_or_imprecise_dtypes=True).then_inc(consts_set, 1)
            pool.memset(no_more[:, :], 0.0).then_inc(consts_set, 1)
            pool.memset(pad[:, 0:D + 1], 0.0).then_inc(consts_set, 1)
            pool.memset(pad[:, D + 1:D + 2].bitcast(I32), SKIP).then_inc(consts_set, 1)
            pool.memset(two_rows[:, :].bitcast(FP32), 0.0).then_inc(consts_set, 1)
            pool.wait_ge(consts_set, CONSTS - 1)
            pool.memset(two_rows[0:1, :].bitcast(FP32), 1.0)
            pool.memset(two_rows[32:33, :].bitcast(FP32), 1.0).then_inc(consts_set, 1)
            pool.wait_ge(consts_set, CONSTS)

            def rstd_of(i, summed, norm, powered, ready):
                pool.wait_ge(summed, i + 1)
                pool.tensor_tensor(norm[:, :, 1], norm[:, :, 1], exponent[:, :], ALU.pow).then_inc(powered, 1)
                pool.wait_ge(powered, i + 1)
                pool.tensor_tensor(norm[:, :, 0], norm[:, :, 0], norm[:, :, 1], ALU.mult).then_inc(ready, 1)

            def low_part(s, i):
                pool.wait_ge(h_hi_ready, i + 1)
                pool.tensor_tensor(h_lo[s], h[s][:, :], h_hi[s].bitcast(FP32), ALU.subtract).then_inc(h_lo_ready, 1)

            def rstd1_of(g, s):
                rstd_of(post_index(g, s), norm1_ready, norm1[s], power1_ready, rstd1_ready)

            def rstd2_of(g, s):
                rstd_of(post_index(g, s), norm2_ready, norm2[s], power2_ready, rstd2_ready)

            def send_rows(g, s, half):
                i = post_index(g, s)
                pool.wait_ge(consts_set, 4)
                pool.wait_ge(slots_ready, i + 1)
                pool.wait_ge(gate_weight_ready, i + 1)
                for c in range(half * C // 2, (half + 1) * C // 2):
                    for k in range(K):
                        pool.indirect_dma_start(
                            out=dispatched[:, :],
                            out_offset=bass.IndirectOffsetOnAxis(ap=slots[s][:, c * K + k:c * K + k + 1], axis=0),
                            in_=payload[s][:, c, k, :], in_offset=None).then_inc(row_sent[s], 16)

            def split_lo(i):
                hi, lo = expert_parts(i)
                pool.wait_ge(expert_hi_ready, i + 1)
                pool.tensor_tensor(lo, raw_piece(i), hi.bitcast(FP32), ALU.subtract).then_inc(experts_split, 1)

            def step(g, k, first, last):
                if not first and k in POST_RSTD:
                    rstd2_of(g - 1, POST_RSTD[k])
                if not last and k in PREP_RSTD:
                    rstd1_of(g + 1, PREP_RSTD[k])
                if not last and not first and k == ST - 1:
                    sent(g)
                if not (last and k >= ST - S):
                    low_part(k % S, g * ST + k + S)
                if not first and k in SEND:
                    send_rows(g - 1, *SEND[k])
                if first and k < LOADS:
                    split_lo(k)
                if first and k == LOADS:
                    pool.wait_ge(loaded_bias, 32)
                    pool.tensor_copy(bias_hi[:, :], bias_raw[:, :]).then_inc(bias_split_hi, 1)
                    pool.wait_ge(bias_split_hi, 1)
                    pool.tensor_tensor(bias_raw[:, :], bias_raw[:, :], bias_hi[:, :].bitcast(FP32), ALU.subtract).then_inc(bias_split, 1)

            def sent(g):
                for s in range(S):
                    pool.wait_ge(row_sent[s], g * C * K * 16)

            for s in range(S):
                rstd1_of(0, s)
            for s in range(S):
                low_part(s, s)
            groups(pool, step)
            pool.wait_ge(z_done, G * ST)
            pool.wait_ge(bias_split, 1)
            pool.memset(b1_parts[:, :].bitcast(FP32), 0.0).then_inc(bias_zeroed, 1)
            pool.memset(b2_parts.bitcast(FP32), 0.0).then_inc(bias_zeroed, 1)
            sent(G - 1)
            for s in range(S):
                rstd2_of(G - 1, s)

            def hold(n, static):
                if static:
                    pool.wait_ge(pool_held, n)
                pool.tensor_tensor(held_pool[:, :], exponent[:, 0:1], exponent[:, 0:1], ALU.add).then_inc(pool_held, 1)

            def send_results(p, static, turn):
                if not 0 <= static < PAIRS:
                    return
                u = static % SLOTS
                pool.wait_ge(res_ready, p + 1)
                hold(p, static)
                for j in range(2):
                    pool.indirect_dma_start(
                        out=result[:, :], out_offset=bass.IndirectOffsetOnAxis(ap=slot[u][:, j, D + 1:D + 2].bitcast(U32), axis=0),
                        in_=res[u][:, j, :], in_offset=None, bounds_check=K * T - 1, oob_is_err=False).then_inc(res_sent[u], 16)
                if static in LAST_SEND:
                    send_rows(G - 1, *LAST_SEND[static])

            pairs(pool, send_results)
            for u in range(SLOTS):
                pool.wait_ge(res_sent[u], PAIRS // SLOTS * 2 * 16)

            def norms(b, static):
                if 0 <= static < B:
                    rstd_of(b, norm3_ready, norm3[static % RING], power3_ready, rstd3_ready)
                if 0 <= static + 1 < B:
                    q = (static + 1) % RING
                    pool.tensor_tensor(x_beta[q], x1[:, bass.ds((b + 1) * C, C), :], beta_sb[:, None, :].to_broadcast([P, C, D]), ALU.add).then_inc(x_beta_ready, 1)

            batches(pool, norms)

        @block.tensor
        def _(pe):
            def mm3(ps, w_hi, w_lo, v_hi, v_lo, start, stop):
                pe.matmul(ps, lhsT=w_hi, rhs=v_lo, start=start, stop=False)
                pe.matmul(ps, lhsT=w_lo, rhs=v_hi, start=False, stop=False)
                return pe.matmul(ps, lhsT=w_hi, rhs=v_hi, start=False, stop=stop)

            R, Z, NN = (slice(i * D, (i + 1) * D) for i in range(3))

            pe.wait_ge(ident_ready, 1)
            pe.wait_ge(loaded_rows, 48)
            nrow = 2 * 3 + B * C
            pe.transpose(ps_agg[:, 0:nrow], rows[:, :], ident[0:nrow, 0:nrow]).then_inc(w_transposed, 1)
            pe.wait_ge(loaded_weights, 64)
            for i in range(3):
                pe.transpose(ps_in[:, i * D:(i + 1) * D], w_ih_raw[:, i, :], ident[:, :])
                last = pe.transpose(ps_hn[:, i * D:(i + 1) * D], w_hh_raw[:, i, :], ident[:, :])
            for l in range(L):
                last = pe.transpose((ps_r if l < 4 else ps_z)[:, (l % 4) * D:(l % 4 + 1) * D], weight_raw[l], ident[:, :])
            last.then_inc(w_transposed, 1)

            def fuse(l):
                pe.matmul(fused_bank[l][:, 0:3 * D], lhsT=weightT[l], rhs=w_ihT, start=True, stop=True).then_inc(w_fused, 1)

            def aggregate(st, g, s):
                pe.wait_ge(ht_hi_ready, st + 1)
                pe.wait_ge(agg_lo_ready, st)
                for c in range(C):
                    pe.matmul(ps_agg[:, :], lhsT=ht_hi[s][:, c, :], rhs=edges[s][:, c, :], start=(c == 0), stop=False)
                pe.wait_ge(ht_lo_ready, st + 1)
                for c in range(C):
                    last = pe.matmul(ps_agg[:, :], lhsT=ht_lo[s][:, c, :], rhs=edges[s][:, c, :], start=False, stop=(c == C - 1))
                last.then_inc(agg_done, 1)

            def hidden_gates(st, s):
                pe.wait_ge(h_lo_ready, st + 1)
                pe.wait_ge(rh_done, st)
                mm3(ps_hn[:, :], w_hh_hi[:, NN], w_hh_lo[:, NN], h_hi[s], h_lo[s], True, True)
                pe.wait_ge(z_ready, st)
                mm3(ps_r[:, :], w_hh_hi[:, R], w_hh_lo[:, R], h_hi[s], h_lo[s], True, False)
                mm3(ps_z[:, :], w_hh_hi[:, Z], w_hh_lo[:, Z], h_hi[s], h_lo[s], True, False)

            def transpose_h(previous, half):
                st, s = previous[:2]
                pe.wait_ge(h_ready, st * 2 + half + 1)
                for c in range(half * C // 2, (half + 1) * C // 2):
                    last = pe.transpose(ps_t[:, c * P:(c + 1) * P], h[s][:, c * P:(c + 1) * P], ident[:, :])
                if half:
                    last.then_inc(t_done, 1)

            def transpose_prepared(g, s):
                pe.wait_ge(xn_ready, post_index(g, s) + 1)
                for c in range(C):
                    last = pe.transpose(ps_prep[:, c * P:(c + 1) * P], xn[s][:, c, :], ident[:, :])
                last.then_inc(prep_t_done, 1)

            def transpose_post(g, s):
                i = post_index(g, s)
                pe.wait_ge(payload_ready, i + 1)
                for c in range(C):
                    last = pe.transpose(post_bank(g, s)[:, c * P:(c + 1) * P], payload[s][:, c, 0, 0:D], ident[:, :])
                last.then_inc(post_t_done, 1)

            def gate(g, s):
                i = post_index(g, s)
                pe.wait_ge(xfT_ready, i + 1)
                for c in range(C):
                    last = pe.matmul(post_bank(g, s)[:, c * E:(c + 1) * E], lhsT=xfT[:, c * P:(c + 1) * P], rhs=gate_w_sb[:, :], start=True, stop=True)
                last.then_inc(logits_done, 1)

            def count(g, s):
                i = post_index(g, s)
                pe.wait_ge(both_ready, i + 1)
                pe.matmul(post_bank(g, s)[:, 0:C * E], lhsT=lower[:, :], rhs=both[:, :], start=True, stop=False, skip_group_check=True)
                for c in range(1, C):
                    pe.matmul(post_bank(g, s)[:, c * E:C * E], lhsT=ones[:, :], rhs=both[:, 0:(C - c) * E], start=False, stop=(c == C - 1), skip_group_check=True)
                for c in range(C):
                    last = pe.matmul(post_bank(g, s)[:, C * E:(C + 1) * E], lhsT=ones[:, :], rhs=both[:, c * E:(c + 1) * E], start=False, stop=(c == C - 1), skip_group_check=True)
                last.then_inc(prefix_done, 1)

            def step(g, k, first, last):
                st = g * ST + k
                l = k // S
                previous = before(g, k, first, last)
                pe.wait_ge(agg_lo_ready, st + 1)
                mm3(ps_r[:, :], w_fused_hi[:, l, R], w_fused_lo[:, l, R], agg_hi[:, :], agg_lo[:, :], False, True).then_inc(r_done, 1)
                pe.wait_ge(pre_n_ready, st)
                pe.matmul(ps_in[:, :], lhsT=w_fused_hi[:, l, NN], rhs=agg_lo[:, :], start=True, stop=False)
                if previous:
                    if k == 1:
                        if not first:
                            pe.wait_ge(x1_ready, g * S)
                    elif k == 0:
                        pe.wait_ge(x1_ready, g * S - 1)
                    else:
                        pe.wait_ge(ht_lo_ready, st + 1)
                    for half in range(2):
                        transpose_h(previous, half)
                    if previous[3] and previous[4]:
                        transpose_prepared(previous[2] + 1, previous[1])
                pe.matmul(ps_in[:, :], lhsT=w_fused_lo[:, l, NN], rhs=agg_hi[:, :], start=False, stop=False)
                pe.matmul(ps_in[:, :], lhsT=w_fused_hi[:, l, NN], rhs=agg_hi[:, :], start=False, stop=True).then_inc(in_done, 1)
                mm3(ps_z[:, :], w_fused_hi[:, l, Z], w_fused_lo[:, l, Z], agg_hi[:, :], agg_lo[:, :], False, True).then_inc(z_done, 1)
                if not first and k in POST_COUNT:
                    count(g - 1, POST_COUNT[k])
                if not first and k in POST_GATE:
                    gate(g - 1, POST_GATE[k])
                if not first and k in POST_T:
                    transpose_post(g - 1, POST_T[k])
                if last and k == ST - 1:
                    pe.wait_ge(mapped, 1)
                    for i in range(2):
                        last_map = pe.matmul(ps_prep[0:1, i * EARLY:(i + 1) * EARLY], lhsT=clipped[:, i, 0:1], rhs=ident[:, 0:EARLY], start=True, stop=True)
                    last_map.then_inc(map_done, 1)
                if not (last and k == ST - 1):
                    if k == ST - 1:
                        pe.wait_ge(edges_ready[0], g + 2)
                    elif k + 1 < S:
                        pe.wait_ge(edges_ready[k + 1], g + 1)
                    aggregate(st + 1, g, (k + 1) % S)
                    hidden_gates(st + 1, (k + 1) % S)

            transpose_prepared(0, 0)
            pe.wait_ge(w_copied, 4)
            for l in range(2):
                fuse(l)
            pe.wait_ge(h_hi_ready, 1)
            transpose_prepared(0, 1)
            for l in range(2, L):
                fuse(l)
            pe.wait_ge(edges_ready[0], 1)
            aggregate(0, 0, 0)
            pe.wait_ge(w_lo_ready, L + 1)
            hidden_gates(0, 0)

            groups(pe, step)
            pe.wait_ge(x1_ready, G * S - 1)
            for half in range(2):
                transpose_h((G * ST - 1, S - 1), half)

            pe.wait_ge(map_ready, 1)
            pe.wait_ge(bias_placed, 4 * 16)
            pe.wait_ge(experts_split, LOADS)

            near = {}

            def load_experts(p, static):
                low, high = max(static - 2, 0), min(static + 2, PAIRS)
                values = tile_values(pe, p * 2 + 2 * (low - static), 2 * (high - low), E - 1)
                near.clear()
                near.update({low + n: values[2 * n:2 * n + 2] for n in range(high - low)})

            def unit(p, static, turn):
                q = static % 2
                up, hidden, down, rows_in = (0 <= static + ahead < PAIRS for ahead in (0, -1, -2, 2))
                if static >= 0 and static % 2 == 0:
                    load_experts(p, static)
                e_up, e_down = near.get(static), near.get(static - 2)
                if static == SLOTS + 1:
                    pe.wait_ge(map_ready, 3)
                if up:
                    pe.wait_ge(xs_lo_ready, p + 1)
                    if static >= 2:
                        pe.wait_ge(hid_ready, p - 1)
                    for j in range(2):
                        o = ps_up[q][:, j * F:(j + 1) * F]
                        hi, lo = (xs[q][:, j * P:(j + 1) * P] for xs in (xs_hi, xs_lo))
                        pe.matmul(o, lhsT=two_rows[:, :], rhs=b1_parts[:, bass.ds(e_up[j] * F, F)], start=True, stop=False)
                        pe.matmul(o, lhsT=lo, rhs=w1_hi[:, bass.ds(e_up[j] * F, F)], start=False, stop=False)
                        pe.matmul(o, lhsT=hi, rhs=w1_lo[:, bass.ds(e_up[j] * F, F)], start=False, stop=False)
                        last = pe.matmul(o, lhsT=hi, rhs=w1_hi[:, bass.ds(e_up[j] * F, F)], start=False, stop=True)
                    last.then_inc(up_done, 1)
                if hidden:
                    r = 1 - q
                    pe.wait_ge(hid_ready, p)
                    if static >= 3:
                        pe.wait_ge(hid_lo_ready, p - 2)
                    for j in range(2):
                        for c in range(FC):
                            last = pe.transpose(ps_hid[r][:, (j * FC + c) * P:(j * FC + c + 1) * P], hid[r][:, j, c * P:(c + 1) * P], ident[:, :])
                    last.then_inc(hid_t_done, 1)
                if rows_in:
                    u = (static + 2) % SLOTS
                    if static >= 0:
                        turn += (static % SLOTS + 2) // SLOTS
                    pe.wait_ge(slot_loaded[u], turn * (2 * 16) + 2 * 16)
                    if static >= -1:
                        pe.wait_ge(xs_lo_ready, p + 2)
                    for j in range(2):
                        last = pe.transpose(ps_xs[:, j * P:(j + 1) * P], slot[u][:, j, 0:D], ident[:, :])
                    last.then_inc(xs_t_done, 1)
                if static in LAST_COUNT:
                    count(G - 1, LAST_COUNT[static])
                if static in LAST_T:
                    if static:
                        pe.wait_ge(slots_ready, B - 1)
                    transpose_post(G - 1, LAST_T[static])
                if static in LAST_GATE:
                    gate(G - 1, LAST_GATE[static])
                if static == LATE_MAP:
                    pe.wait_ge(mapped, 2)
                    for i in range(2):
                        at = i * (TILES - EARLY)
                        pe.matmul(ps_post[0:1, at:at + P - EARLY], lhsT=clipped[:, i, 0:1], rhs=ident[:, EARLY:P], start=True, stop=True)
                        last = pe.matmul(ps_post[0:1, at + P - EARLY:at + TILES - EARLY], lhsT=clipped[:, i, 1:2], rhs=ident[:, 0:TILES - P], start=True, stop=True)
                    last.then_inc(map_done, 1)
                if down:
                    pe.wait_ge(hid_lo_ready, p - 1)
                    if static >= 4:
                        pe.wait_ge(res_ready, p - 3)
                    for j in range(2):
                        o = ps_down[q][:, j * 2 * D:(j + 1) * 2 * D]
                        pe.matmul(o[:, 0:D], lhsT=two_rows[:, :], rhs=b2_parts[:, bass.ds(e_down[j] * D, D)], start=True, stop=False, skip_group_check=True)
                        for c in range(FC):
                            hi, lo = (x[q][:, (j * FC + c) * P:(j * FC + c + 1) * P] for x in (hid_hi, hid_lo))
                            at = e_down[j] * (FC * 2 * D) + c * 2 * D
                            last = pe.matmul(o, lhsT=hi, rhs=w2_flat[:, bass.ds(at, 2 * D)], start=False, stop=(c == FC - 1), skip_group_check=True)
                            last = pe.matmul(o[:, 0:D], lhsT=lo, rhs=w2_flat[:, bass.ds(at, D)], start=False, stop=(c == FC - 1), skip_group_check=True)
                    last.then_inc(down_done, 1)

            pairs(pe, unit)

            def add_up(b, static):
                if 0 <= static < B:
                    q = static % RING
                    pe.wait_ge(xf_ready, b + 1)
                    if static >= RING:
                        pe.wait_ge(yn_ready, b + 1 - RING)
                    pe.matmul(ps_y[q][:, :], lhsT=ident[:, :], rhs=xf[q], start=True, stop=False)
                    pe.wait_ge(loaded_y[q], (b - q) * (32 // RING) + 32)
                    pe.matmul(ps_y[q][:, :], lhsT=ident[:, :], rhs=y0[q], start=False, stop=False)
                    pe.matmul(ps_y[q][:, :], lhsT=ident[:, :], rhs=y1[q], start=False, stop=True).then_inc(y_ready, 1)

            batches(pe, add_up)

        @block.scalar
        def _(act):
            def copy(o, i):
                return act.activation(o, i, ACT.Copy)

            act.dma_start(rows[0:3, :], b_ih.rearrange("(g f) -> g f", f=D)).then_inc(loaded_rows, 16)
            act.dma_start(rows[3:6, :], b_hh.rearrange("(g f) -> g f", f=D)).then_inc(loaded_rows, 16)
            act.dma_start(rows[6:6 + B * C, :], nodemask.rearrange("b (c p) -> (b c) p", p=P)).then_inc(loaded_rows, 16)

            def prepared(g, s, i):
                act.wait_ge(xn_ready, post_index(g, s) + 1)
                copy(ht_hi[s], xn[s][:, :, :]).then_inc(ht_hi_ready, 1)
                act.wait_ge(prep_t_done, post_index(g, s) + 1)
                copy(h[s][:, :], ps_prep[:, :]).then_inc(h_copied, 1)
                copy(h_hi[s], ps_prep[:, :]).then_inc(h_hi_ready, 1)

            def split_agg(st):
                act.wait_ge(agg_done, st + 1)
                copy(agg_hi[:, :], ps_agg[:, :]).then_inc(agg_hi_ready, 1)

            def normalised(out_of, x, norm):
                for c in range(C):
                    last = act.activation(out_of(c), x(c), ACT.Identity, bias=norm[:, c, 0:1], scale=norm[:, c, 1:2])
                return last

            def prep_norm(g, s):
                i = post_index(g, s)
                act.wait_ge(rstd1_ready, i + 1)
                normalised(lambda c: xn[s][:, c, :], lambda c: x1[:, bass.ds(i * C + c, 1), :], norm1[s]).then_inc(xn_ready, 1)

            def post_norm(g, s):
                i = post_index(g, s)
                act.wait_ge(rstd2_ready, i + 1)
                normalised(lambda c: payload[s][:, c, :, 0:D],
                           lambda c: x1[:, bass.ds(i * C + c, 1), :].to_broadcast([P, K, D]), norm2[s]).then_inc(payload_ready, 1)

            def post_copy(g, s):
                i = post_index(g, s)
                act.wait_ge(post_t_done, i + 1)
                copy(xfT[:, :], post_bank(g, s)[:, :]).then_inc(xfT_ready, 1)

            def gate_weights(g, s):
                i = post_index(g, s)
                act.wait_ge(both_ready, i + 1)
                act.activation(payload[s][:, :, :, D], margin[s][:, :, :], ACT.Sigmoid).then_inc(gate_weight_ready, 1)

            def step(g, k, first, last):
                st = g * ST + k
                s = k % S
                act.wait_ge(r_done, st + 1)
                act.wait_ge(rh_done, st)
                act.activation(r_sb[:, :], ps_r[:, :], ACT.Sigmoid, bias=bias_rz[:, 0:1]).then_inc(r_ready, 1)
                previous = before(g, k, first, last)
                if previous:
                    pst, ps, pg, last_layer, followed = previous
                    act.wait_ge(t_done, pst + 1)
                    if not last_layer:
                        copy(ht_hi[ps], ps_t[:, :].rearrange("p (c d) -> p c d", c=C)).then_inc(ht_hi_ready, 1)
                        copy(h_hi[ps], h[ps][:, :]).then_inc(h_hi_ready, 1)
                    elif followed:
                        prepared(pg + 1, ps, pst + 2)
                act.wait_ge(z_done, st + 1)
                act.wait_ge(zd_ready, st * 2)
                act.activation(z_sb[:, :], ps_z[:, :], ACT.Sigmoid, bias=bias_rz[:, 1:2]).then_inc(z_ready, 1)
                act.wait_ge(pre_n_ready, st + 1)
                for i in range(2):
                    half = slice(i * N // 2, (i + 1) * N // 2)
                    act.activation(n_sb[:, half], t_sb[:, half], ACT.Tanh, bias=cols[:, 2:3]).then_inc(n_ready, 1)
                if not (last and k == ST - 1):
                    split_agg(st + 1)
                if not first and k in POST_COPY:
                    post_copy(g - 1, POST_COPY[k])
                if not first and k in POST_WEIGHT:
                    gate_weights(g - 1, POST_WEIGHT[k])
                if not first and k in POST_NORM:
                    post_norm(g - 1, POST_NORM[k])
                if not last and k in PREP_NORM:
                    prep_norm(g + 1, PREP_NORM[k])
                if first and k < LOADS:
                    act.wait_ge(loaded_raw[k % 2], (k // 2 + 1) * 16)
                    copy(expert_parts(k)[0], raw_piece(k)).then_inc(expert_hi_ready, 1)

            act.wait_ge(loaded_x0, 16)
            prep_norm(0, 0)
            act.wait_ge(w_transposed, 2)
            copy(w_hh_hi[:, :], ps_hn[:, 0:3 * D]).then_inc(w_hi_ready, 1)
            prep_norm(0, 1)
            prepared(0, 0, 0)
            for l in range(L):
                act.wait_ge(w_fused, l + 1)
                copy(w_fused_hi[:, l, :], fused_bank[l][:, 0:3 * D]).then_inc(w_hi_ready, 1)
                if l == 1:
                    prepared(0, 1, 1)
            act.wait_ge(bias_ready, 1)
            split_agg(0)
            groups(act, step)
            place_biases(act, b1_parts, 0, F)
            post_norm(G - 1, 0)

            def unit(p, static, turn):
                q = static % 2
                if 0 <= static < PAIRS:
                    act.wait_ge(up_done, p + 1)
                    if static >= 2:
                        act.wait_ge(hid_t_done, p - 1)
                    act.activation(hid[q], ps_up[q][:, :].rearrange("p (j f) -> p j f", j=2), ACT.Relu).then_inc(hid_ready, 1)
                if 0 <= static - 1 < PAIRS:
                    r = 1 - q
                    act.wait_ge(hid_t_done, p)
                    if static >= 3:
                        act.wait_ge(down_done, p - 2)
                    copy(hid_hi[r], ps_hid[r][:, :]).then_inc(hid_hi_ready, 1)
                if 0 <= static + 2 < PAIRS:
                    act.wait_ge(xs_t_done, p + 3)
                    copy(xs_hi[q], ps_xs[:, 0:2 * P]).then_inc(xs_hi_ready, 1)
                if static in LAST_WEIGHT:
                    gate_weights(G - 1, LAST_WEIGHT[static])
                if static == LAST_NORM:
                    post_norm(G - 1, 1)
                if static in LAST_COPY:
                    post_copy(G - 1, LAST_COPY[static])

            pairs(act, unit)

            def norms(b, static):
                if 0 <= static + 2 < B:
                    q = (static + 2) % RING
                    if static + 2 >= RING:
                        act.wait_ge(y_ready, b + 3 - RING)
                    for c in range(C):
                        i = (b + 2) * C + c
                        last = act.activation(xf[q][:, c * D:(c + 1) * D], x1[:, bass.ds(i, 1), :], ACT.Identity,
                                              bias=norm2_all[:, bass.ds(i, 1), 0], scale=norm2_all[:, bass.ds(i, 1), 1])
                    last.then_inc(xf_ready, 1)
                if 0 <= static - 1 < B:
                    q = (static - 1) % RING
                    act.wait_ge(rstd3_ready, b)
                    if static - 1 >= RING:
                        act.wait_ge(final_stored[q], (b - 1 - q) * (16 // RING))
                    normalised(lambda c: final[q][:, c, :], lambda c: ps_y[q][:, c * D:(c + 1) * D], norm3[q]).then_inc(yn_ready, 1)

            batches(act, norms)

        @block.vector
        def _(dve):
            v = dve
            def make_edges(g, s, chunks):
                return v.tensor_scalar(edges[s][:, chunks, :], adj_raw[s][:, chunks, :], 0.0, None, ALU.not_equal)

            def stats(stat, i, ready):
                for c in range(C):
                    v.bn_stats(stat[:, c, :], x1[:, bass.ds(i * C + c, 1), :]).then_inc(ready, 1)

            def moments(stat, norm, stat_ready, aggr_ready, ready, i):
                v.wait_ge(stat_ready, (i + 1) * C)
                v.memset(held[:, :], 0.0)
                for c in range(C):
                    last = v.bn_aggr(norm[:, c, :], stat[:, c, :])
                last.then_inc(aggr_ready, 1)
                v.wait_ge(aggr_ready, i + 1)
                v.tensor_scalar(norm[:, :, 0], norm[:, :, 0], -1.0, None, ALU.mult)
                v.tensor_scalar(norm[:, :, 1], norm[:, :, 1], EPS, None, ALU.add).then_inc(ready, 1)

            def prep_stats(g, s):
                stats(stat1, post_index(g, s), stat1_ready)

            def prep_moments(g, s):
                moments(stat1, norm1[s], stat1_ready, aggr1_ready, norm1_ready, post_index(g, s))

            def post_stats(g, s):
                i = post_index(g, s)
                v.wait_ge(x1_ready, i + 1)
                v.memset(held[:, :], 0.0)
                stats(stat2, i, stat2_ready)

            def post_moments(g, s):
                moments(stat2, norm2[s], stat2_ready, aggr2_ready, norm2_ready, post_index(g, s))

            def prepared(g, s, i):
                v.wait_ge(ht_hi_ready, i + 1)
                v.tensor_tensor(ht_lo[s], xn[s][:, :, :], ht_hi[s].bitcast(FP32), ALU.subtract).then_inc(ht_lo_ready, 1)

            def split_agg(st):
                v.wait_ge(agg_hi_ready, st + 1)
                v.tensor_tensor(agg_lo[:, :], ps_agg[:, :], agg_hi[:, :].bitcast(FP32), ALU.subtract).then_inc(agg_lo_ready, 1)

            def post_x1(g, s):
                i = post_index(g, s)
                v.wait_ge(t_done, g * ST + ST - S + s + 1)
                for c in range(C):
                    b = i * C + c
                    last = v.scalar_tensor_tensor(x1[:, bass.ds(b, 1), :], ps_t[:, c * P:(c + 1) * P], cols[:, bass.ds(6 + b, 1)],
                                                  x1[:, bass.ds(b, 1), :], ALU.mult, ALU.add)
                last.then_inc(x1_ready, 1)

            def post_dest(g, s):
                i = post_index(g, s)
                v.wait_ge(payload_ready, i + 1)
                v.tensor_copy(payload[s][:, :, :, D + 1].bitcast(I32), dest[:, bass.ds(i * C, C), :])
                v.tensor_copy(norm2_all[:, bass.ds(i * C, C), :], norm2[s][:, :, :])

            def post_gate(g, s, part):
                i = post_index(g, s)
                done = [ROUTE_STARTS[part]]

                def chain(ins, then_max=False):
                    done[0] += 1
                    ins.then_inc(route, 1)
                    v.wait_ge(route, i * ROUTE_STEPS + done[0])
                    if then_max:
                        v.memset(held[:, :], 0.0)

                if part == 0:
                    v.wait_ge(logits_done, i + 1)
                    chain(v.tensor_tensor(logits[:, :, :], post_bank(g, s)[:, 0:C * E].rearrange("p (c e) -> p c e", c=C),
                                          gate_b_sb[:, None, :].to_broadcast([P, C, E]), ALU.add), True)
                    for c in range(C):
                        last = v.max(top[:, c, :], logits[:, c, :])
                    chain(last, True)
                elif part == 1:
                    v.tensor_tensor(margin[s][:, :, 0], top[:, :, 0], top[:, :, 1], ALU.subtract)
                    v.tensor_tensor(margin[s][:, :, 1], top[:, :, 1], top[:, :, 0], ALU.subtract)
                    for c in range(C):
                        last = v.max_index(top_at[:, c, :], top[:, c, :], logits[:, c, :])
                    chain(last)
                    chain(v.tensor_copy(chosen[:, :, :], top_at[:, :, 0:K]))
                    chain(v.tensor_tensor(onehot[:, :, :, :], iota_e[:, None, None, :].to_broadcast([P, C, K, E]),
                                          chosen[:, :, :, None].to_broadcast([P, C, K, E]), ALU.is_equal))
                    v.tensor_tensor(both[:, :].rearrange("p (c e) -> p c e", c=C), onehot[:, :, 0, :], onehot[:, :, 1, :], ALU.add).then_inc(both_ready, 1)
                elif part == 2:
                    v.wait_ge(prefix_done, i + 1)
                    chain(v.tensor_tensor(place[:, :, :], post_bank(g, s)[:, 0:C * E].rearrange("p (c e) -> p c e", c=C),
                                          base_e[:, None, :].to_broadcast([P, C, E]), ALU.add))
                    chain(v.tensor_tensor(base_e[:, :], post_bank(g, s)[:, C * E:(C + 1) * E], base_e[:, :], ALU.add))
                    for k in range(K):
                        last = v.tensor_tensor(picked[:, :, k, :], onehot[:, :, k, :], place[:, :, :], ALU.mult)
                    chain(last, True)
                else:
                    chain(v.tensor_reduce(slots_f[:, :, :], picked[:, :, :, :], AX.X, ALU.add))
                    v.tensor_copy(slots[s][:, :].rearrange("p (c k) -> p c k", c=C), slots_f[:, :, :]).then_inc(slots_ready, 1)
                assert done[0] == (*ROUTE_STARTS[1:], ROUTE_STEPS)[part]

            steps = [0]

            def map_chain(ins):
                steps[0] += 1
                ins.then_inc(mapping, 1)
                v.wait_ge(mapping, steps[0])

            def map_tiles(late, part):
                at = tile_late if late else tile_at
                if part == 0:
                    map_chain(v.tensor_tensor(count_f[:, :], base_e[:, :], region_e[:, :], ALU.subtract))
                    map_chain(v.tensor_scalar(count_i[:, :], count_f[:, :], float(P - 1 if late else 0), None, ALU.add))
                    map_chain(v.tensor_scalar(count_i[:, :], count_i[:, :], 7, None, ALU.arith_shift_right))
                    map_chain(v.tensor_copy(tiles_e[:, :], count_i[:, :]))
                elif part == 1:
                    v.tensor_tensor(passed_e[:, :], tiles_e[:, :], taken[:, 1:E + 1], ALU.subtract)
                    map_chain(v.tensor_tensor(open_e[:, :], tiles_e[:, :], taken[:, 0:E], ALU.subtract))
                    map_chain(v.tensor_tensor_scan(tile_end[:, :], open_e[:, :], no_more[:, :], 0.0, ALU.add, ALU.add))
                    map_chain(v.tensor_tensor(ended[:, :, :], tile_end[:, None, :].to_broadcast([P, 2, E]), at[:, :, None].to_broadcast([P, 2, E]), ALU.is_le))
                elif part == 2:
                    v.tensor_reduce(tile_expert[:, :], ended[:, :, :], AX.X, ALU.add)
                    map_chain(v.tensor_tensor(ended_tiles[:, :, :], ended[:, :, :], passed_e[:, None, :].to_broadcast([P, 2, E]), ALU.mult))
                    map_chain(v.tensor_reduce(tile_first[:, :], ended_tiles[:, :, :], AX.X, ALU.add))
                    map_chain(v.tensor_tensor(tile_first[:, :], at[:, :], tile_first[:, :], ALU.subtract))
                    map_chain(v.tensor_tensor(tile_first[:, :], tile_first[:, :], taken[:, 0:1].to_broadcast([P, 2]), ALU.add))
                else:
                    map_chain(v.tensor_scalar(tile_first[:, :], tile_first[:, :], float(P), None, ALU.mult))
                    map_chain(v.scalar_tensor_tensor(tile_row[:, :], tile_expert[:, :], float(REGION), tile_first[:, :], ALU.mult, ALU.add))
                    v.tensor_scalar(clipped[:, 1, :], tile_row[:, :], float(E * REGION), None, ALU.min)
                    v.tensor_scalar(clipped[:, 0, :], tile_expert[:, :], float(E - 1), None, ALU.min).then_inc(mapped, 1)

            def take_early():
                map_chain(v.tensor_tensor(count_f[:, :], tiles_e[:, :], tile_end[:, :], ALU.subtract))
                map_chain(v.tensor_scalar(count_f[:, :], count_f[:, :], float(EARLY), None, ALU.add))
                map_chain(v.tensor_scalar(count_f[:, :], count_f[:, :], 0.0, None, ALU.max))
                map_chain(v.tensor_tensor(taken[:, 0:E], count_f[:, :], tiles_e[:, :], ALU.min))

            def extras(g, k, at, first, last):
                for work in VECTOR_WORK.get((k, at), []):
                    name, _, n = work.partition(" ")
                    n = int(n or 0)
                    if name == "x1":
                        if not (first and k == 0):
                            post_x1(*((g, 0) if k else (g - 1, 1)))
                    elif name == "edges":
                        if not last:
                            s, half = divmod(n, 2)
                            if half == 0:
                                v.wait_ge(loaded_adj[s], (g + 2) * 16)
                                v.wait_ge(agg_done, g * ST + ST - S + s + 1)
                            made = make_edges(g + 1, s, slice(half * C // 2, (half + 1) * C // 2))
                            if half:
                                made.then_inc(edges_ready[s], 1)
                    elif name.startswith("prep"):
                        if not last:
                            (prep_stats if name == "prep_stats" else prep_moments)(g + 1, n)
                    elif not first:
                        if name == "logits":
                            post_dest(g - 1, n)
                        if name in PARTS:
                            post_gate(g - 1, n, PARTS.index(name))
                        else:
                            (post_stats if name == "post_stats" else post_moments)(g - 1, n)
                if last and (k, at) == (7, "a"):
                    map_chain(v.memset(taken[:, :], 0.0))
                if last and (k, at) in EARLY_MAP:
                    map_tiles(False, EARLY_MAP.index((k, at)))
                if last and (k, at) == (9, "b"):
                    take_early()
                    v.wait_ge(map_done, 1)
                    v.tensor_copy(tile_map[:, 0:EARLY], ps_prep[0:1, 0:EARLY])
                    v.tensor_copy(tile_map[:, MAP_ROWS:MAP_ROWS + EARLY], ps_prep[0:1, EARLY:2 * EARLY]).then_inc(map_ready, 1)
                    post_stats(g, 0)
                    post_moments(g, 0)

            EARLY_MAP = ((7, "a"), (7, "b"), (8, "a"), (8, "b"))

            PARTS = ("logits", "chosen", "places", "slots")

            def step(g, k, first, last):
                st = g * ST + k
                s = k % S
                halves_of = [slice(i * N // 2, (i + 1) * N // 2) for i in range(2)]
                v.wait_ge(r_ready, st + 1)
                v.scalar_tensor_tensor(t_sb[:, :], ps_hn[:, :], cols[:, 5:6], r_sb[:, :], ALU.add, ALU.mult).then_inc(rh_done, 1)
                if first and k == 1:
                    v.wait_ge(loaded_x, 16)
                    v.wait_ge(loaded_consts, 64)
                    v.wait_ge(consts_set, CONSTS)
                previous = before(g, k, first, last)
                if previous:
                    pst, ps, pg, last_layer, followed = previous
                    if not last_layer:
                        v.wait_ge(ht_hi_ready, pst + 3)
                        v.tensor_tensor(ht_lo[ps], ps_t[:, :].rearrange("p (c d) -> p c d", c=C), ht_hi[ps].bitcast(FP32), ALU.subtract).then_inc(ht_lo_ready, 1)
                    elif followed:
                        prepared(pg + 1, ps, pst + 2)
                v.wait_ge(in_done, st + 1)
                v.wait_ge(rh_done, st + 1)
                v.tensor_tensor(t_sb[:, :], ps_in[:, :], t_sb[:, :], ALU.add).then_inc(pre_n_ready, 1)
                extras(g, k, "a", first, last)
                for i, half in enumerate(halves_of):
                    v.wait_ge(n_ready, st * 2 + i + 1)
                    v.tensor_tensor(d_sb[:, half], h[s][:, half], n_sb[:, half], ALU.subtract).then_inc(d_ready, 1)
                if not (last and k == ST - 1):
                    split_agg(st + 1)
                for i, half in enumerate(halves_of):
                    v.wait_ge(d_ready, st * 2 + i + 1)
                    v.tensor_tensor(d_sb[:, half], d_sb[:, half], z_sb[:, half], ALU.mult).then_inc(zd_ready, 1)
                for i, half in enumerate(halves_of):
                    v.wait_ge(zd_ready, st * 2 + i + 1)
                    v.tensor_tensor(h[s][:, half], n_sb[:, half], d_sb[:, half], ALU.add).then_inc(h_ready, 1)
                extras(g, k, "b", first, last)

            v.wait_ge(loaded_x0, 16)
            for s in range(S):
                prep_stats(0, s)
                prep_moments(0, s)
            v.wait_ge(w_transposed, 1)
            v.tensor_copy(cols[:, :], ps_agg[:, 0:2 * 3 + B * C]).then_inc(bias_ready, 1)
            v.wait_ge(w_transposed, 2)
            v.tensor_copy(w_ihT, ps_in[:, 0:3 * D]).then_inc(w_copied, 1)
            v.tensor_copy(n_sb[:, :], ps_r[:, :]).then_inc(w_copied, 1)
            v.tensor_copy(weightT[4], ps_z[:, 0:D]).then_inc(w_copied, 1)
            v.wait_ge(bias_ready, 1)
            v.tensor_tensor(bias_rz[:, :], cols[:, 0:2], cols[:, 3:5], ALU.add).then_inc(w_copied, 1)
            v.wait_ge(w_hi_ready, 1)
            v.tensor_tensor(w_hh_lo[:, :], ps_hn[:, 0:3 * D], w_hh_hi[:, :].bitcast(FP32), ALU.subtract).then_inc(w_lo_ready, 1)
            v.wait_ge(loaded_adj[0], 16)
            make_edges(0, 0, slice(0, C)).then_inc(edges_ready[0], 1)
            prepared(0, 0, 0)
            for l in range(L):
                v.wait_ge(w_hi_ready, l + 2)
                v.tensor_tensor(w_fused_lo[:, l, :], fused_bank[l][:, 0:3 * D], w_fused_hi[:, l, :].bitcast(FP32), ALU.subtract).then_inc(w_lo_ready, 1)
                if l == 1:
                    prepared(0, 1, 1)
            split_agg(0)
            v.wait_ge(loaded_adj[1], 16)
            make_edges(0, 1, slice(0, C)).then_inc(edges_ready[1], 1)
            groups(v, step)
            post_x1(G - 1, S - 1)
            post_stats(G - 1, S - 1)
            post_moments(G - 1, S - 1)

            def unit(p, static, turn):
                q = static % 2
                if 0 <= static - 1 < PAIRS:
                    r = 1 - q
                    v.wait_ge(hid_hi_ready, p)
                    v.tensor_tensor(hid_lo[r], ps_hid[r][:, :], hid_hi[r].bitcast(FP32), ALU.subtract).then_inc(hid_lo_ready, 1)
                if 0 <= static + 2 < PAIRS:
                    v.wait_ge(xs_hi_ready, p + 3)
                    v.tensor_tensor(xs_lo[q], ps_xs[:, 0:2 * P], xs_hi[q].bitcast(FP32), ALU.subtract).then_inc(xs_lo_ready, 1)
                for work in LAST_VECTOR.get(static, []):
                    name, _, n = work.partition(" ")
                    if name == "ends":
                        v.wait_ge(slots_ready, B)
                        v.tensor_copy(pad_rows[:, :], base_e[0:1, :]).then_inc(map_ready, 1)
                    elif name == "map" and n:
                        map_tiles(True, int(n))
                    elif name == "map":
                        v.wait_ge(map_done, 2)
                        new = TILES - EARLY
                        v.tensor_copy(tile_map[:, EARLY:TILES], ps_post[0:1, 0:new])
                        v.tensor_copy(tile_map[:, MAP_ROWS + EARLY:MAP_ROWS + TILES], ps_post[0:1, new:2 * new]).then_inc(map_ready, 1)
                    else:
                        if name == "logits":
                            post_dest(G - 1, int(n))
                        post_gate(G - 1, int(n), PARTS.index(name))
                if 0 <= static - 2 < PAIRS:
                    u = (static - 2) % SLOTS
                    v.wait_ge(down_done, p - 1)
                    down = ps_down[q][:, :].rearrange("p (j i d) -> p j i d", j=2, i=2)
                    for j in range(2):
                        v.tensor_scalar(res[u][:, j, :], down[:, j, 0, :], slot[u][:, j, D:D + 1], None, ALU.mult).then_inc(res_part, 1)
                    for j in range(2):
                        v.wait_ge(res_part, (p - 2) * 2 + j + 1)
                        last = v.scalar_tensor_tensor(res[u][:, j, :], down[:, j, 1, :], slot[u][:, j, D:D + 1], res[u][:, j, :], ALU.mult, ALU.add)
                    last.then_inc(res_ready, 1)

            pairs(v, unit)

            def finish(b, static):
                now, before = 0 <= static < B, 0 <= static - 2 < B
                q, r = static % RING, (static - 2) % RING
                if before:
                    v.wait_ge(yn_ready, b - 1)
                    v.tensor_tensor(final[r], final[r], gamma_sb[:, None, :].to_broadcast([P, C, D]), ALU.mult).then_inc(scaled_ready, 1)
                if now:
                    v.wait_ge(y_ready, b + 1)
                    v.memset(held[:, :], 0.0)
                    for c in range(C):
                        last = v.bn_stats(stat2[:, c, :], ps_y[q][:, c * D:(c + 1) * D])
                    last.then_inc(y_stats, 1)
                    v.wait_ge(y_stats, b + 1)
                    v.memset(held[:, :], 0.0)
                    for c in range(C):
                        last = v.bn_aggr(norm3[q][:, c, :], stat2[:, c, :])
                    last.then_inc(y_aggr, 1)
                if before:
                    v.wait_ge(scaled_ready, b - 1)
                    v.wait_ge(x_beta_ready, b - 1)
                    v.tensor_tensor(final[r], final[r], x_beta[r], ALU.add).then_inc(final_ready, 1)
                if now:
                    v.wait_ge(y_aggr, b + 1)
                    v.tensor_scalar(norm3[q][:, :, 0], norm3[q][:, :, 0], -1.0, None, ALU.mult)
                    v.tensor_scalar(norm3[q][:, :, 1], norm3[q][:, :, 1], EPS, None, ALU.add).then_inc(norm3_ready, 1)

            batches(v, finish)


_INS = ['x', 'adj', 'nodemask', 'L0_gnn_weight', 'L0_gnn_w_ih', 'L0_gnn_w_hh', 'L0_gnn_b_ih', 'L0_gnn_b_hh',
        'L0_ffn_gate_w', 'L0_ffn_gate_b', 'L0_ffn_w1', 'L0_ffn_b1', 'L0_ffn_w2', 'L0_ffn_b2', 'L0_ffn_gamma', 'L0_ffn_beta']


def kernel(**inputs):
    import numpy as np
    import concourse.bacc as bacc
    from concourse import mybir as mb
    from concourse.bass_utils import run_bass_kernel_spmd

    nc = bacc.Bacc("TRN2", target_bir_lowering=False, num_devices=1)
    arrays, args = {}, []
    for name in _INS:
        a = np.ascontiguousarray(inputs[name])
        arrays[f"in_{name}"] = a
        args.append(nc.dram_tensor(f"in_{name}", a.shape, mb.dt.from_np(a.dtype), kind="ExternalInput").ap())
    out = nc.dram_tensor("out_x", inputs["x"].shape, mb.dt.from_np(np.dtype("float32")), kind="ExternalOutput").ap()
    build(nc, *args, out)
    r = run_bass_kernel_spmd(nc, [arrays], core_ids=[0])
    return r.results[0]["out_x"]
```
